# Optimizing a Trainium2 kernel written in Bass

```python
import numpy as np
import jax
import jax.numpy as jnp

def _softmax(x, axis=-1):
    return jax.nn.softmax(x, axis=axis)

def _gelu(x):
    return jax.nn.gelu(x, approximate=True)

def _silu(x):
    return jax.nn.silu(x)

def _sigmoid(x):
    return jax.nn.sigmoid(x)

def _layernorm(x, axis=-1, eps=1e-05):
    m = jnp.mean(x, axis=axis, keepdims=True)
    v = jnp.var(x, axis=axis, keepdims=True)
    return (x - m) / jnp.sqrt(v + eps)

def _scatter_add(tgt, idx, src, axis=0):
    return tgt.at[idx].add(src)

def _segment_sum(src, seg, n):
    return jax.ops.segment_sum(src, seg, n)
kernel_name = 'mk_flamingo_gated_d2_seqx_r8_13958d'

def setup_inputs(seed: int=0):
    np.random.seed(seed)
    _w = jnp.asarray

    def _rec_inputs():
        import jax
        import jax.numpy as jnp
        _rk = jax.random.key(seed)
        x = 7.22e-05 + 1 * jax.random.normal(jax.random.fold_in(_rk, 1), (128, 64, 128), jnp.float32)
        _lenS = 64 - jax.random.randint(jax.random.fold_in(_rk, 7), (128,), 0, max(1, 64 // 4) + 1, jnp.int32)
        _lenS2 = 64 - jax.random.randint(jax.random.fold_in(_rk, 8), (128,), 0, max(1, 64 // 4) + 1, jnp.int32)
        _ctx_1024P = jax.random.normal(jax.random.fold_in(_rk, 11), (128, 16, 128), jnp.float32)
        _ctx_1024c = jax.random.dirichlet(jax.random.fold_in(_rk, 511), 0.3 * jnp.ones((16,), jnp.float32), (128, 64))
        _ctx_1024t = jnp.einsum('bsk,bkd->bsd', _ctx_1024c, _ctx_1024P)
        _ctx_1024t = _ctx_1024t * jax.lax.rsqrt(jnp.mean(jnp.square(_ctx_1024t)) + 1e-12) * 0.953939
        ctx_1024 = 4.13588e-05 + 0.999923 * (_ctx_1024t + 0.3 * jax.random.normal(jax.random.fold_in(_rk, 611), (128, 64, 128), jnp.float32))
        _validS = jnp.arange(64)[None, :] < _lenS[:, None]
        _validS2 = jnp.arange(64)[None, :] < _lenS2[:, None]
        _causal = jnp.tril(jnp.ones((64, 64), dtype=bool))
        mask_BxS2_if1 = jnp.where(jnp.ones((128, 64), dtype=bool), 1, 0).astype(jnp.int32)
        mask_Bx1xSxS2_ik1 = jnp.where(jnp.broadcast_to(_validS2[:, None, None, :], (128, 1, 64, 64)), 1, 0).astype(jnp.int32)
        _g = jax.random.normal(jax.random.fold_in(_rk, 9001), (2, 2), jnp.float32)
        _g = jnp.sign(_g) * jnp.maximum(jnp.abs(_g), 1.0) + (_g == 0) * 1.0
        g_xattn = _g[0]
        g_ffn = _g[1]
        return (x, ctx_1024, mask_BxS2_if1, mask_Bx1xSxS2_ik1, g_xattn, g_ffn)
    x, ctx_1024, mask_BxS2_if1, mask_Bx1xSxS2_ik1, g_xattn, g_ffn = _rec_inputs()

    def _L0_xattn_setup():
        import jax, jax.numpy as jnp
        import numpy as np
        import math
        NUM_HEADS = 16
        HIDDEN = 128
        HEAD_DIM = HIDDEN // NUM_HEADS
        ROTARY_BASE = 10000.0
        B, S = (4, 256)

        def _rotary_tables(seq_len):
            inv_freq = 1.0 / ROTARY_BASE ** (jnp.arange(0, HEAD_DIM, 2, dtype=jnp.float32) / HEAD_DIM)
            pos = jnp.arange(seq_len, dtype=jnp.float32)
            freqs = pos[:, None] * inv_freq[None, :]
            return (jnp.cos(freqs), jnp.sin(freqs))

        def _apply_rotary(x, cos, sin):
            even = x[..., 0::2]
            odd = x[..., 1::2]
            c = cos[None, None, :, :]
            s = sin[None, None, :, :]
            return jnp.concatenate([even * c - odd * s, even * s + odd * c], axis=-1)
        key = jax.random.key(seed)
        ks = jax.random.split(key, 12)
        w = 0.02
        return {'query': jax.random.normal(ks[0], (B, S, HIDDEN), jnp.float32), 'key': jax.random.normal(ks[1], (B, S, HIDDEN), jnp.float32), 'value': jax.random.normal(ks[2], (B, S, HIDDEN), jnp.float32), 'padding_mask': jnp.ones((B, S), jnp.int32), 'is_causal': 1, 'Wq': jax.random.normal(ks[3], (HIDDEN, HIDDEN), jnp.float32) * w, 'bq': jnp.zeros((HIDDEN,), jnp.float32), 'Wk': jax.random.normal(ks[4], (HIDDEN, HIDDEN), jnp.float32) * w, 'bk': jnp.zeros((HIDDEN,), jnp.float32), 'Wv': jax.random.normal(ks[5], (HIDDEN, HIDDEN), jnp.float32) * w, 'bv': jnp.zeros((HIDDEN,), jnp.float32), 'Wo': jax.random.normal(ks[6], (HIDDEN, HIDDEN), jnp.float32) * w, 'bo': jnp.zeros((HIDDEN,), jnp.float32)}
    _L0_xattn_all = _L0_xattn_setup()
    _L0_xattn_in = {k: v for k, v in _L0_xattn_all.items() if k in ('Wq', 'bq', 'Wk', 'bk', 'Wv', 'bv', 'Wo', 'bo')}
    del _L0_xattn_all

    def _L0_ffn_setup():
        import jax, jax.numpy as jnp
        import numpy as np
        from jax import lax
        HIDDEN = 128
        INTER = 64
        E = 64
        K = 6
        G = 8
        TG = 4
        NSH = 2
        ISH = INTER * NSH

        def _moe_forward(hidden_states, gate_w, gate_bias, eg_w, eu_w, ed_w, sg_w, su_w, sd_w):
            B, S, H = hidden_states.shape
            x = hidden_states.reshape(-1, H)
            T = x.shape[0]
            shared = jax.nn.silu(x @ sg_w.T) * (x @ su_w.T) @ sd_w.T
            logits = x @ gate_w.T
            scores = jax.nn.sigmoid(logits) + gate_bias
            group_scores = scores.reshape(T, G, E // G).max(axis=-1)
            _, sel_groups = lax.top_k(group_scores, TG)
            group_mask = jnp.zeros((T, G), scores.dtype).at[jnp.arange(T)[:, None], sel_groups].set(1.0)
            mask = jnp.repeat(group_mask, E // G, axis=1)
            masked_scores = scores * mask
            topk_w, topk_i = lax.top_k(masked_scores, K)
            topk_w = topk_w / (topk_w.sum(axis=-1, keepdims=True) + 1e-08)
            comb = jnp.zeros((T, E), x.dtype).at[jnp.arange(T)[:, None], topk_i].add(topk_w)
            h = jax.nn.silu(jnp.einsum('th,eih->eti', x, eg_w)) * jnp.einsum('th,eih->eti', x, eu_w)
            routed = jnp.einsum('eti,ehi,te->th', h, ed_w, comb)
            return (shared + routed).reshape(B, S, H)
        key = jax.random.key(seed)
        ks = jax.random.split(key, 9)
        s = 0.02
        return {'hidden_states': jax.random.normal(ks[0], (1, 128, HIDDEN), jnp.float32), 'gate_w': jax.random.normal(ks[1], (E, HIDDEN), jnp.float32) * s, 'gate_bias': jnp.zeros((E,), jnp.float32), 'eg_w': jax.random.normal(ks[2], (E, INTER, HIDDEN), jnp.float32) * s, 'eu_w': jax.random.normal(ks[3], (E, INTER, HIDDEN), jnp.float32) * s, 'ed_w': jax.random.normal(ks[4], (E, HIDDEN, INTER), jnp.float32) * s, 'sg_w': jax.random.normal(ks[5], (ISH, HIDDEN), jnp.float32) * s, 'su_w': jax.random.normal(ks[6], (ISH, HIDDEN), jnp.float32) * s, 'sd_w': jax.random.normal(ks[7], (HIDDEN, ISH), jnp.float32) * s}
    _L0_ffn_all = _L0_ffn_setup()
    _L0_ffn_in = {k: v for k, v in _L0_ffn_all.items() if k in ('gate_w', 'gate_bias', 'eg_w', 'eu_w', 'ed_w', 'sg_w', 'su_w', 'sd_w')}
    del _L0_ffn_all

    def _L1_xattn_setup():
        import jax, jax.numpy as jnp
        import numpy as np
        EMBED = 128
        HEADS = 16
        HEAD_DIM = EMBED // HEADS
        key = jax.random.key(seed)
        ks = jax.random.split(key, 9)
        N, Q, K = (2, 256, 256)
        queries = jax.random.normal(ks[0], (N, Q, EMBED), dtype=jnp.float32)
        keys_ = jax.random.normal(ks[1], (N, K, EMBED), dtype=jnp.float32)
        values = jax.random.normal(ks[2], (N, K, EMBED), dtype=jnp.float32)
        mask = jax.random.randint(ks[3], (N, 1, Q, K), 0, 2, dtype=jnp.int32)
        s = 1.0 / np.sqrt(EMBED)
        Wq = jax.random.normal(ks[4], (EMBED, EMBED), dtype=jnp.float32) * s
        Wk = jax.random.normal(ks[5], (EMBED, EMBED), dtype=jnp.float32) * s
        Wv = jax.random.normal(ks[6], (EMBED, EMBED), dtype=jnp.float32) * s
        Wo = jax.random.normal(ks[7], (EMBED, EMBED), dtype=jnp.float32) * s
        bo = jax.random.normal(ks[8], (EMBED,), dtype=jnp.float32) * s
        return {'queries': queries, 'keys': keys_, 'values': values, 'mask': mask, 'Wq': Wq, 'Wk': Wk, 'Wv': Wv, 'Wo': Wo, 'bo': bo}
    _L1_xattn_all = _L1_xattn_setup()
    _L1_xattn_in = {k: v for k, v in _L1_xattn_all.items() if k in ('Wq', 'Wk', 'Wv', 'Wo', 'bo')}
    del _L1_xattn_all

    def _L1_ffn_setup():
        import jax, jax.numpy as jnp
        import numpy as np
        TOP_K = 2
        key = jax.random.key(seed)
        k1, k2, k3, k4 = jax.random.split(key, 4)
        B, S, H, I, E = (2, 256, 128, 512, 8)
        return {'hidden_states': jax.random.normal(k1, (B, S, H), jnp.float32), 'gate_w': jax.random.normal(k2, (E, H), jnp.float32) * 0.02, 'gate_up_proj': jax.random.normal(k3, (E, 2 * I, H), jnp.float32) * 0.02, 'down_proj': jax.random.normal(k4, (E, H, I), jnp.float32) * 0.02}
    _L1_ffn_all = _L1_ffn_setup()
    _L1_ffn_in = {k: v for k, v in _L1_ffn_all.items() if k in ('gate_w', 'gate_up_proj', 'down_proj')}
    del _L1_ffn_all
    return {'x': x, 'ctx_1024': ctx_1024, 'mask_BxS2_if1': mask_BxS2_if1, 'mask_Bx1xSxS2_ik1': mask_Bx1xSxS2_ik1, 'g_xattn': g_xattn, 'g_ffn': g_ffn, 'L0_xattn_Wq': _L0_xattn_in['Wq'], 'L0_xattn_bq': _L0_xattn_in['bq'], 'L0_xattn_Wk': _L0_xattn_in['Wk'], 'L0_xattn_bk': _L0_xattn_in['bk'], 'L0_xattn_Wv': _L0_xattn_in['Wv'], 'L0_xattn_bv': _L0_xattn_in['bv'], 'L0_xattn_Wo': _L0_xattn_in['Wo'], 'L0_xattn_bo': _L0_xattn_in['bo'], 'L0_ffn_gate_w': _L0_ffn_in['gate_w'], 'L0_ffn_gate_bias': _L0_ffn_in['gate_bias'], 'L0_ffn_eg_w': _L0_ffn_in['eg_w'], 'L0_ffn_eu_w': _L0_ffn_in['eu_w'], 'L0_ffn_ed_w': _L0_ffn_in['ed_w'], 'L0_ffn_sg_w': _L0_ffn_in['sg_w'], 'L0_ffn_su_w': _L0_ffn_in['su_w'], 'L0_ffn_sd_w': _L0_ffn_in['sd_w'], 'L1_xattn_Wq': _L1_xattn_in['Wq'], 'L1_xattn_Wk': _L1_xattn_in['Wk'], 'L1_xattn_Wv': _L1_xattn_in['Wv'], 'L1_xattn_Wo': _L1_xattn_in['Wo'], 'L1_xattn_bo': _L1_xattn_in['bo'], 'L1_ffn_gate_w': _L1_ffn_in['gate_w'], 'L1_ffn_gate_up_proj': _L1_ffn_in['gate_up_proj'], 'L1_ffn_down_proj': _L1_ffn_in['down_proj']}

def reference(x, ctx_1024, mask_BxS2_if1, mask_Bx1xSxS2_ik1, g_xattn, g_ffn, L0_xattn_Wq, L0_xattn_bq, L0_xattn_Wk, L0_xattn_bk, L0_xattn_Wv, L0_xattn_bv, L0_xattn_Wo, L0_xattn_bo, L0_ffn_gate_w, L0_ffn_gate_bias, L0_ffn_eg_w, L0_ffn_eu_w, L0_ffn_ed_w, L0_ffn_sg_w, L0_ffn_su_w, L0_ffn_sd_w, L1_xattn_Wq, L1_xattn_Wk, L1_xattn_Wv, L1_xattn_Wo, L1_xattn_bo, L1_ffn_gate_w, L1_ffn_gate_up_proj, L1_ffn_down_proj):
    import jax
    import jax.numpy as jnp

    def _L0_xattn_ref(query, key, value, padding_mask, is_causal, Wq, bq, Wk, bk, Wv, bv, Wo, bo):
        import jax, jax.numpy as jnp
        import numpy as np
        import math
        NUM_HEADS = 16
        HIDDEN = 128
        HEAD_DIM = HIDDEN // NUM_HEADS
        ROTARY_BASE = 10000.0
        B, S = (4, 256)

        def _rotary_tables(seq_len):
            inv_freq = 1.0 / ROTARY_BASE ** (jnp.arange(0, HEAD_DIM, 2, dtype=jnp.float32) / HEAD_DIM)
            pos = jnp.arange(seq_len, dtype=jnp.float32)
            freqs = pos[:, None] * inv_freq[None, :]
            return (jnp.cos(freqs), jnp.sin(freqs))

        def _apply_rotary(x, cos, sin):
            even = x[..., 0::2]
            odd = x[..., 1::2]
            c = cos[None, None, :, :]
            s = sin[None, None, :, :]
            return jnp.concatenate([even * c - odd * s, even * s + odd * c], axis=-1)
        b, s, _ = query.shape

        def proj(x, W, bias):
            y = x @ W.T + bias
            return y.reshape(b, s, NUM_HEADS, HEAD_DIM).transpose(0, 2, 1, 3)
        q = proj(query, Wq, bq)
        k = proj(key, Wk, bk)
        v = proj(value, Wv, bv)
        cos, sin = _rotary_tables(s)
        q = _apply_rotary(q, cos, sin)
        k = _apply_rotary(k, cos, sin)
        scores = jnp.einsum('bhqd,bhkd->bhqk', q, k) / math.sqrt(HEAD_DIM)
        scores = jnp.where(padding_mask[:, None, None, :] == 0, -1000000000.0, scores)
        if is_causal:
            causal = jnp.triu(jnp.ones((s, s), bool), k=1)
            scores = jnp.where(causal[None, None, :, :], -1000000000.0, scores)
        probs = jax.nn.softmax(scores, axis=-1)
        hidden = jnp.einsum('bhqk,bhkd->bhqd', probs, v)
        hidden = hidden.transpose(0, 2, 1, 3).reshape(b, s, HIDDEN)
        return hidden @ Wo.T + bo

    def _L0_ffn_ref(hidden_states, gate_w, gate_bias, eg_w, eu_w, ed_w, sg_w, su_w, sd_w):
        import jax, jax.numpy as jnp
        import numpy as np
        from jax import lax
        HIDDEN = 128
        INTER = 64
        E = 64
        K = 6
        G = 8
        TG = 4
        NSH = 2
        ISH = INTER * NSH

        def _moe_forward(hidden_states, gate_w, gate_bias, eg_w, eu_w, ed_w, sg_w, su_w, sd_w):
            B, S, H = hidden_states.shape
            x = hidden_states.reshape(-1, H)
            T = x.shape[0]
            shared = jax.nn.silu(x @ sg_w.T) * (x @ su_w.T) @ sd_w.T
            logits = x @ gate_w.T
            scores = jax.nn.sigmoid(logits) + gate_bias
            group_scores = scores.reshape(T, G, E // G).max(axis=-1)
            _, sel_groups = lax.top_k(group_scores, TG)
            group_mask = jnp.zeros((T, G), scores.dtype).at[jnp.arange(T)[:, None], sel_groups].set(1.0)
            mask = jnp.repeat(group_mask, E // G, axis=1)
            masked_scores = scores * mask
            topk_w, topk_i = lax.top_k(masked_scores, K)
            topk_w = topk_w / (topk_w.sum(axis=-1, keepdims=True) + 1e-08)
            comb = jnp.zeros((T, E), x.dtype).at[jnp.arange(T)[:, None], topk_i].add(topk_w)
            h = jax.nn.silu(jnp.einsum('th,eih->eti', x, eg_w)) * jnp.einsum('th,eih->eti', x, eu_w)
            routed = jnp.einsum('eti,ehi,te->th', h, ed_w, comb)
            return (shared + routed).reshape(B, S, H)
        return _moe_forward(hidden_states, gate_w, gate_bias, eg_w, eu_w, ed_w, sg_w, su_w, sd_w)

    def _L1_xattn_ref(queries, keys, values, mask, Wq, Wk, Wv, Wo, bo):
        import jax, jax.numpy as jnp
        import numpy as np
        EMBED = 128
        HEADS = 16
        HEAD_DIM = EMBED // HEADS
        N, Qlen, _ = queries.shape
        Klen = keys.shape[1]
        q = (queries @ Wq.T).reshape(N, Qlen, HEADS, HEAD_DIM)
        k = (keys @ Wk.T).reshape(N, Klen, HEADS, HEAD_DIM)
        v = (values @ Wv.T).reshape(N, Klen, HEADS, HEAD_DIM)
        energy = jnp.einsum('nqhd,nkhd->nhqk', q, k)
        energy = jnp.where(mask == 0, jnp.float32(-1e+20), energy)
        attention = jax.nn.softmax(energy / jnp.sqrt(jnp.float32(EMBED)), axis=3)
        out = jnp.einsum('nhqk,nkhd->nqhd', attention, v).reshape(N, Qlen, EMBED)
        return out @ Wo.T + bo

    def _L1_ffn_ref(hidden_states, gate_w, gate_up_proj, down_proj):
        import jax, jax.numpy as jnp
        import numpy as np
        TOP_K = 2
        B, S, H = hidden_states.shape
        E = gate_w.shape[0]
        x = hidden_states.reshape(-1, H)
        T = x.shape[0]
        probs = jax.nn.softmax(x @ gate_w.T, axis=-1)
        w, idx = jax.lax.top_k(probs, TOP_K)
        w = w / jnp.sum(w, axis=-1, keepdims=True)
        combine = jnp.zeros((T, E), x.dtype).at[jnp.arange(T)[:, None], idx].add(w)

        def step(acc, inputs):
            gup, dn, ce = inputs
            g, u = jnp.split(x @ gup.T, 2, axis=-1)
            acc = acc + ce[:, None] * (jax.nn.silu(g) * u @ dn.T)
            return (acc, None)
        out, _ = jax.lax.scan(step, jnp.zeros_like(x), (gate_up_proj, down_proj, combine.T))
        return out.reshape(B, S, H)
    x = x + jnp.tanh(g_xattn[0]) * _L0_xattn_ref(_layernorm(x, axis=-1), ctx_1024, ctx_1024, mask_BxS2_if1, 1, L0_xattn_Wq, L0_xattn_bq, L0_xattn_Wk, L0_xattn_bk, L0_xattn_Wv, L0_xattn_bv, L0_xattn_Wo, L0_xattn_bo)
    x = x + jnp.tanh(g_ffn[0]) * _L0_ffn_ref(_layernorm(x, axis=-1), L0_ffn_gate_w, L0_ffn_gate_bias, L0_ffn_eg_w, L0_ffn_eu_w, L0_ffn_ed_w, L0_ffn_sg_w, L0_ffn_su_w, L0_ffn_sd_w)
    x = x + jnp.tanh(g_xattn[1]) * _L1_xattn_ref(_layernorm(x, axis=-1), ctx_1024, ctx_1024, mask_Bx1xSxS2_ik1, L1_xattn_Wq, L1_xattn_Wk, L1_xattn_Wv, L1_xattn_Wo, L1_xattn_bo)
    x = x + jnp.tanh(g_ffn[1]) * _L1_ffn_ref(_layernorm(x, axis=-1), L1_ffn_gate_w, L1_ffn_gate_up_proj, L1_ffn_down_proj)
    return x

_drawn_inputs = setup_inputs


def setup_inputs(seed=0):
    import zlib

    import numpy as np

    out = dict(_drawn_inputs(seed))
    spreads = {'g_ffn': (-1.0, 0.6),
     'L0_xattn_bq': (0.0, 0.8),
     'L0_xattn_bk': (0.0, 0.8),
     'L0_xattn_bv': (0.0, 0.506),
     'L0_xattn_bo': (0.0, 0.1),
     'L0_ffn_gate_bias': (0.0, 0.8)}
    factors = {'L0_xattn_Wq': 8.0,
     'L0_xattn_Wk': 8.0,
     'L0_xattn_Wv': 2.873,
     'L0_ffn_gate_w': 8.0,
     'L0_ffn_eg_w': 8.0,
     'L0_ffn_eu_w': 8.0,
     'L0_ffn_ed_w': 8.0,
     'L0_ffn_sg_w': 8.0,
     'L0_ffn_su_w': 8.0,
     'L0_ffn_sd_w': 8.0,
     'L1_ffn_gate_w': 8.0,
     'L1_ffn_gate_up_proj': 8.0,
     'L1_ffn_down_proj': 8.0}
    for name, (base, spread) in spreads.items():
        noise = np.random.default_rng([zlib.crc32(name.encode()), seed]).standard_normal(out[name].shape)
        drawn = base * np.exp(spread * noise) if base else spread * noise
        out[name] = jnp.asarray(drawn.astype(out[name].dtype))
    for name, factor in factors.items():
        out[name] = (out[name] * factor).astype(out[name].dtype)
    return out
```

```python
from contextlib import ExitStack

import numpy as np
import concourse.bass as bass
from concourse import mybir

F32 = mybir.dt.float32
F32R = mybir.dt.float32r
BF16 = mybir.dt.bfloat16
I32 = mybir.dt.int32
ACT = mybir.ActivationFunctionType
ALU = mybir.AluOpType
AX = mybir.AxisListType

P = 128
B, S, H = 128, 64, 128
HEADS, HD = 16, 8
HP = HEADS // 2
PAIRS = B * S // P
TILES = B * S // 512
NT = 4
EPS = 1e-5
MASKED = -1e30
TAKEN = 3e38
ABSENT = -1e30
LOOK = 3

LAYERS = (
    dict(rotary=True, experts=64, groups=True, topk=6, chunks=33, weighted=32, per_ce=1, hbufs=3,
         scale=1.0 / float(np.sqrt(HD))),
    dict(rotary=False, experts=8, groups=False, topk=2, chunks=32, weighted=32, per_ce=4, hbufs=4,
         scale=1.0 / float(np.sqrt(H))),
)
CHUNKS = 33


def need(eng, sem, value):
    if isinstance(value, int) and value <= 0:
        return
    eng.wait_ge(sem, value)


class Step:

    def __init__(self, i, off, count):
        self.i, self.off, self.count = i, off, count

    def n(self, k=0):
        return self.i * 2 + (self.off + k)

    def times(self, m, k=0, plus=0):
        return self.i * (2 * m) + (m * (self.off + k) + plus)

    def parity(self, k=0):
        return (self.off + k) % 2

    def of_parity(self, m, k=0):
        return self.i * m + m * ((self.off + k) // 2 + 1)

    def has(self, k=0):
        return not isinstance(self.i, int) or 0 <= self.n(k) < self.count


def run_steps(eng, step, first, loop_from, loop_to, last, count):
    for p in range(first, loop_from):
        step(Step(0, p, count))
    with eng.Fori(loop_from // 2, (loop_to + 1) // 2) as i:
        for s in range(2):
            step(Step(i, s, count))
    for p in range(loop_to + 1, last + 1):
        step(Step(0, p, count))


def build(nc, A, rotary, out):
    x_dram = A["x"].rearrange("b s d -> (b s) d").rearrange("(n p) d -> p n d", p=P)
    o_dram = out.rearrange("b s d -> (b s) d").rearrange("(n p) d -> p n d", p=P)
    ctx_dram = A["ctx_1024"].rearrange("b s d -> (b s) d")
    keep0_dram = A["mask_BxS2_if1"]
    keep1_dram = A["mask_Bx1xSxS2_ik1"].rearrange("b u q k -> (b u q) k")

    stack = ExitStack()
    with stack:
        def sb(name, shape, dt=F32):
            return stack.enter_context(nc.sbuf_tensor(name, shape, dt))

        def sem(name):
            return stack.enter_context(nc.semaphore(name))

        x_res = sb("x_res", [P, PAIRS, H])
        stats = sb("stats", [P, PAIRS, 6])
        mean = sb("mean", [P, PAIRS])
        rstd = sb("rstd", [P, PAIRS])
        ln_tmp = sb("ln_tmp", [P, 3, PAIRS])
        ident = sb("ident", [P, P])
        head_mask = sb("head_mask", [P, HEADS])
        spread = sb("spread", [P, 2, S], BF16)
        future = sb("future", [P, 2, S])
        cos_sin = sb("cos_sin", [P, 2, 2, S])
        gates = sb("gates", [P, 4])
        tanh_g = sb("tanh_g", [P, 4])
        gw_nat = sb("gw_nat", [64, H])
        wqk = sb("wqk", [P, 4, H])
        wv = sb("wv", [P, H])
        wo = sb("wo", [P, 2, 2, H])
        bias_col = sb("bias_col", [P, 4])
        one = sb("one", [1, 1])
        tick = sb("tick", [1, 1])
        bias_rot = sb("bias_rot", [P, 2, 2, S])
        bias_v = sb("bias_v", [P, H])
        bias_o = sb("bias_o", [P, H])
        gate_hi = sb("gate_hi", [P, CHUNKS, P], F32R)
        gate_lo = sb("gate_lo", [P, CHUNKS, P], F32R)
        up_hi = sb("up_hi", [P, CHUNKS, P], F32R)
        up_lo = sb("up_lo", [P, CHUNKS, P], F32R)
        down = sb("down", [P, CHUNKS, P])
        w_nat = down[:, 0:4, :]
        wo_nat = down[:, 4:6, :].rearrange("p h (c g d) -> p h c g d", c=2, g=HP)
        bias_row = down[0:1, 6:8, :]
        bias_perm = down[0:1, 8:12, :].rearrange("p (a q) h -> p a q h", a=2)
        stage = [sb(f"stage{i}", [P, 4, P]) for i in range(3)]
        select = sb("select", [P, 64 * 64], F32R)
        pick = sb("pick", [P, 64])
        router_hi = sb("router_hi", [P, 64], F32R)
        router_lo = sb("router_lo", [P, 64], F32R)
        router_bias = sb("router_bias", [P, 64])

        arena = sb("arena", [P, 10480])
        spot = [0]

        def area(*shape, parts=P):
            size = int(np.prod(shape))
            view = arena[0:parts, spot[0]:spot[0] + size]
            spot[0] += size
            if len(shape) == 2:
                view = view.rearrange("p (a b) -> p a b", a=shape[0])
            elif len(shape) == 3:
                view = view.rearrange("p (a b c) -> p a b c", a=shape[0], b=shape[1])
            elif len(shape) == 4:
                view = view.rearrange("p (a b c d) -> p a b c d", a=shape[0], b=shape[1], c=shape[2])
            return view

        q_blocks = [area(HP, 2, 2, S) for _ in range(2)]
        scores = [area(HP, 2, S) for _ in range(2)]
        probs_t = area(HP, P)
        x_norm = [area(H) for _ in range(2)]
        ctx_in = [area(H) for _ in range(2)]
        xc_t = [area(2, P) for _ in range(2)]
        qk_rot = [area(2, P) for _ in range(2)]
        v_blocks = [area(HP, 2, 2 * HD + 1) for _ in range(2)]
        rot_terms = area(2, 2, P)
        rot_sum = area(2, P)
        row_max = [area(HEADS) for _ in range(2)]
        row_rsum = area(HEADS)
        heads_out = [area(2, HP, HD) for _ in range(2)]
        heads_t = area(P)
        assert spot[0] <= 10480, spot
        keep_in = [sb(f"keep_in{i}", [P, S], I32) for i in range(2)]
        masked = [sb(f"masked{i}", [P, 2, S], BF16) for i in range(2)]

        spot[0] = 0
        silu_g = [area(512) for _ in range(2)]
        gated = [area(512) for _ in range(2)]
        hidden = [area(512) for _ in range(4)]
        y_t = area(512)
        xm_norm = area(NT, H)
        rt_score = area(NT, 64)
        rt_tmp = area(NT, 64)
        rt_masked = area(NT, 66)
        rt_marked = area(NT, 66)
        rt_weight = area(NT, 64)
        rt_group = area(NT, 14)
        rt_gmark = area(NT, 12)
        rt_gsel = area(NT, 8)
        rt_top = area(NT, 8)
        rt_gkeys = area(NT, 8)
        rt_keys = area(NT, 8)
        rt_sum = area(NT)
        rt_rsum = area(NT)
        assert spot[0] <= 10480, spot
        x_hi = [sb(f"x_hi{i}", [P, 512], F32R) for i in range(2)]
        x_lo = [sb(f"x_lo{i}", [P, 512], F32R) for i in range(2)]
        weight_t = [sb(f"weight_t{i}", [P, 512], F32R) for i in range(2)]
        weight_cat = sb("weight_cat", [P, NT, P], F32R)

        ps_s = stack.enter_context(nc.psum_tensor("ps_s", [P, 1024], F32))
        ps_t = stack.enter_context(nc.psum_tensor("ps_t", [P, 1024], F32))
        ps = [stack.enter_context(nc.psum_tensor(f"ps_{n}", [P, 512], F32)) for n in "abcd"]
        ps_a, ps_b, ps_c, ps_d = ps
        gate_ps = [ps_s[:, 0:512], ps_s[:, 512:1024]]
        up_ps = [ps_t[:, 0:512], ps_t[:, 512:1024]]
        weight_ps = [ps_a, ps_b]
        y_ps, misc_ps = ps_c, ps_d
        setup_ps = [ps_s[:, 0:512], ps_s[:, 512:1024], ps_t[:, 0:512], ps_t[:, 512:1024]]

        consts = sem("consts_built")
        const_dma = sem("constants_loaded")
        x_in = [sem(f"x_loaded{c}") for c in range(4)]
        bias_link = sem("bias_rotated")
        out_done = sem("out_stored")
        tanh_done = sem("tanh_of_gates")
        names_attn = ["small_in", "w_turned", "wo_arranged", "bias_turned", "attn_ready",
                      "stats_done", "var_done", "std_done", "ln_link", "cleared",
                      "x_norm", "ctx0", "ctx1", "keep0", "keep1", "turned_in", "xc_t", "projected", "v_projected", "rot_terms",
                      "rot_sum", "qk_rot", "q_blocks", "v_blocks", "masked", "qk", "row_max", "shifted", "exp",
                      "p_turned", "probs_t", "pv", "rsum", "heads_out", "heads_turned", "heads_t", "y", "x_mid",
                      "x_new"]
        names_moe = ["stage0", "stage1", "stage2", "w_turned", "w_hi", "w_lo", "w_down", "router_turned", "router_hi", "pick", "select", "router_in",
                     "sentinels", "stats_done", "var_done", "std_done", "ln_link",
                     "x_norm", "x_turned", "x_hi", "x_lo", "logits", "squashed", "rt", "weights_turned", "weight_t",
                     "gate_up", "ce", "silu", "gated", "hidden", "down", "y_kept", "y_turned", "x_new"]
        only_rotary = ("bias_turned", "rot_terms", "rot_sum")
        sa = [{n: sem(f"a{L}_{n}") for n in names_attn if L == 0 or n not in only_rotary} for L in range(2)]
        sm = [{n: sem(f"m{L}_{n}") for n in names_moe} for L in range(2)]

        block = stack.enter_context(nc.Block())

        def attn_loads(eng, L, s):
            W = {n: A[f"L{L}_xattn_{n}"] for n in ("Wq", "Wk", "Wv", "Wo")}
            if L == 1:
                eng.wait_ge(sm[0]["x_new"], TILES)
            for j, n in enumerate(("Wq", "Wk", "Wv", "Wo")):
                eng.dma_start(w_nat[:, j, :], W[n]).then_inc(s["small_in"], 16)
            bo = A[f"L{L}_xattn_bo"]
            eng.dma_start(bias_o[:], bo.partition_broadcast(P)).then_inc(s["small_in"], 16)
            if L == 0:
                eng.dma_start(bias_v[:], A["L0_xattn_bv"].partition_broadcast(P)).then_inc(s["small_in"], 16)
                for j, n in enumerate(("bq", "bk")):
                    eng.dma_start(bias_row[:, j, :], A[f"L0_xattn_{n}"].partition_broadcast(1))\
                       .then_inc(s["small_in"], 16)
                eng.dma_start(gates[:, 0:2], A["g_xattn"].partition_broadcast(P)).then_inc(s["small_in"], 16)
                eng.dma_start(gates[:, 2:4], A["g_ffn"].partition_broadcast(P)).then_inc(s["small_in"], 16)

        SMALL = (16 * 10, 16 * 5)

        def attn_stream(eng, L, s):
            def step(p):
                if not p.has():
                    return
                need(eng, s["turned_in"], p.n(-1))
                eng.dma_start(ctx_in[p.parity()], ctx_dram[bass.ds(p.times(P), P), :])\
                   .then_inc(s[f"ctx{p.parity()}"], 16)
                need(eng, s["masked"], p.times(2, -1))
                keep = s[f"keep{p.parity()}"]
                if L == 0:
                    for b in range(2):
                        eng.dma_start(keep_in[p.parity()][64 * b:64 * b + 64, :],
                                      keep0_dram[bass.ds(p.times(2, plus=b), 1), :].squeeze(0)
                                      .partition_broadcast(64)).then_inc(keep, 16)
                else:
                    eng.dma_start(keep_in[p.parity()][:], keep1_dram[bass.ds(p.times(P), P), :])\
                       .then_inc(keep, 16)
            run_steps(eng, step, 0, 4, 59, PAIRS - 1, PAIRS)

        def stage_jobs(L):
            jobs = []
            if L == 0:
                for kind, w, shared in (("gate", "eg_w", "sg_w"), ("up", "eu_w", "su_w"), ("down", "ed_w", "sd_w")):
                    full, sh = A[f"L0_ffn_{w}"], A[f"L0_ffn_{shared}"]
                    for j in range(8):
                        if kind == "down":
                            src = full[8 * j:8 * j + 8].rearrange("e h i -> h e i")
                        else:
                            src = full[8 * j:8 * j + 8].rearrange("(c e) i h -> (e i) c h", e=2)
                        jobs.append((src, 4, kind, 4 * j))
                    jobs.append((sh, 1, kind, 32))
            else:
                gup, dp = A["L1_ffn_gate_up_proj"], A["L1_ffn_down_proj"]
                for kind in ("gate", "up", "down"):
                    for e in range(8):
                        if kind == "down":
                            src = dp[e]
                        else:
                            at = 512 * (kind == "up")
                            src = gup[e, at:at + 512, :].rearrange("(c p) h -> p c h", p=P)
                        jobs.append((src, 4, kind, 4 * e))
            return jobs

        def moe_loads(eng, L, m):
            if L == 1:
                eng.wait_ge(sm[0]["x_new"], TILES)
            E = LAYERS[L]["experts"]
            eng.dma_start(gw_nat[0:E, :], A[f"L{L}_ffn_gate_w"]).then_inc(m["router_in"], 16)
            if L == 0:
                eng.dma_start(router_bias[:], A["L0_ffn_gate_bias"].partition_broadcast(P))\
                   .then_inc(m["router_in"], 16)
            for j, (src, n, kind, c) in enumerate(stage_jobs(L)):
                need(eng, m["w_turned"], j - 2)
                dst = stage[j % 3][:, 0:n, :]
                if kind == "down" and L == 0 and n == 4:
                    dst = dst.rearrange("p c (e i) -> p (c e) i", e=2)
                elif n == 1 or (kind == "down" and L == 1):
                    dst = dst.rearrange("p c h -> p (c h)")
                eng.dma_start(dst, src).then_inc(m[f"stage{j % 3}"], 16)

        @block.sync
        def _(sp):
            sp.dma_start(cos_sin[:], rotary).then_inc(const_dma, 16)
            attn_loads(sp, 0, sa[0])
            for c in range(4):
                sp.dma_start(x_res[:, 16 * c:16 * c + 16, :], x_dram[:, 16 * c:16 * c + 16, :]).then_inc(x_in[c], 16)
            moe_loads(sp, 0, sm[0])
            attn_stream(sp, 0, sa[0])
            attn_loads(sp, 1, sa[1])
            moe_loads(sp, 1, sm[1])
            attn_stream(sp, 1, sa[1])
            for c in range(TILES):
                sp.wait_ge(sm[1]["x_new"], c + 1)
                sp.dma_start(o_dram[:, NT * c:NT * c + NT, :], x_res[:, NT * c:NT * c + NT, :]).then_inc(out_done, 16)
            sp.wait_ge(out_done, 16 * TILES)

        def attn_pool(eng, L, s):
            g = nc.gpsimd
            if L == 1:
                eng.wait_ge(sm[0]["x_new"], TILES)
            for i in range(2):
                g.memset(q_blocks[i], 0.0).then_inc(s["cleared"], 1)
                g.memset(v_blocks[i], 0.0).then_inc(s["cleared"], 1)
                g.memset(masked[i][:], 0.0).then_inc(s["cleared"], 1)
            eng.wait_ge(s["cleared"], 6)
            for i in range(2):
                for b in range(2):
                    g.memset(v_blocks[i][64 * b:64 * b + 64, :, b, 2 * HD:2 * HD + 1], 1.0).then_inc(s["cleared"], 1)
            eng.wait_ge(s["cleared"], 10)
            eng.wait_ge(s["attn_ready"], 1)

            def step(p):
                if p.has(-2):
                    need(eng, s["x_mid"], p.n(-1))
                    need(eng, s["q_blocks"], p.times(8, 2) if p.has(1) else 8 * PAIRS)
                    row = x_res[:, bass.ds(p.n(-2), 1), :].squeeze(1)
                    g.tensor_tensor(row, row, bias_o[:], ALU.add).then_inc(s["x_new"], 1)
                if p.has(2):
                    par = p.parity()
                    if L == 0:
                        need(eng, s["rot_sum"], p.n(3))
                        need(eng, s["qk"], p.n(1))
                        need(eng, s["q_blocks"], p.times(8, 2))
                        g.tensor_tensor(qk_rot[par], rot_sum, bias_rot[:].rearrange("p a b s -> p a (b s)"),
                                        ALU.add).then_inc(s["qk_rot"], 1)
                    need(eng, s["qk_rot"], p.n(3))
                    need(eng, s["qk"], p.n(1))
                    need(eng, s["x_new"], p.n(-1))
                    for hp in range(HP):
                        rows = slice(32 * (hp // 2), 32 * (hp // 2) + 32)
                        g.tensor_tensor(q_blocks[par][rows, hp].rearrange("p b h s -> p h b s"),
                                        qk_rot[par][rows, 0, :].rearrange("p (b s) -> p b s", b=2).unsqueeze(1)
                                        .to_broadcast([32, 2, 2, S]),
                                        head_mask[rows, 2 * hp:2 * hp + 2].unsqueeze(2).unsqueeze(3)
                                        .to_broadcast([32, 2, 2, S]), ALU.mult).then_inc(s["q_blocks"], 1)
            run_steps(eng, step, -2, 4, 59, PAIRS + 1, PAIRS)

        def moe_pool(eng, L, m):
            g = nc.gpsimd
            eng.wait_ge(sa[L]["x_new"], PAIRS)
            eng.wait_ge(sa[L]["heads_t"], PAIRS)
            k = LAYERS[L]["topk"]
            n = LAYERS[L]["experts"]
            g.memset(rt_masked, ABSENT).then_inc(m["sentinels"], 1)
            g.memset(rt_group, ABSENT).then_inc(m["sentinels"], 1)
            g.memset(rt_keys, ABSENT).then_inc(m["sentinels"], 1)
            g.memset(rt_gkeys, ABSENT).then_inc(m["sentinels"], 1)

        @block.gpsimd
        def _(pool):
            g = nc.gpsimd
            g.memset(ident[:], 0.0).then_inc(consts, 1)
            g.memset(head_mask[:], 1.0).then_inc(consts, 1)
            g.memset(spread[:], 0.0).then_inc(consts, 1)
            g.memset(future[:], 1.0).then_inc(consts, 1)
            g.memset(one[:], 1.0).then_inc(consts, 1)
            g.memset(wo[:], 0.0).then_inc(consts, 1)
            pool.wait_ge(consts, 6)
            g.affine_select(out=ident[:], in_=ident[:], compare_op=ALU.not_equal, fill=1.0, base=0,
                            pattern=[[-1, P]], channel_multiplier=1).then_inc(consts, 1)
            g.affine_select(out=head_mask[:], in_=head_mask[:], compare_op=ALU.is_ge, fill=0.0, base=0,
                            pattern=[[-HD, HEADS]], channel_multiplier=1).then_inc(consts, 1)
            g.affine_select(out=spread[:], in_=spread[:], compare_op=ALU.not_equal, fill=MASKED, base=0,
                            pattern=[[0, 2], [-1, S]], channel_multiplier=1).then_inc(consts, 1)
            g.affine_select(out=future[:], in_=future[:], compare_op=ALU.is_ge, fill=0.0, base=-1,
                            pattern=[[S, 2], [1, S]], channel_multiplier=-1).then_inc(consts, 1)
            pool.wait_ge(consts, 10)
            g.affine_select(out=head_mask[:], in_=head_mask[:], compare_op=ALU.is_ge, fill=0.0, base=HD - 1,
                            pattern=[[HD, HEADS]], channel_multiplier=-1).then_inc(consts, 1)
            g.affine_select(out=spread[:], in_=spread[:], compare_op=ALU.not_equal, fill=MASKED, base=-S,
                            pattern=[[0, 2], [-1, S]], channel_multiplier=1).then_inc(consts, 1)
            pool.wait_ge(consts, 12)
            for L in range(2):
                attn_pool(pool, L, sa[L])
                moe_pool(pool, L, sm[L])

        CONSTS = 12
        RT = (30, 24)

        def attn_pe_setup(eng, L, s):
            t = nc.tensor
            if L == 0:
                eng.wait_ge(consts, CONSTS)
            else:
                eng.wait_ge(sm[0]["x_new"], TILES)
            eng.wait_ge(s["small_in"], SMALL[L])
            for j in range(3):
                mm = t.transpose(ps_a[:, P * j:P * j + P], w_nat[:, j, :], ident[:])
            mm.then_inc(s["w_turned"], 1)
            eng.wait_ge(s["wo_arranged"], 2)
            for j in range(2):
                mm = t.transpose(ps_b[:, P * j:P * j + P], wo_nat[:, j].rearrange("p c g d -> p (c g d)"), ident[:])
            mm.then_inc(s["w_turned"], 1)
            if L == 0:
                eng.wait_ge(s["bias_turned"], 4)
                for j in range(4):
                    mm = t.matmul(ps_c[:, j:j + 1], bias_perm[0:1, j // 2, j % 2, :], one[0:1, 0:1],
                                  start=True, stop=True)
                mm.then_inc(s["w_turned"], 1)

        def attn_pe(eng, L, s):
            t = nc.tensor
            eng.wait_ge(s["attn_ready"], 1)
            eng.wait_ge(s["cleared"], 10)

            def step(p):
                par = p.parity()
                if p.has():
                    need(eng, s["q_blocks"], p.times(8, 1))
                    need(eng, s["masked"], p.times(2, 1))
                    need(eng, s["shifted"], p.n())
                    for half in range(2):
                        t.matmul(ps_s[:, 512 * half:512 * half + 512], spread[:].rearrange("p a s -> p (a s)"),
                                 masked[par][:].rearrange("p b k -> p (b k)").unsqueeze(1).to_broadcast([P, 4, P]),
                                 start=True, stop=True, skip_group_check=True)
                        for n in range(8):
                            hp, b = 4 * half + n // 2, n % 2
                            mm = t.matmul(ps_s[:, P * hp + S * b:P * hp + S * b + S],
                                          q_blocks[par][:, hp, b].rearrange("p h s -> p (h s)"),
                                          qk_rot[par][:, 1, S * b:S * b + S], start=False, stop=True,
                                          skip_group_check=True)
                    mm.then_inc(s["qk"], 1)
                if p.has(-2):
                    need(eng, s["heads_out"], p.times(2, -1))
                    need(eng, s["x_mid"], p.n(-2))
                    t.transpose(ps_d[:, 0:P], heads_out[par].rearrange("p b g d -> p (b g d)"), ident[:])\
                     .then_inc(s["heads_turned"], 1)
                if p.has(-1):
                    need(eng, s["exp"], p.n())
                    need(eng, s["probs_t"], p.n(-1))
                    q = p.parity(-1)
                    for hp in range(HP):
                        mm = t.transpose(ps_t[:, P * hp:P * hp + P],
                                         scores[q][:, hp].rearrange("p b k -> p (b k)"), ident[:])
                    mm.then_inc(s["p_turned"], 1)
                if p.has(-2):
                    need(eng, s["heads_t"], p.n(-1))
                    for b in range(2):
                        rows = slice(S * b, S * b + S)
                        for h in range(2):
                            mm = t.matmul(ps_d[rows, P:2 * P], heads_t[:, S * h:S * h + S], wo[:, b, h, :],
                                          start=(h == 0), stop=(h == 1))
                    mm.then_inc(s["y"], 1)
                if p.has(1):
                    need(eng, s["xc_t"], p.n(2))
                    need(eng, s["v_blocks"], p.times(2, 1))
                    t.matmul(ps_c[:, 0:P], xc_t[p.parity(1)][:, 1, :], wv[:], start=True, stop=True)\
                     .then_inc(s["v_projected"], 1)
                if p.has(3):
                    q = p.parity(3)
                    need(eng, s["x_norm"], p.n(4))
                    need(eng, s[f"ctx{q}"], p.of_parity(16, 3))
                    need(eng, s["heads_out"], p.times(2, -1))
                    need(eng, s["xc_t"], p.n(3))
                    t.transpose(ps_a[:, 0:P], x_norm[q], ident[:])
                    t.transpose(ps_a[:, P:2 * P], ctx_in[q], ident[:]).then_inc(s["turned_in"], 1)
                if p.has(2):
                    need(eng, s["xc_t"], p.n(3))
                    need(eng, s["rot_terms" if L == 0 else "qk_rot"], p.n(2))
                    for j in range(4 if L == 0 else 2):
                        mm = t.matmul(ps_b[:, P * j:P * j + P], wqk[:, j, :], xc_t[par][:, j % 2, :],
                                      start=True, stop=True)
                    mm.then_inc(s["projected"], 1)
                if p.has(-1):
                    q = p.parity(-1)
                    need(eng, s["probs_t"], p.n())
                    need(eng, s["v_blocks"], p.times(2))
                    if p.has(3):
                        need(eng, s["xc_t"], p.n(4))
                    else:
                        need(eng, s["heads_out"], p.times(2, -1))
                    for hp in range(HP):
                        mm = t.matmul(ps_a[:, 34 * hp:34 * hp + 34], probs_t[:, hp, :],
                                      v_blocks[q][:, hp].rearrange("p b c -> p (b c)"), start=True, stop=True)
                    mm.then_inc(s["pv"], 1)
            run_steps(eng, step, -3, 4, 59, PAIRS + 1, PAIRS)

        def moe_pe_setup(eng, L, m):
            t = nc.tensor
            E = LAYERS[L]["experts"]
            eng.wait_ge(m["router_in"], 32 if L == 0 else 16)
            t.transpose(misc_ps[:, 0:E], gw_nat[0:E, :], ident[0:E, 0:E]).then_inc(m["router_turned"], 1)
            for j, (_, n, kind, c) in enumerate(stage_jobs(L)):
                eng.wait_ge(m[f"stage{j % 3}"], 16 * (j // 3 + 1))
                kept = [i for i in range(j) if i % 4 == j % 4]
                if kept:
                    jobs = stage_jobs(L)[:kept[-1] + 1]
                    need(eng, m["w_lo"], sum(k != "down" for _, _, k, _ in jobs))
                    need(eng, m["w_down"], sum(k == "down" for _, _, k, _ in jobs))
                for q in range(n):
                    mm = t.transpose(setup_ps[j % 4][:, P * q:P * q + P], stage[j % 3][:, q, :], ident[:])
                mm.then_inc(m["w_turned"], 1)

        def moe_chunks(L):
            return LAYERS[L]["chunks"]

        def run_tiles(eng, L, slot):
            C = moe_chunks(L)
            for c in range(-LOOK, 0):
                slot(Step(0, 0, TILES), c)
            for s in range(2):
                for c in range(C):
                    slot(Step(0, s, TILES), c)
            with eng.Fori(1, (TILES - 2) // 2) as i:
                for s in range(2):
                    for c in range(C):
                        slot(Step(i, s, TILES), c)
            for s in range(TILES - 2, TILES):
                for c in range(C):
                    slot(Step(0, s, TILES), c)

        def ahead(L, t, c, k):
            C = moe_chunks(L)
            c += k
            if c < 0:
                return None
            if c < C:
                return t, c
            if not t.has(1):
                return None
            return Step(t.i, t.off + 1, TILES), c - C

        def before(L, n):
            per = LAYERS[L]["per_ce"]
            return per * (n + 1)

        def moe_pe(eng, L, m):
            t_ = nc.tensor
            cfg = LAYERS[L]
            C, E, per = cfg["chunks"], cfg["experts"], cfg["per_ce"]
            rows = 2 * E

            def hook(name, t):
                if name == "turn_y" and (t.has(-1)):
                    need(eng, m["y_kept"], t.n())
                    need(eng, m["weight_t"], t.n(1))
                    for q in range(NT):
                        mm = t_.transpose(misc_ps[:, P * q:P * q + P], y_t[:, P * q:P * q + P], ident[:])
                    mm.then_inc(m["y_turned"], 1)
                if not t.has(1):
                    return
                par = t.parity(1)
                if name == "turn_x":
                    need(eng, m["x_norm"], t.n(2))
                    need(eng, m["x_new"], t.n())
                    need(eng, m["weight_t"], t.n(1))
                    for q in range(NT):
                        mm = t_.transpose(misc_ps[:, P * q:P * q + P], xm_norm[:, q, :], ident[:])
                    mm.then_inc(m["x_turned"], 1)
                if name == "logits":
                    need(eng, m["x_lo"], t.n(2))
                    for q in range(NT):
                        toks = slice(P * q, P * q + P)
                        for n, (a, b) in enumerate(((x_hi, router_hi), (x_lo, router_hi), (x_hi, router_lo))):
                            mm = t_.matmul(misc_ps[:, E * q:E * q + E], a[par][:, toks], b[:, 0:E],
                                           start=(n == 0), stop=(n == 2))
                    mm.then_inc(m["logits"], 1)
                if name == "turn_weights":
                    need(eng, m["rt"], t.times(RT[L], 2))
                    for q in range(NT):
                        mm = t_.transpose(misc_ps[0:rows, P * q:P * q + P], weight_cat[:, q, 0:rows].bitcast(F32),
                                          ident[:])
                    mm.then_inc(m["weights_turned"], 1)

            def gate_up(t, c):
                par = t.parity()
                g = t.times(C, plus=c)
                k = (t.off * C + c) % 2
                if c == 0:
                    need(eng, m["x_lo"], t.n(1))
                need(eng, m["silu"], t.times(C, plus=c - 1))
                need(eng, m["gated"], t.times(C, plus=c - 1))
                for dst, hi, lo in ((gate_ps[k], gate_hi, gate_lo), (up_ps[k], up_hi, up_lo)):
                    t_.matmul(dst, hi[:, c, :], x_hi[par][:], start=True, stop=False)
                    t_.matmul(dst, hi[:, c, :], x_lo[par][:], start=False, stop=False)
                    mm = t_.matmul(dst, lo[:, c, :], x_hi[par][:], start=False, stop=True)
                mm.then_inc(m["gate_up"], 1)
                if c < cfg["weighted"] and c % per == 0:
                    n = c // per
                    if c == 0:
                        need(eng, m["weight_t"], t.n(1))
                    N = cfg["weighted"] // per
                    if n >= 2:
                        need(eng, m["hidden"], t.times(C, plus=per * (n - 1)))
                    elif t.has(-1):
                        need(eng, m["hidden"], t.times(C, -1, per * (N + n - 1)))
                    if L == 0:
                        lhs = select[:, P * c:P * c + P]
                    else:
                        lhs = select[0:rows, P * n:P * n + P]
                    t_.matmul(weight_ps[n % 2][:], lhs, weight_t[par][0:rows, :], start=True, stop=True)\
                      .then_inc(m["ce"], 1)

            def down_product(t, c):
                need(eng, m["hidden"], t.times(C, plus=c + 1))
                if c == 0:
                    need(eng, m["y_kept"], t.n())
                k = (t.off * C + c) % cfg["hbufs"]
                t_.matmul(y_ps[:], down[:, c, :], hidden[k], start=(c == 0), stop=(c == C - 1))\
                  .then_inc(m["down"], 1)

            def slot(t, c):
                nxt = ahead(L, t, c, LOOK)
                if nxt:
                    gate_up(*nxt)
                if c >= 0:
                    down_product(t, c)
                for at, name in ((2, "turn_y"), (6, "turn_x"), (9, "logits"), (C - 8, "turn_weights")):
                    if c == at:
                        hook(name, t)

            eng.wait_ge(sa[L]["x_new"], PAIRS)
            eng.wait_ge(m["select"], 2)
            start = Step(0, -1, TILES)
            for name in ("turn_x", "logits", "turn_weights"):
                hook(name, start)
            jobs = stage_jobs(L)
            eng.wait_ge(m["w_lo"], sum(k != "down" for _, _, k, _ in jobs))
            eng.wait_ge(m["w_down"], sum(k == "down" for _, _, k, _ in jobs))
            run_tiles(eng, L, slot)
            need(eng, m["y_kept"], TILES)
            for q in range(NT):
                mm = t_.transpose(misc_ps[:, P * q:P * q + P], y_t[:, P * q:P * q + P], ident[:])
            mm.then_inc(m["y_turned"], 1)

        @block.tensor
        def _(pe):
            for L in range(2):
                attn_pe_setup(pe, L, sa[L])
                moe_pe_setup(pe, L, sm[L])
                attn_pe(pe, L, sa[L])
                moe_pe(pe, L, sm[L])

        def std(eng, s):
            eng.wait_ge(s["var_done"], 1)
            nc.scalar.activation(ln_tmp[:, 0, :], ln_tmp[:, 2, :], ACT.Sqrt).then_inc(s["std_done"], 1)

        def attn_act(eng, L, s):
            a = nc.scalar
            std(eng, s)
            scale = LAYERS[L]["scale"]

            def step(p):
                par = p.parity()
                if p.has(-2):
                    need(eng, s["heads_turned"], p.n(-1))
                    need(eng, s["y"], p.n(-2))
                    a.copy(heads_t, ps_d[:, 0:P]).then_inc(s["heads_t"], 1)
                if p.has(-1):
                    need(eng, s["p_turned"], p.n())
                    need(eng, s["pv"], p.n(-1))
                    a.copy(probs_t.rearrange("p a b -> p (a b)"), ps_t[:]).then_inc(s["probs_t"], 1)
                if p.has(3):
                    need(eng, s["turned_in"], p.n(4))
                    need(eng, s["v_projected"], p.n(2))
                    a.copy(xc_t[p.parity(3)].rearrange("p a b -> p (a b)"), ps_a[:, 0:2 * P]).then_inc(s["xc_t"], 1)
                if L == 1 and p.has(2):
                    need(eng, s["projected"], p.n(3))
                    need(eng, s["qk"], p.n(1))
                    a.copy(qk_rot[par].rearrange("p a b -> p (a b)"), ps_b[:, 0:2 * P])\
                     .then_inc(s["qk_rot"], 1)
                if p.has():
                    need(eng, s["shifted"], p.n(1))
                    flat = scores[par].rearrange("p g b k -> p (g b k)")
                    a.activation(flat, flat, ACT.Exp, scale=scale).then_inc(s["exp"], 1)
            run_steps(eng, step, -3, 4, 59, PAIRS + 1, PAIRS)

        def moe_act_setup(eng, L, m):
            a = nc.scalar
            E = LAYERS[L]["experts"]
            eng.wait_ge(m["router_turned"], 1)
            a.copy(router_hi[:, 0:E], misc_ps[:, 0:E]).then_inc(m["router_hi"], 1)
            for j, (_, n, kind, c) in enumerate(stage_jobs(L)):
                eng.wait_ge(m["w_turned"], j + 1)
                dst = {"gate": gate_hi, "up": up_hi, "down": down}[kind]
                ins = a.copy(dst[:, c:c + n, :].rearrange("p c h -> p (c h)"), setup_ps[j % 4][:, 0:P * n])
                ins.then_inc(m["w_down" if kind == "down" else "w_hi"], 1)

        def moe_act(eng, L, m):
            a = nc.scalar
            cfg = LAYERS[L]
            C, E = cfg["chunks"], cfg["experts"]

            def hook(name, t):
                if name == "keep_y" and t.has(-1):
                    need(eng, m["down"], t.times(C))
                    need(eng, m["y_turned"], t.n(-1))
                    a.copy(y_t, y_ps[:]).then_inc(m["y_kept"], 1)
                if not t.has(1):
                    return
                par = t.parity(1)
                if name == "x_hi":
                    need(eng, m["x_turned"], t.n(2))
                    need(eng, m["gate_up"], t.times(C))
                    a.copy(x_hi[par][:], misc_ps[:]).then_inc(m["x_hi"], 1)
                if name == "squash" and L == 0:
                    need(eng, m["logits"], t.n(2))
                    a.activation(rt_tmp.rearrange("p a b -> p (a b)"), misc_ps[:, 0:NT * E], ACT.Tanh, scale=0.5)\
                     .then_inc(m["squashed"], 1)
                if name == "squash" and L == 1:
                    need(eng, m["rt"], t.times(RT[L], 1, 2))
                    a.activation(rt_tmp[:, :, 0:E], rt_group[:, :, 0:E], ACT.Tanh, scale=-0.5)\
                     .then_inc(m["squashed"], 1)
                if name == "weight_t":
                    need(eng, m["weights_turned"], t.n(2))
                    need(eng, m["ce"], t.times(cfg["weighted"] // cfg["per_ce"]))
                    a.copy(weight_t[par][0:2 * E, :], misc_ps[0:2 * E, :]).then_inc(m["weight_t"], 1)

            def slot(t, c):
                if c == 0:
                    hook("keep_y", t)
                nxt = ahead(L, t, c, LOOK)
                if nxt:
                    u, k = nxt
                    need(eng, m["gate_up"], u.times(C, plus=k + 1))
                    need(eng, m["gated"], u.times(C, plus=k - 1))
                    par = (u.off * C + k) % 2
                    a.activation(silu_g[par], gate_ps[par], ACT.Silu).then_inc(m["silu"], 1)
                for at, name in ((6, "x_hi"), (11, "squash"), (C - 7, "weight_t")):
                    if c == at:
                        hook(name, t)

            std(eng, m)
            start = Step(0, -1, TILES)
            for name in ("x_hi", "squash", "weight_t"):
                hook(name, start)
            run_tiles(eng, L, slot)
            need(eng, m["down"], TILES * C)
            need(eng, m["y_turned"], TILES - 1)
            a.copy(y_t, y_ps[:]).then_inc(m["y_kept"], 1)

        @block.scalar
        def _(act):
            for L in range(2):
                if L == 0:
                    act.wait_ge(sa[0]["small_in"], SMALL[0])
                    nc.scalar.activation(tanh_g[:], gates[:], ACT.Tanh).then_inc(tanh_done, 1)
                moe_act_setup(act, L, sm[L])
                attn_act(act, L, sa[L])
                moe_act(act, L, sm[L])

        def layer_norm_scales(eng, s):
            v = nc.vector
            eng.wait_ge(s["stats_done"], PAIRS)
            me, qe, mo, qo = stats[:, :, 1], stats[:, :, 2], stats[:, :, 4], stats[:, :, 5]
            v.tensor_tensor(ln_tmp[:, 0, :], me, mo, ALU.subtract).then_inc(s["ln_link"], 1)
            v.tensor_tensor(ln_tmp[:, 1, :], qe, qo, ALU.add).then_inc(s["ln_link"], 1)
            v.tensor_tensor(mean[:], me, mo, ALU.add).then_inc(s["ln_link"], 1)
            eng.wait_ge(s["ln_link"], 3)
            v.scalar_tensor_tensor(ln_tmp[:, 2, :], ln_tmp[:, 0, :], 0.25, ln_tmp[:, 0, :], ALU.mult, ALU.mult)\
             .then_inc(s["ln_link"], 1)
            v.tensor_scalar(mean[:], mean[:], 0.5, None, ALU.mult).then_inc(s["ln_link"], 1)
            v.tensor_scalar(ln_tmp[:, 1, :], ln_tmp[:, 1, :], 1.0 / H, EPS, ALU.mult, ALU.add)\
             .then_inc(s["ln_link"], 1)
            eng.wait_ge(s["ln_link"], 6)
            v.tensor_tensor(ln_tmp[:, 2, :], ln_tmp[:, 2, :], ln_tmp[:, 1, :], ALU.add).then_inc(s["var_done"], 1)
            eng.wait_ge(s["std_done"], 1)
            v.reciprocal(rstd[:], ln_tmp[:, 0, :]).then_inc(s["ln_link"], 1)
            eng.wait_ge(s["ln_link"], 7)

        def attn_dve_setup(eng, L, s):
            v = nc.vector
            eng.wait_ge(s["small_in"], SMALL[L])
            if L == 0:
                eng.wait_ge(tanh_done, 1)
            else:
                eng.wait_ge(sm[0]["x_new"], TILES)
            by_head = w_nat[:, 3, :].rearrange("p (g h d) -> p h g d", g=HP, h=2)
            for copy in range(2):
                v.tensor_copy(wo_nat[:, :, copy], by_head).then_inc(s["wo_arranged"], 1)
            eng.wait_ge(s["w_turned"], 1)
            if L == 0:
                for j in range(2):
                    src = ps_a[:, P * j:P * j + P].rearrange("p (h j r) -> p h r j", h=HEADS, r=2)
                    for half in range(2):
                        for ab in range(2):
                            dst = wqk[:, 2 * ab + j, :].rearrange("p (h r j) -> p h r j", h=HEADS, r=2)
                            v.tensor_copy(dst[:, :, half, :], src[:, :, (half + ab) % 2, :])
                rows = bias_row.rearrange("p q (h j r) -> p q h r j", h=HEADS, r=2)
                for ab in range(2):
                    for half in range(2):
                        dst = bias_perm[:, ab].rearrange("p q (h r j) -> p q h r j", h=HEADS, r=2)
                        for q in range(2):
                            ins = v.tensor_copy(dst[:, q, :, half, :], rows[:, q, :, (half + ab) % 2, :])
                        ins.then_inc(s["bias_turned"], 1)
            else:
                v.tensor_copy(wqk[:, 0:2, :].rearrange("p a b -> p (a b)"), ps_a[:, 0:2 * P])
            v.tensor_copy(wv[:], ps_a[:, 2 * P:3 * P])
            eng.wait_ge(s["w_turned"], 2)
            eng.wait_ge(consts, CONSTS)
            for b in range(2):
                rows = slice(S * b, S * b + S)
                v.tensor_scalar(wo[rows, b].rearrange("p a b -> p (a b)"), ps_b[rows, 0:2 * P],
                                tanh_g[rows, L:L + 1], None, ALU.mult)
            last = v.tensor_scalar(bias_o[:], bias_o[:], tanh_g[:, L:L + 1], None, ALU.mult)
            if L == 0:
                eng.wait_ge(s["w_turned"], 3)
                eng.wait_ge(const_dma, 16)
                v.tensor_copy(bias_col[:], ps_c[:, 0:4]).then_inc(bias_link, 1)
                eng.wait_ge(bias_link, 1)
                for q in range(2):
                    v.tensor_scalar(bias_rot[:, q].rearrange("p b s -> p (b s)"),
                                    cos_sin[:, 0].rearrange("p b s -> p (b s)"), bias_col[:, q:q + 1], None, ALU.mult)\
                     .then_inc(bias_link, 1)
                eng.wait_ge(bias_link, 3)
                for q in range(2):
                    flat = bias_rot[:, q].rearrange("p b s -> p (b s)")
                    last = v.scalar_tensor_tensor(flat, cos_sin[:, 1].rearrange("p b s -> p (b s)"),
                                                  bias_col[:, 2 + q:3 + q], flat, ALU.mult, ALU.add)
            last.then_inc(s["attn_ready"], 1)
            eng.wait_ge(s["attn_ready"], 1)

        def moe_dve_setup(eng, L, m):
            v = nc.vector
            E = LAYERS[L]["experts"]
            if L == 0:
                eng.wait_ge(consts, CONSTS)
            v.tensor_tensor(pick[:, 0:E], ident[:, 0:E], ident[:, E:2 * E], ALU.add).then_inc(m["pick"], 1)
            eng.wait_ge(m["pick"], 1)
            eng.wait_ge(m["router_hi"], 1)
            width = 64 if L == 0 else P
            v.tensor_copy(select[:, 0:E * width].rearrange("p (e m) -> p e m", e=E),
                          pick[:, 0:E].unsqueeze(2).to_broadcast([P, E, width])).then_inc(m["select"], 1)
            v.tensor_tensor(router_lo[:, 0:E], misc_ps[:, 0:E], router_hi[:, 0:E].bitcast(F32), ALU.subtract)\
             .then_inc(m["select"], 1)
            n_lo = 0
            for j, (_, n, kind, c) in enumerate(stage_jobs(L)):
                if kind == "down":
                    continue
                n_lo += 1
                eng.wait_ge(m["w_hi"], n_lo)
                hi, lo = (gate_hi, gate_lo) if kind == "gate" else (up_hi, up_lo)
                v.tensor_tensor(lo[:, c:c + n, :].rearrange("p c h -> p (c h)"), setup_ps[j % 4][:, 0:P * n],
                                hi[:, c:c + n, :].bitcast(F32).rearrange("p c h -> p (c h)"), ALU.subtract)\
                 .then_inc(m["w_lo"], 1)

        def attn_dve(eng, L, s):
            v = nc.vector
            m = sm[L]
            layer_norm_scales(eng, s)
            eng.wait_ge(s["cleared"], 10)

            def step(p):
                par = p.parity()
                if p.has():
                    need(eng, s["qk"], p.n(1))
                    v.tensor_reduce(row_max[par], ps_s[:].rearrange("p (r k) -> p r k", k=S), AX.X, ALU.max)\
                     .then_inc(s["row_max"], 1)
                if p.has(4):
                    need(eng, s["turned_in"], p.n(3))
                    v.tensor_scalar(x_norm[par], x_res[:, bass.ds(p.n(4), 1), :].squeeze(1),
                                    mean[:, bass.ds(p.n(4), 1)], rstd[:, bass.ds(p.n(4), 1)],
                                    ALU.subtract, ALU.mult).then_inc(s["x_norm"], 1)
                if p.has():
                    need(eng, s["row_max"], p.n(1))
                    need(eng, s["p_turned"], p.n(-1))
                    v.tensor_tensor(scores[par].rearrange("p g b k -> p (g b) k"),
                                    ps_s[:].rearrange("p (r k) -> p r k", k=S),
                                    row_max[par].unsqueeze(2).to_broadcast([P, HEADS, S]), ALU.subtract)\
                     .then_inc(s["shifted"], 1)
                if p.has(-2):
                    need(eng, s["y"], p.n(-1))
                    row = x_res[:, bass.ds(p.n(-2), 1), :].squeeze(1)
                    v.tensor_tensor(row, ps_d[:, P:2 * P], row, ALU.add).then_inc(s["x_mid"], 1)
                if p.has(-3):
                    need(eng, s["x_new"], p.n(-2))
                    v.bn_stats(stats[:, bass.ds(p.n(-3), 1), :].squeeze(1),
                               x_res[:, bass.ds(p.n(-3), 1), :].squeeze(1)).then_inc(m["stats_done"], 1)
                if p.has(1):
                    q = p.parity(1)
                    need(eng, s[f"keep{q}"], p.of_parity(32 if L == 0 else 16, 1))
                    need(eng, s["qk"], p.n())
                    for b in range(2):
                        rows = slice(S * b, S * b + S)
                        if L == 0:
                            ins = v.scalar_tensor_tensor(masked[q][rows, b, :], keep_in[q][rows, :], 0.0,
                                                         future[rows, b, :], ALU.is_equal, ALU.max)
                        else:
                            ins = v.tensor_scalar(masked[q][rows, b, :], keep_in[q][rows, :], 0.0, None, ALU.is_equal)
                        ins.then_inc(s["masked"], 1)
                if L == 0 and p.has(2):
                    need(eng, s["projected"], p.n(3))
                    need(eng, s["rot_sum"], p.n(2))
                    v.tensor_tensor(rot_terms, ps_b[:].rearrange("p (a q t) -> p a q t", a=2, q=2),
                                    cos_sin[:].rearrange("p a b s -> p a (b s)").unsqueeze(2)
                                    .to_broadcast([P, 2, 2, P]), ALU.mult).then_inc(s["rot_terms"], 1)
                if p.has(1):
                    q = p.parity(1)
                    need(eng, s["v_projected"], p.n(2))
                    need(eng, s["pv"], p.n())
                    for b in range(2):
                        rows = slice(S * b, S * b + S)
                        dst = v_blocks[q][rows, :, b, 0:2 * HD]
                        src = ps_c[rows, 0:P].rearrange("p (g c) -> p g c", g=HP)
                        if L == 0:
                            ins = v.tensor_tensor(dst, src, bias_v[rows, :].rearrange("p (g c) -> p g c", g=HP),
                                                  ALU.add)
                        else:
                            ins = v.tensor_copy(dst, src)
                        ins.then_inc(s["v_blocks"], 1)
                if L == 0 and p.has(2):
                    need(eng, s["rot_terms"], p.n(3))
                    need(eng, s["qk_rot"], p.n(2))
                    v.tensor_tensor(rot_sum, rot_terms[:, 0], rot_terms[:, 1], ALU.add)\
                     .then_inc(s["rot_sum"], 1)
                if p.has(-1):
                    q = p.parity(-1)
                    need(eng, s["pv"], p.n())
                    need(eng, s["heads_out"], p.times(2, -1))
                    sums = ps_a[:, 0:34 * HP].rearrange("p (r c) -> p r c", c=2 * HD + 1)
                    v.reciprocal(row_rsum, sums[:, :, 2 * HD]).then_inc(s["rsum"], 1)
                    need(eng, s["rsum"], p.n())
                    need(eng, s["heads_turned"], p.n(-2))
                    for h in range(2):
                        rows = slice(S * h, S * h + S)
                        src = ps_a[rows, 0:34 * HP].rearrange("p (g b c) -> p g b c", g=HP, b=2)
                        v.tensor_tensor(heads_out[q][rows].rearrange("p b g d -> p g b d"),
                                        src[:, :, :, HD * h:HD * h + HD],
                                        row_rsum[rows].rearrange("p (g b) -> p g b", g=HP).unsqueeze(3)
                                        .to_broadcast([S, HP, 2, HD]), ALU.mult).then_inc(s["heads_out"], 1)
            run_steps(eng, step, -4, 4, 59, PAIRS + 2, PAIRS)

        def moe_dve(eng, L, m):
            v = nc.vector
            cfg = LAYERS[L]
            C, E, K = cfg["chunks"], cfg["experts"], cfg["topk"]
            nxt_stats = sa[1] if L == 0 else None
            layer_norm_scales(eng, m)
            eng.wait_ge(m["sentinels"], 4)

            def each(f):
                return [lambda q=q: f(q) for q in range(NT)]

            def keep_keys(dst, n):
                return lambda: v.tensor_copy(dst[:, :, 0:n], rt_top[:, :, 0:n])

            choose = [
                each(lambda q: v.max(rt_top[:, q, :], (rt_masked if L == 0 else rt_group)[:, q, 0:E])),
                [keep_keys(rt_keys, K)],
                each(lambda q: v.match_replace(rt_marked[:, q, 0:E + 8 - K], rt_keys[:, q, :],
                                               (rt_masked if L == 0 else rt_group)[:, q, 0:E + 8 - K], TAKEN)),
                [lambda: v.scalar_tensor_tensor(rt_weight[:, :, 0:E], rt_marked[:, :, 0:E], TAKEN,
                                                rt_masked[:, :, 0:E], ALU.is_equal, ALU.mult)],
                [lambda: v.tensor_reduce(rt_sum, rt_weight[:, :, 0:E], AX.X, ALU.add)],
            ]
            if L == 0:
                choose.append([lambda: v.tensor_scalar(rt_sum, rt_sum, 1e-8, None, ALU.add)])
            choose += [
                [lambda: v.reciprocal(rt_rsum, rt_sum)],
                [lambda: v.tensor_tensor(rt_weight[:, :, 0:E], rt_weight[:, :, 0:E],
                                         rt_rsum.unsqueeze(2).to_broadcast([P, NT, E]), ALU.mult)],
                [lambda: v.tensor_copy(weight_cat[:, :, 0:E], rt_weight[:, :, 0:E])],
                [lambda: v.tensor_tensor(weight_cat[:, :, E:2 * E], rt_weight[:, :, 0:E],
                                         weight_cat[:, :, 0:E].bitcast(F32), ALU.subtract)],
            ]
            if L == 0:
                before_act = []
                after_act = [
                    [lambda: v.tensor_scalar(rt_score, rt_tmp, 0.5, 0.5, ALU.mult, ALU.add)],
                    [lambda: v.tensor_tensor(rt_score, rt_score, router_bias[:].unsqueeze(1).to_broadcast([P, NT, E]),
                                             ALU.add)],
                    [lambda: v.tensor_reduce(rt_group[:, :, 0:8],
                                             rt_score.rearrange("p q (g e) -> p q g e", g=8), AX.X, ALU.max)],
                    each(lambda q: v.max(rt_top[:, q, :], rt_group[:, q, 0:8])),
                    [keep_keys(rt_gkeys, 4)],
                    each(lambda q: v.match_replace(rt_gmark[:, q, :], rt_gkeys[:, q, :],
                                                   rt_group[:, q, 0:12], TAKEN)),
                    [lambda: v.tensor_scalar(rt_gsel, rt_gmark[:, :, 0:8], TAKEN, None, ALU.is_equal)],
                    [lambda: v.tensor_tensor(rt_masked[:, :, 0:E].rearrange("p q (g e) -> p q g e", g=8),
                                             rt_score.rearrange("p q (g e) -> p q g e", g=8),
                                             rt_gsel.unsqueeze(3).to_broadcast([P, NT, 8, 8]), ALU.mult)],
                ] + choose
            else:
                lg = misc_ps[:, 0:NT * E].rearrange("p (q e) -> p q e", q=NT)
                t1 = rt_score[:, :, 0:E]
                before_act = [
                    [lambda: v.tensor_reduce(rt_sum, lg, AX.X, ALU.max)],
                    [lambda: v.tensor_tensor(rt_group[:, :, 0:E], lg, rt_sum.unsqueeze(2).to_broadcast([P, NT, E]),
                                             ALU.subtract)],
                ]
                after_act = [
                    [lambda: v.tensor_scalar(t1, rt_tmp[:, :, 0:E], 1.0, None, ALU.add),
                     lambda: v.tensor_scalar(rt_tmp[:, :, 8:16], rt_tmp[:, :, 0:E], -1.0, 1.0, ALU.mult, ALU.add)],
                    [lambda: v.reciprocal(rt_score[:, :, 8:16], t1)],
                    [lambda: v.tensor_tensor(t1, rt_score[:, :, 8:16], rt_tmp[:, :, 8:16], ALU.mult)],
                    [lambda: v.tensor_reduce(rt_sum, t1, AX.X, ALU.add)],
                    [lambda: v.reciprocal(rt_rsum, rt_sum)],
                    [lambda: v.tensor_tensor(rt_masked[:, :, 0:E], t1, rt_rsum.unsqueeze(2).to_broadcast([P, NT, E]),
                                             ALU.mult)],
                ] + choose
            stages = before_act + after_act
            assert sum(len(x) for x in stages) == RT[L], sum(len(x) for x in stages)
            done = [0]
            for x in stages:
                done.append(done[-1] + len(x))

            def route(t, k):
                need(eng, m["rt"], t.times(RT[L], 1, done[k]))
                if k == 0 and L == 1:
                    need(eng, m["logits"], t.n(2))
                if k == len(before_act):
                    need(eng, m["squashed"], t.n(2))
                if k == len(stages) - 2:
                    need(eng, m["weights_turned"], t.n(1))
                if len(stages[k]) == NT and not isinstance(t.i, int):
                    v.tensor_copy(tick[:], one[:])
                for f in stages[k]:
                    f().then_inc(m["rt"], 1)

            def x_out(t):
                need(eng, m["y_turned"], t.n())
                rows = x_res[:, bass.ds(t.times(NT, -1), NT), :]
                v.scalar_tensor_tensor(rows, misc_ps[:].rearrange("p (q h) -> p q h", q=NT), tanh_g[:, 2 + L:3 + L],
                                       rows, ALU.mult, ALU.add).then_inc(m["x_new"], 1)

            def x_stats(t):
                if nxt_stats is None:
                    return
                need(eng, m["x_new"], t.n())
                for q in range(NT):
                    v.bn_stats(stats[:, bass.ds(t.times(NT, -1, q), 1), :].squeeze(1),
                               x_res[:, bass.ds(t.times(NT, -1, q), 1), :].squeeze(1))\
                     .then_inc(nxt_stats["stats_done"], 1)

            def hook(c, t):
                if t.has(-1):
                    if c == 2:
                        x_out(t)
                    if c == 3:
                        x_stats(t)
                if not t.has(1):
                    return
                if c == 4:
                    need(eng, m["x_turned"], t.n(1))
                    for q in range(NT):
                        n = t.times(NT, 1, q)
                        ins = v.tensor_scalar(xm_norm[:, q, :], x_res[:, bass.ds(n, 1), :].squeeze(1),
                                              mean[:, bass.ds(n, 1)], rstd[:, bass.ds(n, 1)],
                                              ALU.subtract, ALU.mult)
                    ins.then_inc(m["x_norm"], 1)
                if c == 7:
                    need(eng, m["x_hi"], t.n(2))
                    par = t.parity(1)
                    v.tensor_tensor(x_lo[par][:], misc_ps[:], x_hi[par][:].bitcast(F32), ALU.subtract)\
                     .then_inc(m["x_lo"], 1)
                if L == 1 and c == 10:
                    for k in range(len(before_act)):
                        route(t, k)
                if 12 <= c < C - 8:
                    todo = list(range(len(before_act), len(stages)))
                    slots = C - 8 - 12
                    per = -(-len(todo) // slots)
                    for k in todo[(c - 12) * per:(c - 11) * per]:
                        route(t, k)

            def gate_times_up(t, c):
                need(eng, m["silu"], t.times(C, plus=c + 1))
                need(eng, m["gate_up"], t.times(C, plus=c + 1))
                par = (t.off * C + c) % 2
                if c >= cfg["weighted"]:
                    dst = hidden[(t.off * C + c) % cfg["hbufs"]]
                    need(eng, m["down"], t.times(C, plus=c + 1 - cfg["hbufs"]))
                else:
                    dst = gated[par]
                    need(eng, m["hidden"], t.times(C, plus=c - 1))
                v.tensor_tensor(dst, up_ps[par], silu_g[par], ALU.mult).then_inc(m["gated"], 1)

            def times_weight(t, c):
                par = (t.off * C + c) % 2
                if c >= cfg["weighted"]:
                    eng.wait_ge(m["gated"], t.times(C, plus=c + 1))
                    v.tensor_copy(rt_rsum[:, 0:1], rt_rsum[:, 0:1]).then_inc(m["hidden"], 1)
                    return
                need(eng, m["gated"], t.times(C, plus=c + 1))
                n = c // cfg["per_ce"]
                need(eng, m["ce"], t.times(cfg["weighted"] // cfg["per_ce"], plus=n + 1))
                need(eng, m["down"], t.times(C, plus=c + 1 - cfg["hbufs"]))
                v.tensor_tensor(hidden[(t.off * C + c) % cfg["hbufs"]], weight_ps[n % 2][:], gated[par], ALU.mult)\
                 .then_inc(m["hidden"], 1)

            def slot(t, c):
                nxt = ahead(L, t, c, LOOK)
                if nxt:
                    gate_times_up(*nxt)
                nxt = ahead(L, t, c, LOOK - 1)
                if nxt:
                    times_weight(*nxt)
                if c >= 0:
                    hook(c, t)

            start = Step(0, -1, TILES)
            for c in range(C):
                hook(c, start)
            run_tiles(eng, L, slot)
            end = Step(0, TILES, TILES)
            x_out(end)
            x_stats(end)

        @block.vector
        def _(dve):
            for c in range(4):
                dve.wait_ge(x_in[c], 16)
                for n in range(16 * c, 16 * c + 16):
                    nc.vector.bn_stats(stats[:, n, :], x_res[:, n, :]).then_inc(sa[0]["stats_done"], 1)
            for L in range(2):
                attn_dve_setup(dve, L, sa[L])
                moe_dve_setup(dve, L, sm[L])
                attn_dve(dve, L, sa[L])
                moe_dve(dve, L, sm[L])


def rotary_constants():
    inv = (1.0 / np.float32(10000.0) ** (np.arange(0, HD, 2, dtype=np.float32) / np.float32(HD))).astype(np.float32)
    freq = (np.arange(S, dtype=np.float32)[:, None] * inv[None, :]).astype(np.float32)
    cos, sin = np.cos(freq).T, np.sin(freq).T
    c = np.tile(np.concatenate([cos, cos]), (HEADS, 1))
    s = np.tile(np.concatenate([-sin, sin]), (HEADS, 1))
    table = np.stack([c, s], axis=1)
    return np.ascontiguousarray(np.repeat(table[:, :, None, :], 2, axis=2).astype(np.float32))


def kernel(**inputs):
    import numpy as _np
    import concourse.bacc as _bacc
    from concourse import mybir as _mybir
    from concourse.bass_utils import run_bass_kernel_spmd as _run

    nc = _bacc.Bacc("TRN2", target_bir_lowering=False, num_devices=1)
    arrays, args = {}, {}
    for name in inputs:
        a = _np.ascontiguousarray(inputs[name])
        arrays[f"in_{name}_dram"] = a
        args[name] = nc.dram_tensor(f"in_{name}_dram", a.shape, _mybir.dt.from_np(a.dtype), kind="ExternalInput").ap()
    table = rotary_constants()
    arrays["rotary_dram"] = table
    rot = nc.dram_tensor("rotary_dram", table.shape, _mybir.dt.float32, kind="ExternalInput").ap()
    out = nc.dram_tensor("out_0_dram", (B, S, H), _mybir.dt.float32, kind="ExternalOutput").ap()
    build(nc, args, rot, out)
    r = _run(nc, [arrays], core_ids=[0])
    return r.results[0]["out_0_dram"]
```

```python
from contextlib import ExitStack

import numpy as np
import concourse.bass as bass
from concourse import mybir

F32 = mybir.dt.float32
F32R = mybir.dt.float32r
BF16 = mybir.dt.bfloat16
I32 = mybir.dt.int32
ACT = mybir.ActivationFunctionType
ALU = mybir.AluOpType
AX = mybir.AxisListType

P = 128
B, S, H = 128, 64, 128
HEADS, HD = 16, 8
HP = HEADS // 2
PAIRS = B * S // P
TILES = B * S // 512
NT = 4
EPS = 1e-5
MASKED = -1e30
TAKEN = 3e38
ABSENT = -1e30
LOOK = 3

LAYERS = (
    dict(rotary=True, experts=64, groups=True, topk=6, chunks=33, weighted=32, per_ce=1, hbufs=3,
         scale=1.0 / float(np.sqrt(HD))),
    dict(rotary=False, experts=8, groups=False, topk=2, chunks=32, weighted=32, per_ce=4, hbufs=4,
         scale=1.0 / float(np.sqrt(H))),
)
CHUNKS = 33

E1, TOP1 = 8, 2
TOKENS = B * S
BLOCKS = TOKENS * TOP1 // P + E1
NO_ROW = 1 << 23


def need(eng, sem, value):
    if isinstance(value, int) and value <= 0:
        return
    eng.wait_ge(sem, value)


class Step:

    def __init__(self, i, off, count):
        self.i, self.off, self.count = i, off, count

    def n(self, k=0):
        return self.i * 2 + (self.off + k)

    def times(self, m, k=0, plus=0):
        return self.i * (2 * m) + (m * (self.off + k) + plus)

    def parity(self, k=0):
        return (self.off + k) % 2

    def of_parity(self, m, k=0):
        return self.i * m + m * ((self.off + k) // 2 + 1)

    def has(self, k=0):
        return not isinstance(self.i, int) or 0 <= self.n(k) < self.count


def run_steps(eng, step, first, loop_from, loop_to, last, count):
    for p in range(first, loop_from):
        step(Step(0, p, count))
    with eng.Fori(loop_from // 2, (loop_to + 1) // 2) as i:
        for s in range(2):
            step(Step(i, s, count))
    for p in range(loop_to + 1, last + 1):
        step(Step(0, p, count))


def build(nc, A, rotary, out):
    x_dram = A["x"].rearrange("b s d -> (b s) d").rearrange("(n p) d -> p n d", p=P)
    o_dram = out.rearrange("b s d -> (b s) d").rearrange("(n p) d -> p n d", p=P)
    ctx_dram = A["ctx_1024"].rearrange("b s d -> (b s) d")
    keep0_dram = A["mask_BxS2_if1"]
    keep1_dram = A["mask_Bx1xSxS2_ik1"].rearrange("b u q k -> (b u q) k")

    stack = ExitStack()
    with stack:
        def sb(name, shape, dt=F32):
            return stack.enter_context(nc.sbuf_tensor(name, shape, dt))

        def sem(name):
            return stack.enter_context(nc.semaphore(name))

        x_res = sb("x_res", [P, PAIRS, H])
        stats = sb("stats", [P, PAIRS, 6])
        mean = sb("mean", [P, PAIRS])
        rstd = sb("rstd", [P, PAIRS])
        ln_tmp = sb("ln_tmp", [P, 3, PAIRS])
        ident = sb("ident", [P, P])
        head_mask = sb("head_mask", [P, HEADS])
        half_mask = sb("half_mask", [P, HP])
        spread = sb("spread", [P, 2, S], BF16)
        future = sb("future", [P, 2, S])
        cos_sin = sb("cos_sin", [P, 2, 2, S])
        gates = sb("gates", [P, 4])
        tanh_g = sb("tanh_g", [P, 4])
        gw_nat = sb("gw_nat", [64, H])
        wqk = sb("wqk", [P, 4, H])
        wv = sb("wv", [P, H])
        wo = sb("wo", [P, 2, 2, H])
        bias_col = sb("bias_col", [P, 4])
        one = sb("one", [1, 1])
        tick = sb("tick", [1, 1])
        bias_rot = sb("bias_rot", [P, 2, 2, S])
        bias_v = sb("bias_v", [P, H])
        bias_o = sb("bias_o", [P, H])
        gate_hi = sb("gate_hi", [P, CHUNKS, P], F32R)
        gate_lo = sb("gate_lo", [P, CHUNKS, P], F32R)
        up_hi = sb("up_hi", [P, CHUNKS, P], F32R)
        up_lo = sb("up_lo", [P, CHUNKS, P], F32R)
        down = sb("down", [P, CHUNKS, P])
        w_nat = down[:, 0:4, :]
        wo_nat = down[:, 4:6, :].rearrange("p h (c g d) -> p h c g d", c=2, g=HP)
        bias_row = down[0:1, 6:8, :]
        bias_perm = down[0:1, 8:12, :].rearrange("p (a q) h -> p a q h", a=2)
        stage = [sb(f"stage{i}", [P, 4, P]) for i in range(3)]
        router = sb("router", [P, E1])
        descend = sb("descend", [P, E1])
        number = sb("number", [P, BLOCKS])
        spare_row = sb("spare_row", [P, BLOCKS], I32)
        earlier = sb("earlier", [P, P], BF16)
        all_ones = sb("all_ones", [P, P], BF16)
        targets = sb("targets", [P, PAIRS, TOP1], I32)
        filler = sb("filler", [P, H + 1])
        block_expert = sb("block_expert", [1, BLOCKS], I32)
        slot_now = [sb(f"slot_now{i}", [P, TOP1], I32) for i in range(2)]
        target_now = [sb(f"target_now{i}", [P, 1], I32) for i in range(2)]
        select = sb("select", [P, 64 * 64], F32R)
        pick = sb("pick", [P, 64])
        router_hi = sb("router_hi", [P, 64], F32R)
        router_lo = sb("router_lo", [P, 64], F32R)
        router_bias = sb("router_bias", [P, 64])

        arena = sb("arena", [P, 10480])
        spot = [0]

        def area(*shape, parts=P):
            size = int(np.prod(shape))
            view = arena[0:parts, spot[0]:spot[0] + size]
            spot[0] += size
            if len(shape) == 2:
                view = view.rearrange("p (a b) -> p a b", a=shape[0])
            elif len(shape) == 3:
                view = view.rearrange("p (a b c) -> p a b c", a=shape[0], b=shape[1])
            elif len(shape) == 4:
                view = view.rearrange("p (a b c d) -> p a b c d", a=shape[0], b=shape[1], c=shape[2])
            return view

        q_halves = [area(2, 2, S) for _ in range(2)]
        k_blocks = [area(2, HP, S) for _ in range(2)]
        scores = [area(HP, 2, S) for _ in range(2)]
        probs_t = area(HP, P)
        x_norm = [area(H) for _ in range(2)]
        ctx_in = [area(H) for _ in range(2)]
        xc_t = [area(2, P) for _ in range(2)]
        k_rot = [area(P) for _ in range(2)]
        v_blocks = [area(HP, 2, 2 * HD + 1) for _ in range(2)]
        rot_terms = area(2, 2, P)
        rot_sum = area(2, P)
        row_max = [area(HEADS) for _ in range(2)]
        row_rsum = area(HEADS)
        heads_out = [area(2, HP, HD) for _ in range(2)]
        heads_t = area(P)
        assert spot[0] <= 10480, spot
        keep_in = [sb(f"keep_in{i}", [P, S], I32) for i in range(2)]
        masked = [sb(f"masked{i}", [P, 2, S], BF16) for i in range(2)]

        spot[0] = 0
        silu_g = [area(512) for _ in range(2)]
        gated = [area(512) for _ in range(2)]
        hidden = [area(512) for _ in range(4)]
        y_t = area(512)
        xm_norm = area(NT, H)
        rt_score = area(NT, 64)
        rt_tmp = area(NT, 64)
        rt_masked = area(NT, 66)
        rt_marked = area(NT, 66)
        rt_weight = area(NT, 64)
        rt_group = area(NT, 14)
        rt_gmark = area(NT, 12)
        rt_gsel = area(NT, 8)
        rt_top = area(NT, 8)
        rt_gkeys = area(NT, 8)
        rt_keys = area(NT, 8)
        rt_sum = area(NT)
        rt_rsum = area(NT)
        weight_cat = area(NT, P).bitcast(F32R)
        assert spot[0] <= 10480, spot
        weight_t = [sb(f"weight_t{i}", [P, 512], F32R) for i in range(2)]
        spot[0] = 10000
        slots = area(PAIRS, TOP1).bitcast(I32)
        share = area(TOP1, PAIRS)
        block_target = area(BLOCKS).bitcast(I32)
        spot[0] = 9750
        ticks = area(PAIRS + BLOCKS)
        assert spot[0] <= 10480, spot
        spot[0] = 0
        d_x = [area(NT, H) for _ in range(2)]
        d_xt = [area(NT, H) for _ in range(2)]
        prob, others, key, place, scan0, scan1 = [area(PAIRS, E1) for _ in range(6)]
        chosen = [area(PAIRS, E1) for _ in range(TOP1)]
        top = [area(PAIRS) for _ in range(TOP1)]
        best = area(PAIRS)
        total = area(PAIRS)
        held, held_end0, held_end1 = [area(E1) for _ in range(3)]
        table = area(BLOCKS, E1)
        table_e = area(BLOCKS)
        picked = area(PAIRS * E1 // 2).bitcast(BF16)
        assert spot[0] <= 9750, spot
        spot[0] = 0
        row_out = [area(TOP1, H + 1) for _ in range(2)]
        row_in = [area(H + 1) for _ in range(2)]
        b_silu = [area(512) for _ in range(2)]
        b_hidden = [area(512) for _ in range(2)]
        b_hidden_t = [area(512) for _ in range(2)]
        b_y = [area(H) for _ in range(2)]
        y_in = [area(TOP1, NT, H) for _ in range(2)]
        assert spot[0] <= 9750, spot
        x_hi = [sb(f"x_hi{i}", [P, 512], F32R) for i in range(2)]
        x_lo = [sb(f"x_lo{i}", [P, 512], F32R) for i in range(2)]

        ps_s = stack.enter_context(nc.psum_tensor("ps_s", [P, 1024], F32))
        ps_t = stack.enter_context(nc.psum_tensor("ps_t", [P, 1024], F32))
        ps = [stack.enter_context(nc.psum_tensor(f"ps_{n}", [P, 512], F32)) for n in "abcd"]
        ps_a, ps_b, ps_c, ps_d = ps
        gate_ps = [ps_s[:, 0:512], ps_s[:, 512:1024]]
        up_ps = [ps_t[:, 0:512], ps_t[:, 512:1024]]
        weight_ps = [ps_a, ps_b]
        y_ps, misc_ps = ps_c, ps_d
        setup_ps = [ps_s[:, 0:512], ps_s[:, 512:1024], ps_t[:, 0:512], ps_t[:, 512:1024]]

        var_done = sem("variance_done")
        std_done = sem("deviation_done")
        norm_link = sem("norm_step")
        fill_done = sem("rows_filled")
        consts = sem("consts_built")
        const_dma = sem("constants_loaded")
        x_in = [sem(f"x_loaded{c}") for c in range(4)]
        bias_link = sem("bias_rotated")
        out_done = sem("out_stored")
        tanh_done = sem("tanh_of_gates")
        names_attn = ["small_in", "w_turned", "wo_arranged", "bias_turned", "attn_ready",
                      "stats_done", "cleared",
                      "x_norm", "ctx0", "ctx1", "keep0", "keep1", "turned_in", "xc_t", "projected", "v_projected", "rot_terms",
                      "rot_sum", "q_halves", "k_rot", "k_blocks", "v_blocks", "masked", "qk", "row_max", "shifted", "exp",
                      "p_turned", "probs_t", "pv", "rsum", "heads_out", "heads_turned", "heads_t", "y", "x_mid",
                      "x_new"]
        names_moe = ["stage0", "stage1", "stage2", "w_turned", "w_hi", "w_lo", "w_down", "router_turned", "router_hi", "pick", "select", "router_in",
                     "sentinels", "stats_done",
                     "x_norm", "x_turned", "x_hi", "x_lo", "logits", "squashed", "rt", "weights_turned", "weight_t",
                     "gate_up", "ce", "silu", "gated", "hidden", "down", "y_kept", "y_turned", "x_new"]
        only_rotary = ("bias_turned", "rot_terms", "rot_sum")
        sa = [{n: sem(f"a{L}_{n}") for n in names_attn if L == 0 or n not in only_rotary} for L in range(2)]
        names_sparse = ["stage0", "stage1", "stage2", "w_turned", "w_hi", "w_lo", "w_down", "router_turned",
                        "router", "router_in", "stats_done",
                        "x_norm", "x_turned", "x_t", "logits", "exp", "rt", "prefix", "rows", "scattered0",
                        "scattered1", "block_in0", "block_in1", "b_turned", "x_hi", "x_lo", "gate_up", "silu",
                        "hidden", "h_turned", "h_t", "y", "y_kept", "y_out0", "y_out1", "y_in0", "y_in1", "mixed",
                        "x_new"]
        sm = [{n: sem(f"m{L}_{n}") for n in (names_moe, names_sparse)[L]} for L in range(2)]
        rows_dram = nc.dram_tensor("expert_rows", [BLOCKS * P, H + 1], F32).ap()
        y_dram = nc.dram_tensor("expert_results", [TOP1 * TOKENS + BLOCKS * P, H], F32).ap()

        block = stack.enter_context(nc.Block())

        def attn_loads(eng, L, s):
            W = {n: A[f"L{L}_xattn_{n}"] for n in ("Wq", "Wk", "Wv", "Wo")}
            if L == 1:
                eng.wait_ge(sm[0]["x_new"], TILES)
            for j, n in enumerate(("Wq", "Wk", "Wv", "Wo")):
                eng.dma_start(w_nat[:, j, :], W[n]).then_inc(s["small_in"], 16)
            bo = A[f"L{L}_xattn_bo"]
            eng.dma_start(bias_o[:], bo.partition_broadcast(P)).then_inc(s["small_in"], 16)
            if L == 0:
                eng.dma_start(bias_v[:], A["L0_xattn_bv"].partition_broadcast(P)).then_inc(s["small_in"], 16)
                for j, n in enumerate(("bq", "bk")):
                    eng.dma_start(bias_row[:, j, :], A[f"L0_xattn_{n}"].partition_broadcast(1))\
                       .then_inc(s["small_in"], 16)
                eng.dma_start(gates[:, 0:2], A["g_xattn"].partition_broadcast(P)).then_inc(s["small_in"], 16)
                eng.dma_start(gates[:, 2:4], A["g_ffn"].partition_broadcast(P)).then_inc(s["small_in"], 16)

        SMALL = (16 * 10, 16 * 5)

        def attn_stream(eng, L, s):
            def step(p):
                if not p.has():
                    return
                need(eng, s["turned_in"], p.n(-1))
                eng.dma_start(ctx_in[p.parity()], ctx_dram[bass.ds(p.times(P), P), :])\
                   .then_inc(s[f"ctx{p.parity()}"], 16)
                need(eng, s["masked"], p.times(2, -1))
                keep = s[f"keep{p.parity()}"]
                if L == 0:
                    for b in range(2):
                        eng.dma_start(keep_in[p.parity()][64 * b:64 * b + 64, :],
                                      keep0_dram[bass.ds(p.times(2, plus=b), 1), :].squeeze(0)
                                      .partition_broadcast(64)).then_inc(keep, 16)
                else:
                    eng.dma_start(keep_in[p.parity()][:], keep1_dram[bass.ds(p.times(P), P), :])\
                       .then_inc(keep, 16)
            run_steps(eng, step, 0, 4, 59, PAIRS - 1, PAIRS)

        def stage_jobs(L):
            jobs = []
            if L == 0:
                for kind, w, shared in (("gate", "eg_w", "sg_w"), ("up", "eu_w", "su_w"), ("down", "ed_w", "sd_w")):
                    full, sh = A[f"L0_ffn_{w}"], A[f"L0_ffn_{shared}"]
                    for j in range(8):
                        if kind == "down":
                            src = full[8 * j:8 * j + 8].rearrange("e h i -> h e i")
                        else:
                            src = full[8 * j:8 * j + 8].rearrange("(c e) i h -> (e i) c h", e=2)
                        jobs.append((src, 4, kind, 4 * j))
                    jobs.append((sh, 1, kind, 32))
            else:
                gup, dp = A["L1_ffn_gate_up_proj"], A["L1_ffn_down_proj"]
                for kind in ("gate", "up", "down"):
                    for e in range(8):
                        if kind == "down":
                            src = dp[e]
                        else:
                            at = 512 * (kind == "up")
                            src = gup[e, at:at + 512, :].rearrange("(c p) h -> p c h", p=P)
                        jobs.append((src, 4, kind, 4 * e))
            return jobs

        def moe_loads(eng, L, m):
            if L == 1:
                eng.wait_ge(sm[0]["x_new"], TILES)
            E = LAYERS[L]["experts"]
            eng.dma_start(gw_nat[0:E, :], A[f"L{L}_ffn_gate_w"]).then_inc(m["router_in"], 16)
            if L == 0:
                eng.dma_start(router_bias[:], A["L0_ffn_gate_bias"].partition_broadcast(P))\
                   .then_inc(m["router_in"], 16)
            for j, (src, n, kind, c) in enumerate(stage_jobs(L)):
                need(eng, m["w_turned"], j - 2)
                dst = stage[j % 3][:, 0:n, :]
                if kind == "down" and L == 0 and n == 4:
                    dst = dst.rearrange("p c (e i) -> p (c e) i", e=2)
                elif n == 1 or (kind == "down" and L == 1):
                    dst = dst.rearrange("p c h -> p (c h)")
                eng.dma_start(dst, src).then_inc(m[f"stage{j % 3}"], 16)

        def sparse_sync(eng, m):
            for par in range(2):
                eng.wait_ge(m[f"scattered{par}"], 16 * TOP1 * PAIRS // 2)

            def load_block(j):
                if not j.has():
                    return
                need(eng, m["x_lo"], j.n(-1))
                eng.dma_start(row_in[j.parity()], rows_dram[bass.ds(j.times(P), P), :])\
                   .then_inc(m[f"block_in{j.parity()}"], 16)
            run_steps(eng, load_block, 0, 2, BLOCKS - 3, BLOCKS - 1, BLOCKS)
            for par in range(2):
                eng.wait_ge(m[f"y_out{par}"], 16 * BLOCKS // 2)

            def finish(c):
                par = c.parity()
                if c.has():
                    need(eng, m["x_new"], c.n(-1))
                    for k in range(TOP1):
                        eng.dma_start(y_in[par][:, k], y_dram[bass.ds(c.times(4 * P, plus=k * TOKENS), 4 * P), :]
                                      .rearrange("(q p) d -> p q d", p=P)).then_inc(m[f"y_in{par}"], 16)
                if c.has(-2):
                    need(eng, m["x_new"], c.n(-1))
                    eng.dma_start(o_dram[:, bass.ds(c.times(NT, -2), NT), :],
                                  x_res[:, bass.ds(c.times(NT, -2), NT), :]).then_inc(out_done, 16)
            run_steps(eng, finish, 0, 2, TILES - 3, TILES + 1, TILES)
            eng.wait_ge(out_done, 16 * TILES)

        @block.sync
        def _(sp):
            sp.dma_start(cos_sin[:], rotary).then_inc(const_dma, 16)
            attn_loads(sp, 0, sa[0])
            for c in range(4):
                sp.dma_start(x_res[:, 16 * c:16 * c + 16, :], x_dram[:, 16 * c:16 * c + 16, :]).then_inc(x_in[c], 16)
            moe_loads(sp, 0, sm[0])
            attn_stream(sp, 0, sa[0])
            sp.dma_start(rows_dram.rearrange("(n p) d -> p n d", p=P),
                         filler[:].unsqueeze(1).to_broadcast([P, BLOCKS, H + 1])).then_inc(fill_done, 16)
            attn_loads(sp, 1, sa[1])
            moe_loads(sp, 1, sm[1])
            attn_stream(sp, 1, sa[1])
            sparse_sync(sp, sm[1])

        def attn_pool(eng, L, s):
            g = nc.gpsimd
            if L == 1:
                eng.wait_ge(sm[0]["x_new"], TILES)
            for i in range(2):
                g.memset(q_halves[i], 0.0).then_inc(s["cleared"], 1)
                g.memset(v_blocks[i], 0.0).then_inc(s["cleared"], 1)
                g.memset(masked[i][:], 0.0).then_inc(s["cleared"], 1)
            eng.wait_ge(s["cleared"], 6)
            for i in range(2):
                for b in range(2):
                    g.memset(v_blocks[i][64 * b:64 * b + 64, :, b, 2 * HD:2 * HD + 1], 1.0).then_inc(s["cleared"], 1)
            eng.wait_ge(s["cleared"], 10)
            eng.wait_ge(s["attn_ready"], 1)

            def step(p):
                if p.has(-2):
                    need(eng, s["x_mid"], p.n(-1))
                    need(eng, s["k_blocks"], p.times(2, 2) if p.has(1) else 2 * PAIRS)
                    row = x_res[:, bass.ds(p.n(-2), 1), :].squeeze(1)
                    g.tensor_tensor(row, row, bias_o[:], ALU.add).then_inc(s["x_new"], 1)
                if p.has(2):
                    par = p.parity()
                    if L == 0:
                        need(eng, s["rot_sum"], p.n(3))
                        need(eng, s["qk"], p.n(1))
                        need(eng, s["k_blocks"], p.times(2, 2))
                        g.tensor_tensor(k_rot[par], rot_sum[:, 1, :], bias_rot[:, 1].rearrange("p b s -> p (b s)"),
                                        ALU.add).then_inc(s["k_rot"], 1)
                        need(eng, s["k_rot"], p.n(3))
                        for half in range(2):
                            rows = slice(S * half, S * half + S)
                            g.tensor_tensor(q_halves[par][rows, :, half, :],
                                            rot_sum[rows, 0, :].rearrange("p (b s) -> p b s", b=2),
                                            bias_rot[rows, 0], ALU.add).then_inc(s["q_halves"], 1)
                        need(eng, s["q_halves"], p.times(2, 3))
                    need(eng, s["k_rot"], p.n(3))
                    need(eng, s["qk"], p.n(1))
                    need(eng, s["x_new"], p.n(-1))
                    for b in range(2):
                        g.tensor_tensor(k_blocks[par][:, b],
                                        k_rot[par][:, S * b:S * b + S].unsqueeze(1).to_broadcast([P, HP, S]),
                                        half_mask[:].unsqueeze(2).to_broadcast([P, HP, S]), ALU.mult)\
                         .then_inc(s["k_blocks"], 1)
            run_steps(eng, step, -2, 4, 59, PAIRS + 1, PAIRS)

        def moe_pool(eng, L, m):
            g = nc.gpsimd
            eng.wait_ge(sa[L]["x_new"], PAIRS)
            eng.wait_ge(sa[L]["heads_t"], PAIRS)
            k = LAYERS[L]["topk"]
            n = LAYERS[L]["experts"]
            g.memset(rt_masked, ABSENT).then_inc(m["sentinels"], 1)
            g.memset(rt_group, ABSENT).then_inc(m["sentinels"], 1)
            g.memset(rt_keys, ABSENT).then_inc(m["sentinels"], 1)
            g.memset(rt_gkeys, ABSENT).then_inc(m["sentinels"], 1)

        def sparse_pool(eng, m):
            eng.wait_ge(fill_done, 16)

            def scatter_rows(p):
                par = p.parity()
                need(eng, m["rows"], p.n(1))
                nc.gpsimd.tensor_tensor(ticks[0:1, bass.ds(p.n(), 1)], one[:], one[:], ALU.add)
                for k in range(TOP1):
                    eng.indirect_dma_start(rows_dram, bass.IndirectOffsetOnAxis(ap=slot_now[par][:, k:k + 1], axis=0),
                                           row_out[par][:, k, :], None).then_inc(m[f"scattered{par}"], 16)
            run_steps(eng, scatter_rows, 0, 2, PAIRS - 3, PAIRS - 1, PAIRS)

            def scatter_results(j):
                par = j.parity()
                need(eng, m["y_kept"], j.n(1))
                nc.gpsimd.tensor_tensor(ticks[0:1, bass.ds(j.n(PAIRS), 1)], one[:], one[:], ALU.add)
                eng.indirect_dma_start(y_dram, bass.IndirectOffsetOnAxis(ap=target_now[par][:, 0:1], axis=0),
                                       b_y[par], None).then_inc(m[f"y_out{par}"], 16)
            run_steps(eng, scatter_results, 0, 2, BLOCKS - 3, BLOCKS - 1, BLOCKS)

        CONSTS = 24
        RT_PICKED, RT_DONE = 17, 57

        @block.gpsimd
        def _(pool):
            g = nc.gpsimd
            g.memset(ident[:], 0.0).then_inc(consts, 1)
            g.memset(head_mask[:], 1.0).then_inc(consts, 1)
            g.memset(spread[:], 0.0).then_inc(consts, 1)
            g.memset(future[:], 1.0).then_inc(consts, 1)
            g.memset(one[:], 1.0).then_inc(consts, 1)
            g.memset(wo[:], 0.0).then_inc(consts, 1)
            g.memset(earlier[:], 1.0).then_inc(consts, 1)
            g.memset(all_ones[:], 1.0).then_inc(consts, 1)
            g.memset(filler[:], 0.0).then_inc(consts, 1)
            count_up = arena[:, 0:BLOCKS].bitcast(I32)
            g.iota(count_up, [[1, BLOCKS]], channel_multiplier=0).then_inc(consts, 1)
            g.iota(spare_row[:], [[P, BLOCKS]], base=TOP1 * TOKENS, channel_multiplier=1).then_inc(consts, 1)
            for k in range(TOP1):
                g.iota(targets[:, :, k], [[P, PAIRS]], base=k * TOKENS, channel_multiplier=1).then_inc(consts, 1)
            pool.wait_ge(consts, 13)
            g.tensor_copy(number[:], count_up).then_inc(consts, 1)
            g.iota(filler[:, H:H + 1].bitcast(I32), [[1, 1]], base=NO_ROW, channel_multiplier=0)\
             .then_inc(consts, 1)
            g.affine_select(out=earlier[:], in_=earlier[:], compare_op=ALU.is_ge, fill=0.0, base=-1,
                            pattern=[[1, P]], channel_multiplier=-1).then_inc(consts, 1)
            g.affine_select(out=ident[:], in_=ident[:], compare_op=ALU.not_equal, fill=1.0, base=0,
                            pattern=[[-1, P]], channel_multiplier=1).then_inc(consts, 1)
            g.affine_select(out=head_mask[:], in_=head_mask[:], compare_op=ALU.is_ge, fill=0.0, base=0,
                            pattern=[[-HD, HEADS]], channel_multiplier=1).then_inc(consts, 1)
            g.affine_select(out=spread[:], in_=spread[:], compare_op=ALU.not_equal, fill=MASKED, base=0,
                            pattern=[[0, 2], [-1, S]], channel_multiplier=1).then_inc(consts, 1)
            g.affine_select(out=future[:], in_=future[:], compare_op=ALU.is_ge, fill=0.0, base=-1,
                            pattern=[[S, 2], [1, S]], channel_multiplier=-1).then_inc(consts, 1)
            pool.wait_ge(consts, 20)
            g.tensor_scalar(descend[:], number[:, 0:E1], -1.0, float(E1), ALU.mult, ALU.add).then_inc(consts, 1)
            g.affine_select(out=head_mask[:], in_=head_mask[:], compare_op=ALU.is_ge, fill=0.0, base=HD - 1,
                            pattern=[[HD, HEADS]], channel_multiplier=-1).then_inc(consts, 1)
            g.affine_select(out=spread[:], in_=spread[:], compare_op=ALU.not_equal, fill=MASKED, base=-S,
                            pattern=[[0, 2], [-1, S]], channel_multiplier=1).then_inc(consts, 1)
            pool.wait_ge(consts, CONSTS - 1)
            g.tensor_tensor(half_mask[:], head_mask[:, 0:HP], head_mask[:, HP:HEADS], ALU.add).then_inc(consts, 1)
            pool.wait_ge(consts, CONSTS)
            attn_pool(pool, 0, sa[0])
            moe_pool(pool, 0, sm[0])
            attn_pool(pool, 1, sa[1])
            sparse_pool(pool, sm[1])

        RT = (30, 24)

        def attn_pe_setup(eng, L, s):
            t = nc.tensor
            if L == 0:
                eng.wait_ge(consts, CONSTS)
            else:
                eng.wait_ge(sm[0]["x_new"], TILES)
            eng.wait_ge(s["small_in"], SMALL[L])
            for j in range(3):
                mm = t.transpose(ps_a[:, P * j:P * j + P], w_nat[:, j, :], ident[:])
            mm.then_inc(s["w_turned"], 1)
            eng.wait_ge(s["wo_arranged"], 2)
            for j in range(2):
                mm = t.transpose(ps_b[:, P * j:P * j + P], wo_nat[:, j].rearrange("p c g d -> p (c g d)"), ident[:])
            mm.then_inc(s["w_turned"], 1)
            if L == 0:
                eng.wait_ge(s["bias_turned"], 4)
                for j in range(4):
                    mm = t.matmul(ps_c[:, j:j + 1], bias_perm[0:1, j // 2, j % 2, :], one[0:1, 0:1],
                                  start=True, stop=True)
                mm.then_inc(s["w_turned"], 1)

        def attn_pe(eng, L, s):
            t = nc.tensor
            eng.wait_ge(s["attn_ready"], 1)
            eng.wait_ge(s["cleared"], 10)

            def step(p):
                par = p.parity()
                if p.has():
                    need(eng, s["q_halves"], p.times(2, 1))
                    need(eng, s["k_blocks"], p.times(2, 1))
                    need(eng, s["masked"], p.times(2, 1))
                    need(eng, s["shifted"], p.n())
                    for b in range(2):
                        t.matmul(ps_s[:, 512 * b:512 * b + 512], spread[:].rearrange("p a s -> p (a s)"),
                                 masked[par][:, b, :].unsqueeze(1).to_broadcast([P, HP, S]),
                                 start=True, stop=True, skip_group_check=True)
                        mm = t.matmul(ps_s[:, 512 * b:512 * b + 512], q_halves[par][:, b].rearrange("p h s -> p (h s)"),
                                      k_blocks[par][:, b].rearrange("p g k -> p (g k)"), start=False, stop=True,
                                      skip_group_check=True)
                    mm.then_inc(s["qk"], 1)
                if p.has(-2):
                    need(eng, s["heads_out"], p.times(2, -1))
                    need(eng, s["x_mid"], p.n(-2))
                    t.transpose(ps_d[:, 0:P], heads_out[par].rearrange("p b g d -> p (b g d)"), ident[:])\
                     .then_inc(s["heads_turned"], 1)
                if p.has(-1):
                    need(eng, s["exp"], p.n())
                    need(eng, s["probs_t"], p.n(-1))
                    q = p.parity(-1)
                    for hp in range(HP):
                        mm = t.transpose(ps_t[:, P * hp:P * hp + P],
                                         scores[q][:, hp].rearrange("p b k -> p (b k)"), ident[:])
                    mm.then_inc(s["p_turned"], 1)
                if p.has(-2):
                    need(eng, s["heads_t"], p.n(-1))
                    for b in range(2):
                        rows = slice(S * b, S * b + S)
                        for h in range(2):
                            mm = t.matmul(ps_d[rows, P:2 * P], heads_t[:, S * h:S * h + S], wo[:, b, h, :],
                                          start=(h == 0), stop=(h == 1))
                    mm.then_inc(s["y"], 1)
                if p.has(1):
                    need(eng, s["xc_t"], p.n(2))
                    need(eng, s["v_blocks"], p.times(2, 1))
                    t.matmul(ps_c[:, 0:P], xc_t[p.parity(1)][:, 1, :], wv[:], start=True, stop=True)\
                     .then_inc(s["v_projected"], 1)
                if p.has(3):
                    q = p.parity(3)
                    need(eng, s["x_norm"], p.n(4))
                    need(eng, s[f"ctx{q}"], p.of_parity(16, 3))
                    need(eng, s["heads_out"], p.times(2, -1))
                    need(eng, s["xc_t"], p.n(3))
                    t.transpose(ps_a[:, 0:P], x_norm[q], ident[:])
                    t.transpose(ps_a[:, P:2 * P], ctx_in[q], ident[:]).then_inc(s["turned_in"], 1)
                if p.has(2):
                    need(eng, s["xc_t"], p.n(3))
                    need(eng, s["rot_terms" if L == 0 else "k_rot"], p.n(2))
                    for j in range(4 if L == 0 else 2):
                        mm = t.matmul(ps_b[:, P * j:P * j + P], wqk[:, j, :], xc_t[par][:, j % 2, :],
                                      start=True, stop=True)
                    mm.then_inc(s["projected"], 1)
                if p.has(-1):
                    q = p.parity(-1)
                    need(eng, s["probs_t"], p.n())
                    need(eng, s["v_blocks"], p.times(2))
                    if p.has(3):
                        need(eng, s["xc_t"], p.n(4))
                    else:
                        need(eng, s["heads_out"], p.times(2, -1))
                    for hp in range(HP):
                        mm = t.matmul(ps_a[:, 34 * hp:34 * hp + 34], probs_t[:, hp, :],
                                      v_blocks[q][:, hp].rearrange("p b c -> p (b c)"), start=True, stop=True)
                    mm.then_inc(s["pv"], 1)
            run_steps(eng, step, -3, 4, 59, PAIRS + 1, PAIRS)

        def moe_pe_setup(eng, L, m):
            t = nc.tensor
            E = LAYERS[L]["experts"]
            eng.wait_ge(m["router_in"], 32 if L == 0 else 16)
            t.transpose(misc_ps[:, 0:E], gw_nat[0:E, :], ident[0:E, 0:E]).then_inc(m["router_turned"], 1)
            for j, (_, n, kind, c) in enumerate(stage_jobs(L)):
                eng.wait_ge(m[f"stage{j % 3}"], 16 * (j // 3 + 1))
                kept = [i for i in range(j) if i % 4 == j % 4]
                if kept:
                    jobs = stage_jobs(L)[:kept[-1] + 1]
                    need(eng, m["w_lo"], sum(k != "down" for _, _, k, _ in jobs))
                    need(eng, m["w_down"], sum(k == "down" for _, _, k, _ in jobs))
                for q in range(n):
                    mm = t.transpose(setup_ps[j % 4][:, P * q:P * q + P], stage[j % 3][:, q, :], ident[:])
                mm.then_inc(m["w_turned"], 1)

        def moe_chunks(L):
            return LAYERS[L]["chunks"]

        def run_tiles(eng, L, slot):
            C = moe_chunks(L)
            for c in range(-LOOK, 0):
                slot(Step(0, 0, TILES), c)
            for s in range(2):
                for c in range(C):
                    slot(Step(0, s, TILES), c)
            with eng.Fori(1, (TILES - 2) // 2) as i:
                for s in range(2):
                    for c in range(C):
                        slot(Step(i, s, TILES), c)
            for s in range(TILES - 2, TILES):
                for c in range(C):
                    slot(Step(0, s, TILES), c)

        def ahead(L, t, c, k):
            C = moe_chunks(L)
            c += k
            if c < 0:
                return None
            if c < C:
                return t, c
            if not t.has(1):
                return None
            return Step(t.i, t.off + 1, TILES), c - C

        def before(L, n):
            per = LAYERS[L]["per_ce"]
            return per * (n + 1)

        def moe_pe(eng, L, m):
            t_ = nc.tensor
            cfg = LAYERS[L]
            C, E, per = cfg["chunks"], cfg["experts"], cfg["per_ce"]
            rows = 2 * E

            def hook(name, t):
                if name == "turn_y" and (t.has(-1)):
                    need(eng, m["y_kept"], t.n())
                    need(eng, m["weight_t"], t.n(1))
                    for q in range(NT):
                        mm = t_.transpose(misc_ps[:, P * q:P * q + P], y_t[:, P * q:P * q + P], ident[:])
                    mm.then_inc(m["y_turned"], 1)
                if not t.has(1):
                    return
                par = t.parity(1)
                if name == "turn_x":
                    need(eng, m["x_norm"], t.n(2))
                    need(eng, m["x_new"], t.n())
                    need(eng, m["weight_t"], t.n(1))
                    for q in range(NT):
                        mm = t_.transpose(misc_ps[:, P * q:P * q + P], xm_norm[:, q, :], ident[:])
                    mm.then_inc(m["x_turned"], 1)
                if name == "logits":
                    need(eng, m["x_lo"], t.n(2))
                    for q in range(NT):
                        toks = slice(P * q, P * q + P)
                        for n, (a, b) in enumerate(((x_hi, router_hi), (x_lo, router_hi), (x_hi, router_lo))):
                            mm = t_.matmul(misc_ps[:, E * q:E * q + E], a[par][:, toks], b[:, 0:E],
                                           start=(n == 0), stop=(n == 2))
                    mm.then_inc(m["logits"], 1)
                if name == "turn_weights":
                    need(eng, m["rt"], t.times(RT[L], 2))
                    for q in range(NT):
                        mm = t_.transpose(misc_ps[0:rows, P * q:P * q + P], weight_cat[:, q, 0:rows].bitcast(F32),
                                          ident[:])
                    mm.then_inc(m["weights_turned"], 1)

            def gate_up(t, c):
                par = t.parity()
                g = t.times(C, plus=c)
                k = (t.off * C + c) % 2
                if c == 0:
                    need(eng, m["x_lo"], t.n(1))
                need(eng, m["silu"], t.times(C, plus=c - 1))
                need(eng, m["gated"], t.times(C, plus=c - 1))
                for dst, hi, lo in ((gate_ps[k], gate_hi, gate_lo), (up_ps[k], up_hi, up_lo)):
                    t_.matmul(dst, hi[:, c, :], x_hi[par][:], start=True, stop=False)
                    t_.matmul(dst, hi[:, c, :], x_lo[par][:], start=False, stop=False)
                    mm = t_.matmul(dst, lo[:, c, :], x_hi[par][:], start=False, stop=True)
                mm.then_inc(m["gate_up"], 1)
                if c < cfg["weighted"] and c % per == 0:
                    n = c // per
                    if c == 0:
                        need(eng, m["weight_t"], t.n(1))
                    N = cfg["weighted"] // per
                    if n >= 2:
                        need(eng, m["hidden"], t.times(C, plus=per * (n - 1)))
                    elif t.has(-1):
                        need(eng, m["hidden"], t.times(C, -1, per * (N + n - 1)))
                    if L == 0:
                        lhs = select[:, P * c:P * c + P]
                    else:
                        lhs = select[0:rows, P * n:P * n + P]
                    t_.matmul(weight_ps[n % 2][:], lhs, weight_t[par][0:rows, :], start=True, stop=True)\
                      .then_inc(m["ce"], 1)

            def down_product(t, c):
                need(eng, m["hidden"], t.times(C, plus=c + 1))
                if c == 0:
                    need(eng, m["y_kept"], t.n())
                k = (t.off * C + c) % cfg["hbufs"]
                t_.matmul(y_ps[:], down[:, c, :], hidden[k], start=(c == 0), stop=(c == C - 1))\
                  .then_inc(m["down"], 1)

            def slot(t, c):
                nxt = ahead(L, t, c, LOOK)
                if nxt:
                    gate_up(*nxt)
                if c >= 0:
                    down_product(t, c)
                for at, name in ((2, "turn_y"), (6, "turn_x"), (9, "logits"), (C - 8, "turn_weights")):
                    if c == at:
                        hook(name, t)

            eng.wait_ge(sa[L]["x_new"], PAIRS)
            eng.wait_ge(m["select"], 2)
            start = Step(0, -1, TILES)
            for name in ("turn_x", "logits", "turn_weights"):
                hook(name, start)
            jobs = stage_jobs(L)
            eng.wait_ge(m["w_lo"], sum(k != "down" for _, _, k, _ in jobs))
            eng.wait_ge(m["w_down"], sum(k == "down" for _, _, k, _ in jobs))
            run_tiles(eng, L, slot)
            need(eng, m["y_kept"], TILES)
            for q in range(NT):
                mm = t_.transpose(misc_ps[:, P * q:P * q + P], y_t[:, P * q:P * q + P], ident[:])
            mm.then_inc(m["y_turned"], 1)

        def sparse_pe(eng, m):
            t_ = nc.tensor

            def turn_and_route(t):
                par = t.parity()
                if t.has():
                    need(eng, m["x_norm"], t.n(1))
                    need(eng, m["x_t"], t.n(-1))
                    for q in range(NT):
                        mm = t_.transpose(gate_ps[par][:, P * q:P * q + P], d_x[par][:, q, :], ident[:])
                    mm.then_inc(m["x_turned"], 1)
                if t.has(-1):
                    need(eng, m["x_t"], t.n())
                    q0 = t.parity(-1)
                    for q in range(NT):
                        mm = t_.matmul(misc_ps[:, bass.ds(t.times(NT * E1, -1, E1 * q), E1)], d_xt[q0][:, q, :],
                                       router[:], start=True, stop=True)
                    mm.then_inc(m["logits"], 1)
            run_steps(eng, turn_and_route, 0, 2, TILES - 3, TILES, TILES)

            eng.wait_ge(m["rt"], RT_PICKED)
            t_.matmul(ps_a[:], earlier[:], picked, start=True, stop=True)
            t_.matmul(ps_b[:], all_ones[:], picked, start=True, stop=True).then_inc(m["prefix"], 1)

            eng.wait_ge(m["rt"], RT_DONE)
            eng.wait_ge(m["w_lo"], 16)
            eng.wait_ge(m["w_down"], 8)

            def turn_rows(j):
                if not j.has():
                    return
                par = j.parity()
                need(eng, m[f"block_in{par}"], j.of_parity(16))
                need(eng, m["x_lo"], j.n())
                t_.transpose(ps_c[:, 0:P], row_in[par][:, 0:H], ident[:]).then_inc(m["b_turned"], 1)

            def step(j):
                par = j.parity()
                turn_rows(Step(j.i, j.off + 1, BLOCKS))
                if j.has():
                    first = eng.value_load(block_expert[0:1, bass.ds(j.n(), 1)], min_val=0, max_val=4 * (E1 - 1))
                    need(eng, m["x_lo"], j.n(1))
                    need(eng, m["silu"], j.n(-1))
                    need(eng, m["hidden"], j.n(-1))
                    for dst, hi, lo in ((gate_ps[par], gate_hi, gate_lo), (up_ps[par], up_hi, up_lo)):
                        w_hi = hi[:, bass.ds(first, 4), :].rearrange("p c h -> p (c h)")
                        w_lo = lo[:, bass.ds(first, 4), :].rearrange("p c h -> p (c h)")
                        t_.matmul(dst, x_hi[par][:, 0:P], w_hi, start=True, stop=False)
                        t_.matmul(dst, x_lo[par][:, 0:P], w_hi, start=False, stop=False)
                        mm = t_.matmul(dst, x_hi[par][:, 0:P], w_lo, start=False, stop=True)
                    mm.then_inc(m["gate_up"], 1)
                if j.has(-1):
                    need(eng, m["hidden"], j.n())
                    need(eng, m["h_t"], j.n(-1))
                    for c in range(4):
                        mm = t_.transpose(ps_a[:, P * c:P * c + P], b_hidden[j.parity(-1)][:, P * c:P * c + P],
                                          ident[:])
                    mm.then_inc(m["h_turned"], 1)
                if j.has(-2):
                    first = eng.value_load(block_expert[0:1, bass.ds(j.n(-2), 1)], min_val=0, max_val=4 * (E1 - 1))
                    need(eng, m["h_t"], j.n(-1))
                    need(eng, m["y_kept"], j.n(-2))
                    for c in range(4):
                        mm = t_.matmul(ps_b[:, 0:P], b_hidden_t[par][:, P * c:P * c + P],
                                       down[:, bass.ds(first + c, 1), :].squeeze(1), start=(c == 0), stop=(c == 3))
                    mm.then_inc(m["y"], 1)
            turn_rows(Step(0, 0, BLOCKS))
            run_steps(eng, step, 0, 4, BLOCKS - 3, BLOCKS + 1, BLOCKS)

        @block.tensor
        def _(pe):
            for L in range(2):
                attn_pe_setup(pe, L, sa[L])
                moe_pe_setup(pe, L, sm[L])
                attn_pe(pe, L, sa[L])
                (moe_pe(pe, 0, sm[0]) if L == 0 else sparse_pe(pe, sm[1]))

        def std(eng, k):
            eng.wait_ge(var_done, k + 1)
            nc.scalar.activation(ln_tmp[:, 0, :], ln_tmp[:, 2, :], ACT.Sqrt).then_inc(std_done, 1)

        def attn_act(eng, L, s):
            a = nc.scalar
            std(eng, 2 * L)
            scale = LAYERS[L]["scale"]

            def step(p):
                par = p.parity()
                if p.has(-2):
                    need(eng, s["heads_turned"], p.n(-1))
                    need(eng, s["y"], p.n(-2))
                    a.copy(heads_t, ps_d[:, 0:P]).then_inc(s["heads_t"], 1)
                if p.has(-1):
                    need(eng, s["p_turned"], p.n())
                    need(eng, s["pv"], p.n(-1))
                    a.copy(probs_t.rearrange("p a b -> p (a b)"), ps_t[:]).then_inc(s["probs_t"], 1)
                if p.has(3):
                    need(eng, s["turned_in"], p.n(4))
                    need(eng, s["v_projected"], p.n(2))
                    a.copy(xc_t[p.parity(3)].rearrange("p a b -> p (a b)"), ps_a[:, 0:2 * P]).then_inc(s["xc_t"], 1)
                if L == 1 and p.has(2):
                    need(eng, s["projected"], p.n(3))
                    need(eng, s["qk"], p.n(1))
                    for half in range(2):
                        rows = slice(S * half, S * half + S)
                        a.copy(q_halves[par][rows, :, half, :], ps_b[rows, 0:P].rearrange("p (b s) -> p b s", b=2))\
                         .then_inc(s["q_halves"], 1)
                    need(eng, s["k_blocks"], p.times(2, 1))
                    a.copy(k_rot[par], ps_b[:, P:2 * P]).then_inc(s["k_rot"], 1)
                if p.has():
                    need(eng, s["shifted"], p.n(1))
                    flat = scores[par].rearrange("p g b k -> p (g b k)")
                    a.activation(flat, flat, ACT.Exp, scale=scale).then_inc(s["exp"], 1)
            run_steps(eng, step, -3, 4, 59, PAIRS + 1, PAIRS)

        def moe_act_setup(eng, L, m):
            a = nc.scalar
            E = LAYERS[L]["experts"]
            eng.wait_ge(m["router_turned"], 1)
            if L == 0:
                a.copy(router_hi[:, 0:E], misc_ps[:, 0:E]).then_inc(m["router_hi"], 1)
            else:
                a.copy(router[:], misc_ps[:, 0:E]).then_inc(m["router"], 1)
            for j, (_, n, kind, c) in enumerate(stage_jobs(L)):
                eng.wait_ge(m["w_turned"], j + 1)
                dst = {"gate": gate_hi, "up": up_hi, "down": down}[kind]
                ins = a.copy(dst[:, c:c + n, :].rearrange("p c h -> p (c h)"), setup_ps[j % 4][:, 0:P * n])
                ins.then_inc(m["w_down" if kind == "down" else "w_hi"], 1)

        def moe_act(eng, L, m):
            a = nc.scalar
            cfg = LAYERS[L]
            C, E = cfg["chunks"], cfg["experts"]

            def hook(name, t):
                if name == "keep_y" and t.has(-1):
                    need(eng, m["down"], t.times(C))
                    need(eng, m["y_turned"], t.n(-1))
                    a.copy(y_t, y_ps[:]).then_inc(m["y_kept"], 1)
                if not t.has(1):
                    return
                par = t.parity(1)
                if name == "x_hi":
                    need(eng, m["x_turned"], t.n(2))
                    need(eng, m["gate_up"], t.times(C))
                    a.copy(x_hi[par][:], misc_ps[:]).then_inc(m["x_hi"], 1)
                if name == "squash" and L == 0:
                    need(eng, m["logits"], t.n(2))
                    a.activation(rt_tmp.rearrange("p a b -> p (a b)"), misc_ps[:, 0:NT * E], ACT.Tanh, scale=0.5)\
                     .then_inc(m["squashed"], 1)
                if name == "squash" and L == 1:
                    need(eng, m["rt"], t.times(RT[L], 1, 2))
                    a.activation(rt_tmp[:, :, 0:E], rt_group[:, :, 0:E], ACT.Tanh, scale=-0.5)\
                     .then_inc(m["squashed"], 1)
                if name == "weight_t":
                    need(eng, m["weights_turned"], t.n(2))
                    need(eng, m["ce"], t.times(cfg["weighted"] // cfg["per_ce"]))
                    a.copy(weight_t[par][0:2 * E, :], misc_ps[0:2 * E, :]).then_inc(m["weight_t"], 1)

            def slot(t, c):
                if c == 0:
                    hook("keep_y", t)
                nxt = ahead(L, t, c, LOOK)
                if nxt:
                    u, k = nxt
                    need(eng, m["gate_up"], u.times(C, plus=k + 1))
                    need(eng, m["gated"], u.times(C, plus=k - 1))
                    par = (u.off * C + k) % 2
                    a.activation(silu_g[par], gate_ps[par], ACT.Silu).then_inc(m["silu"], 1)
                for at, name in ((6, "x_hi"), (11, "squash"), (C - 7, "weight_t")):
                    if c == at:
                        hook(name, t)

            std(eng, 1)
            start = Step(0, -1, TILES)
            for name in ("x_hi", "squash", "weight_t"):
                hook(name, start)
            run_tiles(eng, L, slot)
            need(eng, m["down"], TILES * C)
            need(eng, m["y_turned"], TILES - 1)
            a.copy(y_t, y_ps[:]).then_inc(m["y_kept"], 1)

        def sparse_act(eng, m):
            a = nc.scalar
            std(eng, 3)

            def keep_x(t):
                par = t.parity()
                need(eng, m["x_turned"], t.n(1))
                need(eng, m["logits"], t.n(-1))
                a.copy(d_xt[par].rearrange("p q h -> p (q h)"), gate_ps[par]).then_inc(m["x_t"], 1)
            run_steps(eng, keep_x, 0, 2, TILES - 3, TILES - 1, TILES)
            eng.wait_ge(m["rt"], 2)
            a.activation(prob, prob, ACT.Exp).then_inc(m["exp"], 1)

            def keep_rows(j):
                if j.has():
                    need(eng, m["b_turned"], j.n(1))
                    need(eng, m["gate_up"], j.n(-1))
                    a.copy(x_hi[j.parity()][:, 0:P], ps_c[:, 0:P]).then_inc(m["x_hi"], 1)

            def step(j):
                keep_rows(Step(j.i, j.off + 1, BLOCKS))
                if j.has():
                    need(eng, m["gate_up"], j.n(1))
                    need(eng, m["hidden"], j.n(-1))
                    a.activation(b_silu[j.parity()], gate_ps[j.parity()], ACT.Silu).then_inc(m["silu"], 1)
                if j.has(-1):
                    need(eng, m["h_turned"], j.n())
                    need(eng, m["y"], j.n(-3))
                    a.copy(b_hidden_t[j.parity(-1)], ps_a[:]).then_inc(m["h_t"], 1)
            keep_rows(Step(0, 0, BLOCKS))
            run_steps(eng, step, 0, 4, BLOCKS - 3, BLOCKS, BLOCKS)

        @block.scalar
        def _(act):
            for L in range(2):
                if L == 0:
                    act.wait_ge(sa[0]["small_in"], SMALL[0])
                    nc.scalar.activation(tanh_g[:], gates[:], ACT.Tanh).then_inc(tanh_done, 1)
                moe_act_setup(act, L, sm[L])
                attn_act(act, L, sa[L])
                (moe_act(act, 0, sm[0]) if L == 0 else sparse_act(act, sm[1]))

        def layer_norm_scales(eng, s, k):
            v = nc.vector
            eng.wait_ge(s["stats_done"], PAIRS)
            me, qe, mo, qo = stats[:, :, 1], stats[:, :, 2], stats[:, :, 4], stats[:, :, 5]
            v.tensor_tensor(ln_tmp[:, 0, :], me, mo, ALU.subtract).then_inc(norm_link, 1)
            v.tensor_tensor(ln_tmp[:, 1, :], qe, qo, ALU.add).then_inc(norm_link, 1)
            v.tensor_tensor(mean[:], me, mo, ALU.add).then_inc(norm_link, 1)
            eng.wait_ge(norm_link, 7 * k + 3)
            v.scalar_tensor_tensor(ln_tmp[:, 2, :], ln_tmp[:, 0, :], 0.25, ln_tmp[:, 0, :], ALU.mult, ALU.mult)\
             .then_inc(norm_link, 1)
            v.tensor_scalar(mean[:], mean[:], 0.5, None, ALU.mult).then_inc(norm_link, 1)
            v.tensor_scalar(ln_tmp[:, 1, :], ln_tmp[:, 1, :], 1.0 / H, EPS, ALU.mult, ALU.add)\
             .then_inc(norm_link, 1)
            eng.wait_ge(norm_link, 7 * k + 6)
            v.tensor_tensor(ln_tmp[:, 2, :], ln_tmp[:, 2, :], ln_tmp[:, 1, :], ALU.add).then_inc(var_done, 1)
            eng.wait_ge(std_done, k + 1)
            v.reciprocal(rstd[:], ln_tmp[:, 0, :]).then_inc(norm_link, 1)
            eng.wait_ge(norm_link, 7 * k + 7)

        def attn_dve_setup(eng, L, s):
            v = nc.vector
            eng.wait_ge(s["small_in"], SMALL[L])
            if L == 0:
                eng.wait_ge(tanh_done, 1)
            else:
                eng.wait_ge(sm[0]["x_new"], TILES)
            by_head = w_nat[:, 3, :].rearrange("p (h g d) -> p h g d", g=HP, h=2)
            for copy in range(2):
                v.tensor_copy(wo_nat[:, :, copy], by_head).then_inc(s["wo_arranged"], 1)
            eng.wait_ge(s["w_turned"], 1)
            if L == 0:
                for j in range(2):
                    src = ps_a[:, P * j:P * j + P].rearrange("p (h j r) -> p h r j", h=HEADS, r=2)
                    for half in range(2):
                        for ab in range(2):
                            dst = wqk[:, 2 * ab + j, :].rearrange("p (h r j) -> p h r j", h=HEADS, r=2)
                            v.tensor_copy(dst[:, :, half, :], src[:, :, (half + ab) % 2, :])
                rows = bias_row.rearrange("p q (h j r) -> p q h r j", h=HEADS, r=2)
                for ab in range(2):
                    for half in range(2):
                        dst = bias_perm[:, ab].rearrange("p q (h r j) -> p q h r j", h=HEADS, r=2)
                        for q in range(2):
                            ins = v.tensor_copy(dst[:, q, :, half, :], rows[:, q, :, (half + ab) % 2, :])
                        ins.then_inc(s["bias_turned"], 1)
            else:
                v.tensor_copy(wqk[:, 0:2, :].rearrange("p a b -> p (a b)"), ps_a[:, 0:2 * P])
            v.tensor_copy(wv[:], ps_a[:, 2 * P:3 * P])
            eng.wait_ge(s["w_turned"], 2)
            eng.wait_ge(consts, CONSTS)
            for b in range(2):
                rows = slice(S * b, S * b + S)
                v.tensor_scalar(wo[rows, b].rearrange("p a b -> p (a b)"), ps_b[rows, 0:2 * P],
                                tanh_g[rows, L:L + 1], None, ALU.mult)
            last = v.tensor_scalar(bias_o[:], bias_o[:], tanh_g[:, L:L + 1], None, ALU.mult)
            if L == 0:
                eng.wait_ge(s["w_turned"], 3)
                eng.wait_ge(const_dma, 16)
                v.tensor_copy(bias_col[:], ps_c[:, 0:4]).then_inc(bias_link, 1)
                eng.wait_ge(bias_link, 1)
                for q in range(2):
                    v.tensor_scalar(bias_rot[:, q].rearrange("p b s -> p (b s)"),
                                    cos_sin[:, 0].rearrange("p b s -> p (b s)"), bias_col[:, q:q + 1], None, ALU.mult)\
                     .then_inc(bias_link, 1)
                eng.wait_ge(bias_link, 3)
                for q in range(2):
                    flat = bias_rot[:, q].rearrange("p b s -> p (b s)")
                    last = v.scalar_tensor_tensor(flat, cos_sin[:, 1].rearrange("p b s -> p (b s)"),
                                                  bias_col[:, 2 + q:3 + q], flat, ALU.mult, ALU.add)
            last.then_inc(s["attn_ready"], 1)
            eng.wait_ge(s["attn_ready"], 1)

        def moe_dve_setup(eng, L, m):
            v = nc.vector
            E = LAYERS[L]["experts"]
            if L == 0:
                eng.wait_ge(consts, CONSTS)
            if L == 1:
                split_weights(eng, L, m)
                return
            v.tensor_tensor(pick[:, 0:E], ident[:, 0:E], ident[:, E:2 * E], ALU.add).then_inc(m["pick"], 1)
            eng.wait_ge(m["pick"], 1)
            eng.wait_ge(m["router_hi"], 1)
            width = 64 if L == 0 else P
            v.tensor_copy(select[:, 0:E * width].rearrange("p (e m) -> p e m", e=E),
                          pick[:, 0:E].unsqueeze(2).to_broadcast([P, E, width])).then_inc(m["select"], 1)
            v.tensor_tensor(router_lo[:, 0:E], misc_ps[:, 0:E], router_hi[:, 0:E].bitcast(F32), ALU.subtract)\
             .then_inc(m["select"], 1)
            split_weights(eng, L, m)

        def split_weights(eng, L, m):
            v = nc.vector
            n_lo = 0
            for j, (_, n, kind, c) in enumerate(stage_jobs(L)):
                if kind == "down":
                    continue
                n_lo += 1
                eng.wait_ge(m["w_hi"], n_lo)
                hi, lo = (gate_hi, gate_lo) if kind == "gate" else (up_hi, up_lo)
                v.tensor_tensor(lo[:, c:c + n, :].rearrange("p c h -> p (c h)"), setup_ps[j % 4][:, 0:P * n],
                                hi[:, c:c + n, :].bitcast(F32).rearrange("p c h -> p (c h)"), ALU.subtract)\
                 .then_inc(m["w_lo"], 1)

        def attn_dve(eng, L, s):
            v = nc.vector
            m = sm[L]
            layer_norm_scales(eng, s, 2 * L)
            eng.wait_ge(s["cleared"], 10)

            def step(p):
                par = p.parity()
                if p.has():
                    need(eng, s["qk"], p.n(1))
                    v.tensor_reduce(row_max[par], ps_s[:].rearrange("p (r k) -> p r k", k=S), AX.X, ALU.max)\
                     .then_inc(s["row_max"], 1)
                if p.has(4):
                    need(eng, s["turned_in"], p.n(3))
                    v.tensor_scalar(x_norm[par], x_res[:, bass.ds(p.n(4), 1), :].squeeze(1),
                                    mean[:, bass.ds(p.n(4), 1)], rstd[:, bass.ds(p.n(4), 1)],
                                    ALU.subtract, ALU.mult).then_inc(s["x_norm"], 1)
                if p.has():
                    need(eng, s["row_max"], p.n(1))
                    need(eng, s["p_turned"], p.n(-1))
                    v.tensor_tensor(scores[par].rearrange("p g b k -> p b g k"),
                                    ps_s[:].rearrange("p (b g k) -> p b g k", b=2, g=HP),
                                    row_max[par].rearrange("p (b g) -> p b g", b=2).unsqueeze(3)
                                    .to_broadcast([P, 2, HP, S]), ALU.subtract)\
                     .then_inc(s["shifted"], 1)
                if p.has(-2):
                    need(eng, s["y"], p.n(-1))
                    row = x_res[:, bass.ds(p.n(-2), 1), :].squeeze(1)
                    v.tensor_tensor(row, ps_d[:, P:2 * P], row, ALU.add).then_inc(s["x_mid"], 1)
                if p.has(-3):
                    need(eng, s["x_new"], p.n(-2))
                    v.bn_stats(stats[:, bass.ds(p.n(-3), 1), :].squeeze(1),
                               x_res[:, bass.ds(p.n(-3), 1), :].squeeze(1)).then_inc(m["stats_done"], 1)
                if p.has(1):
                    q = p.parity(1)
                    need(eng, s[f"keep{q}"], p.of_parity(32 if L == 0 else 16, 1))
                    need(eng, s["qk"], p.n())
                    for b in range(2):
                        rows = slice(S * b, S * b + S)
                        if L == 0:
                            ins = v.scalar_tensor_tensor(masked[q][rows, b, :], keep_in[q][rows, :], 0.0,
                                                         future[rows, b, :], ALU.is_equal, ALU.max)
                        else:
                            ins = v.tensor_scalar(masked[q][rows, b, :], keep_in[q][rows, :], 0.0, None, ALU.is_equal)
                        ins.then_inc(s["masked"], 1)
                if L == 0 and p.has(2):
                    need(eng, s["projected"], p.n(3))
                    need(eng, s["rot_sum"], p.n(2))
                    v.tensor_tensor(rot_terms, ps_b[:].rearrange("p (a q t) -> p a q t", a=2, q=2),
                                    cos_sin[:].rearrange("p a b s -> p a (b s)").unsqueeze(2)
                                    .to_broadcast([P, 2, 2, P]), ALU.mult).then_inc(s["rot_terms"], 1)
                if p.has(1):
                    q = p.parity(1)
                    need(eng, s["v_projected"], p.n(2))
                    need(eng, s["pv"], p.n())
                    for b in range(2):
                        rows = slice(S * b, S * b + S)
                        dst = v_blocks[q][rows, :, b, 0:2 * HD].rearrange("p g (h d) -> p g h d", h=2)
                        src = ps_c[rows, 0:P].rearrange("p (h g d) -> p g h d", g=HP, h=2)
                        if L == 0:
                            ins = v.tensor_tensor(dst, src, bias_v[rows, :]
                                                  .rearrange("p (h g d) -> p g h d", g=HP, h=2),
                                                  ALU.add)
                        else:
                            ins = v.tensor_copy(dst, src)
                        ins.then_inc(s["v_blocks"], 1)
                if L == 0 and p.has(2):
                    need(eng, s["rot_terms"], p.n(3))
                    need(eng, s["q_halves"], p.times(2, 2))
                    v.tensor_tensor(rot_sum, rot_terms[:, 0], rot_terms[:, 1], ALU.add)\
                     .then_inc(s["rot_sum"], 1)
                if p.has(-1):
                    q = p.parity(-1)
                    need(eng, s["pv"], p.n())
                    need(eng, s["heads_out"], p.times(2, -1))
                    sums = ps_a[:, 0:34 * HP].rearrange("p (r c) -> p r c", c=2 * HD + 1)
                    v.reciprocal(row_rsum, sums[:, :, 2 * HD]).then_inc(s["rsum"], 1)
                    need(eng, s["rsum"], p.n())
                    need(eng, s["heads_turned"], p.n(-2))
                    for h in range(2):
                        rows = slice(S * h, S * h + S)
                        src = ps_a[rows, 0:34 * HP].rearrange("p (g b c) -> p g b c", g=HP, b=2)
                        v.tensor_tensor(heads_out[q][rows].rearrange("p b g d -> p g b d"),
                                        src[:, :, :, HD * h:HD * h + HD],
                                        row_rsum[rows].rearrange("p (g b) -> p g b", g=HP).unsqueeze(3)
                                        .to_broadcast([S, HP, 2, HD]), ALU.mult).then_inc(s["heads_out"], 1)
            run_steps(eng, step, -4, 4, 59, PAIRS + 2, PAIRS)

        def moe_dve(eng, L, m):
            v = nc.vector
            cfg = LAYERS[L]
            C, E, K = cfg["chunks"], cfg["experts"], cfg["topk"]
            nxt_stats = sa[1] if L == 0 else None
            layer_norm_scales(eng, m, 1)
            eng.wait_ge(m["sentinels"], 4)

            def each(f):
                return [lambda q=q: f(q) for q in range(NT)]

            def keep_keys(dst, n):
                return lambda: v.tensor_copy(dst[:, :, 0:n], rt_top[:, :, 0:n])

            choose = [
                each(lambda q: v.max(rt_top[:, q, :], (rt_masked if L == 0 else rt_group)[:, q, 0:E])),
                [keep_keys(rt_keys, K)],
                each(lambda q: v.match_replace(rt_marked[:, q, 0:E + 8 - K], rt_keys[:, q, :],
                                               (rt_masked if L == 0 else rt_group)[:, q, 0:E + 8 - K], TAKEN)),
                [lambda: v.scalar_tensor_tensor(rt_weight[:, :, 0:E], rt_marked[:, :, 0:E], TAKEN,
                                                rt_masked[:, :, 0:E], ALU.is_equal, ALU.mult)],
                [lambda: v.tensor_reduce(rt_sum, rt_weight[:, :, 0:E], AX.X, ALU.add)],
            ]
            if L == 0:
                choose.append([lambda: v.tensor_scalar(rt_sum, rt_sum, 1e-8, None, ALU.add)])
            choose += [
                [lambda: v.reciprocal(rt_rsum, rt_sum)],
                [lambda: v.tensor_tensor(rt_weight[:, :, 0:E], rt_weight[:, :, 0:E],
                                         rt_rsum.unsqueeze(2).to_broadcast([P, NT, E]), ALU.mult)],
                [lambda: v.tensor_copy(weight_cat[:, :, 0:E], rt_weight[:, :, 0:E])],
                [lambda: v.tensor_tensor(weight_cat[:, :, E:2 * E], rt_weight[:, :, 0:E],
                                         weight_cat[:, :, 0:E].bitcast(F32), ALU.subtract)],
            ]
            if L == 0:
                before_act = []
                after_act = [
                    [lambda: v.tensor_scalar(rt_score, rt_tmp, 0.5, 0.5, ALU.mult, ALU.add)],
                    [lambda: v.tensor_tensor(rt_score, rt_score, router_bias[:].unsqueeze(1).to_broadcast([P, NT, E]),
                                             ALU.add)],
                    [lambda: v.tensor_reduce(rt_group[:, :, 0:8],
                                             rt_score.rearrange("p q (g e) -> p q g e", g=8), AX.X, ALU.max)],
                    each(lambda q: v.max(rt_top[:, q, :], rt_group[:, q, 0:8])),
                    [keep_keys(rt_gkeys, 4)],
                    each(lambda q: v.match_replace(rt_gmark[:, q, :], rt_gkeys[:, q, :],
                                                   rt_group[:, q, 0:12], TAKEN)),
                    [lambda: v.tensor_scalar(rt_gsel, rt_gmark[:, :, 0:8], TAKEN, None, ALU.is_equal)],
                    [lambda: v.tensor_tensor(rt_masked[:, :, 0:E].rearrange("p q (g e) -> p q g e", g=8),
                                             rt_score.rearrange("p q (g e) -> p q g e", g=8),
                                             rt_gsel.unsqueeze(3).to_broadcast([P, NT, 8, 8]), ALU.mult)],
                ] + choose
            else:
                lg = misc_ps[:, 0:NT * E].rearrange("p (q e) -> p q e", q=NT)
                t1 = rt_score[:, :, 0:E]
                before_act = [
                    [lambda: v.tensor_reduce(rt_sum, lg, AX.X, ALU.max)],
                    [lambda: v.tensor_tensor(rt_group[:, :, 0:E], lg, rt_sum.unsqueeze(2).to_broadcast([P, NT, E]),
                                             ALU.subtract)],
                ]
                after_act = [
                    [lambda: v.tensor_scalar(t1, rt_tmp[:, :, 0:E], 1.0, None, ALU.add),
                     lambda: v.tensor_scalar(rt_tmp[:, :, 8:16], rt_tmp[:, :, 0:E], -1.0, 1.0, ALU.mult, ALU.add)],
                    [lambda: v.reciprocal(rt_score[:, :, 8:16], t1)],
                    [lambda: v.tensor_tensor(t1, rt_score[:, :, 8:16], rt_tmp[:, :, 8:16], ALU.mult)],
                    [lambda: v.tensor_reduce(rt_sum, t1, AX.X, ALU.add)],
                    [lambda: v.reciprocal(rt_rsum, rt_sum)],
                    [lambda: v.tensor_tensor(rt_masked[:, :, 0:E], t1, rt_rsum.unsqueeze(2).to_broadcast([P, NT, E]),
                                             ALU.mult)],
                ] + choose
            stages = before_act + after_act
            assert sum(len(x) for x in stages) == RT[L], sum(len(x) for x in stages)
            done = [0]
            for x in stages:
                done.append(done[-1] + len(x))

            def route(t, k):
                need(eng, m["rt"], t.times(RT[L], 1, done[k]))
                if k == 0 and L == 1:
                    need(eng, m["logits"], t.n(2))
                if k == len(before_act):
                    need(eng, m["squashed"], t.n(2))
                if k == len(stages) - 2:
                    need(eng, m["weights_turned"], t.n(1))
                if len(stages[k]) == NT and not isinstance(t.i, int):
                    v.tensor_copy(tick[:], one[:])
                for f in stages[k]:
                    f().then_inc(m["rt"], 1)

            def x_out(t):
                need(eng, m["y_turned"], t.n())
                rows = x_res[:, bass.ds(t.times(NT, -1), NT), :]
                v.scalar_tensor_tensor(rows, misc_ps[:].rearrange("p (q h) -> p q h", q=NT), tanh_g[:, 2 + L:3 + L],
                                       rows, ALU.mult, ALU.add).then_inc(m["x_new"], 1)

            def x_stats(t):
                if nxt_stats is None:
                    return
                need(eng, m["x_new"], t.n())
                for q in range(NT):
                    v.bn_stats(stats[:, bass.ds(t.times(NT, -1, q), 1), :].squeeze(1),
                               x_res[:, bass.ds(t.times(NT, -1, q), 1), :].squeeze(1))\
                     .then_inc(nxt_stats["stats_done"], 1)

            def hook(c, t):
                if t.has(-1):
                    if c == 2:
                        x_out(t)
                    if c == 3:
                        x_stats(t)
                if not t.has(1):
                    return
                if c == 4:
                    need(eng, m["x_turned"], t.n(1))
                    for q in range(NT):
                        n = t.times(NT, 1, q)
                        ins = v.tensor_scalar(xm_norm[:, q, :], x_res[:, bass.ds(n, 1), :].squeeze(1),
                                              mean[:, bass.ds(n, 1)], rstd[:, bass.ds(n, 1)],
                                              ALU.subtract, ALU.mult)
                    ins.then_inc(m["x_norm"], 1)
                if c == 7:
                    need(eng, m["x_hi"], t.n(2))
                    par = t.parity(1)
                    v.tensor_tensor(x_lo[par][:], misc_ps[:], x_hi[par][:].bitcast(F32), ALU.subtract)\
                     .then_inc(m["x_lo"], 1)
                if L == 1 and c == 10:
                    for k in range(len(before_act)):
                        route(t, k)
                if 12 <= c < C - 8:
                    todo = list(range(len(before_act), len(stages)))
                    slots = C - 8 - 12
                    per = -(-len(todo) // slots)
                    for k in todo[(c - 12) * per:(c - 11) * per]:
                        route(t, k)

            def gate_times_up(t, c):
                need(eng, m["silu"], t.times(C, plus=c + 1))
                need(eng, m["gate_up"], t.times(C, plus=c + 1))
                par = (t.off * C + c) % 2
                if c >= cfg["weighted"]:
                    dst = hidden[(t.off * C + c) % cfg["hbufs"]]
                    need(eng, m["down"], t.times(C, plus=c + 1 - cfg["hbufs"]))
                else:
                    dst = gated[par]
                    need(eng, m["hidden"], t.times(C, plus=c - 1))
                v.tensor_tensor(dst, up_ps[par], silu_g[par], ALU.mult).then_inc(m["gated"], 1)

            def times_weight(t, c):
                par = (t.off * C + c) % 2
                if c >= cfg["weighted"]:
                    eng.wait_ge(m["gated"], t.times(C, plus=c + 1))
                    v.tensor_copy(rt_rsum[:, 0:1], rt_rsum[:, 0:1]).then_inc(m["hidden"], 1)
                    return
                need(eng, m["gated"], t.times(C, plus=c + 1))
                n = c // cfg["per_ce"]
                need(eng, m["ce"], t.times(cfg["weighted"] // cfg["per_ce"], plus=n + 1))
                need(eng, m["down"], t.times(C, plus=c + 1 - cfg["hbufs"]))
                v.tensor_tensor(hidden[(t.off * C + c) % cfg["hbufs"]], weight_ps[n % 2][:], gated[par], ALU.mult)\
                 .then_inc(m["hidden"], 1)

            def slot(t, c):
                nxt = ahead(L, t, c, LOOK)
                if nxt:
                    gate_times_up(*nxt)
                nxt = ahead(L, t, c, LOOK - 1)
                if nxt:
                    times_weight(*nxt)
                if c >= 0:
                    hook(c, t)

            start = Step(0, -1, TILES)
            for c in range(C):
                hook(c, start)
            run_tiles(eng, L, slot)
            end = Step(0, TILES, TILES)
            x_out(end)
            x_stats(end)

        def sparse_dve(eng, m):
            v = nc.vector
            layer_norm_scales(eng, m, 3)
            wide = [P, PAIRS, E1]

            def normalise(t):
                par = t.parity()
                need(eng, m["x_turned"], t.n(-1))
                for q in range(NT):
                    n = t.times(NT, plus=q)
                    ins = v.tensor_scalar(d_x[par][:, q, :], x_res[:, bass.ds(n, 1), :].squeeze(1),
                                          mean[:, bass.ds(n, 1)], rstd[:, bass.ds(n, 1)], ALU.subtract, ALU.mult)
                ins.then_inc(m["x_norm"], 1)
            run_steps(eng, normalise, 0, 2, TILES - 3, TILES - 1, TILES)

            done = [0]

            def count(ins):
                done[0] += 1
                return ins.then_inc(m["rt"], 1)

            def all_done():
                eng.wait_ge(m["rt"], done[0])

            def over_experts(per_token):
                return per_token.unsqueeze(2).to_broadcast(wide)

            def over_tokens(per_expert):
                return per_expert.unsqueeze(1).to_broadcast(wide)

            logits = misc_ps[:].rearrange("p (n e) -> p n e", e=E1)
            eng.wait_ge(m["logits"], TILES)
            count(v.tensor_reduce(best, logits, AX.X, ALU.max))
            all_done()
            count(v.tensor_tensor(prob, logits, over_experts(best), ALU.subtract))
            eng.wait_ge(m["exp"], 1)
            count(v.tensor_reduce(total, prob, AX.X, ALU.add))
            all_done()
            count(v.reciprocal(total, total))
            all_done()
            count(v.tensor_tensor(prob, prob, over_experts(total), ALU.mult))
            all_done()
            for k in range(TOP1):
                left = (prob, others)[k]
                count(v.tensor_reduce(top[k], left, AX.X, ALU.max))
                all_done()
                count(v.tensor_tensor(key, left, over_experts(top[k]), ALU.is_equal))
                all_done()
                count(v.tensor_tensor(key, key, over_tokens(descend[:]), ALU.mult))
                all_done()
                count(v.tensor_reduce(best, key, AX.X, ALU.max))
                all_done()
                count(v.tensor_tensor(chosen[k], over_tokens(descend[:]), over_experts(best), ALU.is_equal))
                all_done()
                if k == 0:
                    count(v.scalar_tensor_tensor(others, chosen[0], -2.0, prob, ALU.mult, ALU.add))
                    all_done()
            count(v.tensor_tensor(picked.rearrange("p (n e) -> p n e", e=E1), chosen[0], chosen[1], ALU.add))
            assert done[0] == RT_PICKED, done[0]
            count(v.tensor_tensor(total, top[0], top[1], ALU.add))
            all_done()
            count(v.reciprocal(total, total))
            all_done()
            for k in range(TOP1):
                count(v.scalar_tensor_tensor(share[:, k, :], top[k], tanh_g[:, 3:4], total, ALU.mult, ALU.mult))
            all_done()
            eng.wait_ge(m["prefix"], 1)
            count(v.tensor_copy(scan0, ps_b[:].rearrange("p (n e) -> p n e", e=E1)))
            all_done()
            src, dst = scan0, scan1
            for s in (1, 2, 4, 8, 16, 32):
                count(v.tensor_copy(dst[:, 0:s, :], src[:, 0:s, :]))
                count(v.tensor_tensor(dst[:, s:, :], src[:, s:, :], src[:, :PAIRS - s, :], ALU.add))
                all_done()
                src, dst = dst, src
            count(v.tensor_scalar(held_end1, src[:, PAIRS - 1, :], 1.0 / P, None, ALU.mult))
            all_done()
            by_block = table[:, 0:PAIRS, :].rearrange("p n e -> p (n e)").rearrange("p (e n) -> p e n", e=E1)
            count(v.tensor_tensor(by_block, held_end1.unsqueeze(2).to_broadcast([P, E1, PAIRS]),
                                  number[:, 0:PAIRS].unsqueeze(1).to_broadcast([P, E1, PAIRS]), ALU.is_gt))
            all_done()
            count(v.tensor_reduce(held, by_block, AX.X, ALU.add))
            all_done()
            a, b = held, held_end0
            for s in (1, 2, 4):
                count(v.tensor_copy(b[:, 0:s], a[:, 0:s]))
                count(v.tensor_tensor(b[:, s:], a[:, s:], a[:, :E1 - s], ALU.add))
                all_done()
                a, b = b, (held_end1 if a is held else a)
            ends, first = a, b
            count(v.tensor_tensor(table[0:1], ends[0:1].unsqueeze(1).to_broadcast([1, BLOCKS, E1]),
                                  number[0:1, :].unsqueeze(2).to_broadcast([1, BLOCKS, E1]), ALU.is_le))
            count(v.tensor_tensor(first, ends, held, ALU.subtract))
            all_done()
            count(v.tensor_reduce(table_e[0:1], table[0:1], AX.X, ALU.add))
            count(v.tensor_scalar(first, first, float(P), None, ALU.mult))
            count(v.tensor_tensor(place, src, ps_b[:].rearrange("p (n e) -> p n e", e=E1), ALU.subtract))
            all_done()
            count(v.tensor_scalar(block_expert[:], table_e[0:1], float(E1 - 1), 4.0, ALU.min, ALU.mult))
            count(v.tensor_tensor(place, place, ps_a[:].rearrange("p (n e) -> p n e", e=E1), ALU.add))
            all_done()
            count(v.tensor_tensor(place, place, over_tokens(first), ALU.add))
            all_done()
            for k in range(TOP1):
                count(v.tensor_tensor((key, others)[k], chosen[k], place, ALU.mult))
            all_done()
            for k in range(TOP1):
                count(v.tensor_reduce(top[k], (key, others)[k], AX.X, ALU.add))
            all_done()
            for k in range(TOP1):
                count(v.tensor_copy(slots[:, :, k], top[k]))
            all_done()
            assert done[0] == RT_DONE, done[0]

            def make_rows(p):
                par = p.parity()
                need(eng, m[f"scattered{par}"], p.of_parity(16 * TOP1, -2))
                v.tensor_scalar(row_out[par][:, :, 0:H], x_res[:, bass.ds(p.n(), 1), :].to_broadcast([P, TOP1, H]),
                                mean[:, bass.ds(p.n(), 1)], rstd[:, bass.ds(p.n(), 1)], ALU.subtract, ALU.mult)
                v.tensor_copy(row_out[par][:, :, H].bitcast(I32), targets[:, bass.ds(p.n(), 1), :].squeeze(1))
                v.tensor_copy(slot_now[par][:], slots[:, bass.ds(p.n(), 1), :].squeeze(1)).then_inc(m["rows"], 1)
            run_steps(eng, make_rows, 0, 2, PAIRS - 3, PAIRS - 1, PAIRS)

            def split_rows(j):
                if j.has():
                    par = j.parity()
                    need(eng, m["x_hi"], j.n(1))
                    v.tensor_tensor(block_target[:, bass.ds(j.n(), 1)], row_in[par][:, H:H + 1].bitcast(I32),
                                    spare_row[:, bass.ds(j.n(), 1)], ALU.min)
                    v.tensor_tensor(x_lo[par][:, 0:P], ps_c[:, 0:P], x_hi[par][:, 0:P].bitcast(F32), ALU.subtract)\
                     .then_inc(m["x_lo"], 1)

            def step(j):
                par = j.parity()
                split_rows(Step(j.i, j.off + 1, BLOCKS))
                if j.has(-3):
                    q = j.parity(-3)
                    need(eng, m["y"], j.n(-2))
                    need(eng, m[f"y_out{q}"], j.of_parity(16, -5))
                    v.tensor_copy(target_now[q][:], block_target[:, bass.ds(j.n(-3), 1)])
                    v.tensor_copy(b_y[q], ps_b[:, 0:P]).then_inc(m["y_kept"], 1)
                if j.has():
                    need(eng, m["silu"], j.n(1))
                    need(eng, m["h_turned"], j.n(-1))
                    v.tensor_tensor(b_hidden[par], up_ps[par], b_silu[par], ALU.mult).then_inc(m["hidden"], 1)
            split_rows(Step(0, 0, BLOCKS))
            run_steps(eng, step, 0, 6, BLOCKS - 3, BLOCKS + 2, BLOCKS)

            def mix(c):
                par = c.parity()
                need(eng, m[f"y_in{par}"], c.of_parity(16 * TOP1))
                for k in range(TOP1):
                    if k == 1:
                        need(eng, m["mixed"], c.n(1))
                    for q in range(NT):
                        n = c.times(NT, plus=q)
                        row = x_res[:, bass.ds(n, 1), :].squeeze(1)
                        ins = v.scalar_tensor_tensor(row, y_in[par][:, k, q, :],
                                                     share[:, k, :][:, bass.ds(n, 1)], row, ALU.mult, ALU.add)
                    ins.then_inc(m["mixed" if k == 0 else "x_new"], 1)
            run_steps(eng, mix, 0, 2, TILES - 3, TILES - 1, TILES)

        @block.vector
        def _(dve):
            for c in range(4):
                dve.wait_ge(x_in[c], 16)
                for n in range(16 * c, 16 * c + 16):
                    nc.vector.bn_stats(stats[:, n, :], x_res[:, n, :]).then_inc(sa[0]["stats_done"], 1)
            for L in range(2):
                attn_dve_setup(dve, L, sa[L])
                moe_dve_setup(dve, L, sm[L])
                attn_dve(dve, L, sa[L])
                (moe_dve(dve, 0, sm[0]) if L == 0 else sparse_dve(dve, sm[1]))


def rotary_constants():
    inv = (1.0 / np.float32(10000.0) ** (np.arange(0, HD, 2, dtype=np.float32) / np.float32(HD))).astype(np.float32)
    freq = (np.arange(S, dtype=np.float32)[:, None] * inv[None, :]).astype(np.float32)
    cos, sin = np.cos(freq).T, np.sin(freq).T
    c = np.tile(np.concatenate([cos, cos]), (HEADS, 1))
    s = np.tile(np.concatenate([-sin, sin]), (HEADS, 1))
    table = np.stack([c, s], axis=1)
    return np.ascontiguousarray(np.repeat(table[:, :, None, :], 2, axis=2).astype(np.float32))


def kernel(**inputs):
    import numpy as _np
    import concourse.bacc as _bacc
    from concourse import mybir as _mybir
    from concourse.bass_utils import run_bass_kernel_spmd as _run

    nc = _bacc.Bacc("TRN2", target_bir_lowering=False, num_devices=1)
    arrays, args = {}, {}
    for name in inputs:
        a = _np.ascontiguousarray(inputs[name])
        arrays[f"in_{name}_dram"] = a
        args[name] = nc.dram_tensor(f"in_{name}_dram", a.shape, _mybir.dt.from_np(a.dtype), kind="ExternalInput").ap()
    table = rotary_constants()
    arrays["rotary_dram"] = table
    rot = nc.dram_tensor("rotary_dram", table.shape, _mybir.dt.float32, kind="ExternalInput").ap()
    out = nc.dram_tensor("out_0_dram", (B, S, H), _mybir.dt.float32, kind="ExternalOutput").ap()
    build(nc, args, rot, out)
    r = _run(nc, [arrays], core_ids=[0])
    return r.results[0]["out_0_dram"]
```

```python
from contextlib import ExitStack

import numpy as np
import concourse.bass as bass
from concourse import mybir

F32 = mybir.dt.float32
F32R = mybir.dt.float32r
BF16 = mybir.dt.bfloat16
I32 = mybir.dt.int32
ACT = mybir.ActivationFunctionType
ALU = mybir.AluOpType
AX = mybir.AxisListType

P = 128
B, S, H = 128, 64, 128
HEADS, HD = 16, 8
HP = HEADS // 2
PAIRS = B * S // P
TILES = B * S // 512
NT = 4
EPS = 1e-5
MASKED = -1e30
TAKEN = 3e38
ABSENT = -1e30
LOOK = 3

SCALES = (1.0 / float(np.sqrt(HD)), 1.0 / float(np.sqrt(H)))
EXPERTS = (64, 8)
TOP0 = 6
WEIGHTED = 32
CHUNKS = WEIGHTED + 1
HBUFS = 3

E1, TOP1 = EXPERTS[1], 2
TOKENS = B * S
PARTS = 2
PART_PAIRS = PAIRS // PARTS
PART_BLOCKS = TOKENS * TOP1 // PARTS // P + E1
BLOCKS = PARTS * PART_BLOCKS
NO_ROW = 1 << 23


def need(eng, sem, value):
    if isinstance(value, int) and value <= 0:
        return
    eng.wait_ge(sem, value)


class Step:

    def __init__(self, i, off, count):
        self.i, self.off, self.count = i, off, count

    def n(self, k=0):
        return self.i * 2 + (self.off + k)

    def times(self, m, k=0, plus=0):
        return self.i * (2 * m) + (m * (self.off + k) + plus)

    def parity(self, k=0):
        return (self.off + k) % 2

    def of_parity(self, m, k=0):
        return self.i * m + m * ((self.off + k) // 2 + 1)

    def has(self, k=0):
        return not isinstance(self.i, int) or 0 <= self.n(k) < self.count


def run_steps(eng, step, first, loop_from, loop_to, last, count):
    for p in range(first, loop_from):
        step(Step(0, p, count))
    with eng.Fori(loop_from // 2, (loop_to + 1) // 2) as i:
        for s in range(2):
            step(Step(i, s, count))
    for p in range(loop_to + 1, last + 1):
        step(Step(0, p, count))


def build(nc, A, rotary, out):
    x_dram = A["x"].rearrange("b s d -> (b s) d").rearrange("(n p) d -> p n d", p=P)
    o_dram = out.rearrange("b s d -> (b s) d").rearrange("(n p) d -> p n d", p=P)
    ctx_dram = A["ctx_1024"].rearrange("b s d -> (b s) d")
    keep0_dram = A["mask_BxS2_if1"]
    keep1_dram = A["mask_Bx1xSxS2_ik1"].rearrange("b u q k -> (b u q) k")

    stack = ExitStack()
    with stack:
        def sb(name, shape, dt=F32):
            return stack.enter_context(nc.sbuf_tensor(name, shape, dt))

        def sem(name):
            return stack.enter_context(nc.semaphore(name))

        x_res = sb("x_res", [P, PAIRS, H])
        stats = sb("stats", [P, PAIRS, 6])
        mean = sb("mean", [P, PAIRS])
        rstd = sb("rstd", [P, PAIRS])
        ln_tmp = sb("ln_tmp", [P, 3, PAIRS])
        ident = sb("ident", [P, P])
        head_mask = sb("head_mask", [P, HEADS])
        half_mask = sb("half_mask", [P, HP])
        spread = sb("spread", [P, 2, S], BF16)
        future = sb("future", [P, 2, S])
        cos_sin = sb("cos_sin", [P, 2, 2, S])
        gates = sb("gates", [P, 4])
        tanh_g = sb("tanh_g", [P, 4])
        gw_nat = sb("gw_nat", [64, H])
        wqk = sb("wqk", [P, 4, H])
        wv = sb("wv", [P, H])
        wo = sb("wo", [P, 2, 2, H])
        bias_col = sb("bias_col", [P, 4])
        one = sb("one", [1, 1])
        tick = sb("tick", [1, 1])
        bias_rot = sb("bias_rot", [P, 2, 2, S])
        bias_v = sb("bias_v", [P, H])
        bias_o = sb("bias_o", [P, H])
        gate_hi = sb("gate_hi", [P, CHUNKS, P], F32R)
        gate_lo = sb("gate_lo", [P, CHUNKS, P], F32R)
        up_hi = sb("up_hi", [P, CHUNKS, P], F32R)
        up_lo = sb("up_lo", [P, CHUNKS, P], F32R)
        down = sb("down", [P, CHUNKS, P])
        w_nat = down[:, 0:4, :]
        wo_nat = down[:, 4:6, :].rearrange("p h (c g d) -> p h c g d", c=2, g=HP)
        bias_row = down[0:1, 6:8, :]
        bias_perm = down[0:1, 8:12, :].rearrange("p (a q) h -> p a q h", a=2)
        stage = [sb(f"stage{i}", [P, 4, P]) for i in range(3)]
        router = sb("router", [P, E1])
        descend = sb("descend", [P, E1])
        number = sb("number", [P, BLOCKS])
        spare_row = sb("spare_row", [P, BLOCKS], I32)
        earlier = sb("earlier", [P, P], BF16)
        all_ones = sb("all_ones", [P, P], BF16)
        targets = sb("targets", [P, PAIRS, TOP1], I32)
        filler = sb("filler", [P, H + 1])
        block_experts = sb("block_experts", [1, BLOCKS // 2 + 2], I32)
        slot_now = [[sb(f"slot_now{i}{n}", [P, TOP1], I32) for n in range(2)] for i in range(2)]
        target_now = [sb(f"target_now{i}", [P, 1], I32) for i in range(2)]
        select = sb("select", [P, 64 * 64], F32R)
        pick = sb("pick", [P, 64])
        router_hi = sb("router_hi", [P, 64], F32R)
        router_lo = sb("router_lo", [P, 64], F32R)
        router_bias = sb("router_bias", [P, 64])

        arena = sb("arena", [P, 10480])
        spot = [0]

        def area(*shape, parts=P):
            size = int(np.prod(shape))
            view = arena[0:parts, spot[0]:spot[0] + size]
            spot[0] += size
            if len(shape) == 2:
                view = view.rearrange("p (a b) -> p a b", a=shape[0])
            elif len(shape) == 3:
                view = view.rearrange("p (a b c) -> p a b c", a=shape[0], b=shape[1])
            elif len(shape) == 4:
                view = view.rearrange("p (a b c d) -> p a b c d", a=shape[0], b=shape[1], c=shape[2])
            return view

        q_halves = [area(2, 2, S) for _ in range(2)]
        k_blocks = [area(2, HP, S) for _ in range(2)]
        scores = [area(HP, 2, S) for _ in range(2)]
        probs_t = area(HP, P)
        x_norm = [area(H) for _ in range(2)]
        ctx_in = [area(H) for _ in range(2)]
        xc_t = [area(2, P) for _ in range(2)]
        k_rot = [area(P) for _ in range(2)]
        v_blocks = [area(HP, 2, 2 * HD + 1) for _ in range(2)]
        rot_terms = area(2, 2, P)
        rot_sum = area(2, P)
        row_max = [area(HEADS) for _ in range(2)]
        row_rsum = area(HEADS)
        heads_out = [area(2, HP, HD) for _ in range(2)]
        heads_t = area(P)
        stage += [scores[i][:, 4 * h:4 * h + 4].rearrange("p g b k -> p g (b k)") for i in range(2) for h in range(2)]
        stage.append(probs_t[:, 0:4])
        STAGES = len(stage)
        assert spot[0] <= 10480, spot
        keep_in = [sb(f"keep_in{i}", [P, S], I32) for i in range(2)]
        masked = [sb(f"masked{i}", [P, 2, S], BF16) for i in range(2)]

        spot[0] = 0
        silu_g = [area(512) for _ in range(2)]
        gated = [area(512) for _ in range(2)]
        hidden = [area(512) for _ in range(HBUFS)]
        y_t = area(512)
        xm_norm = area(NT, H)
        rt_score = area(NT, 64)
        rt_tmp = area(NT, 64)
        rt_masked = area(NT, 66)
        rt_marked = area(NT, 66)
        rt_weight = area(NT, 64)
        rt_group = area(NT, 14)
        rt_gmark = area(NT, 12)
        rt_gsel = area(NT, 8)
        rt_top = area(NT, 8)
        rt_gkeys = area(NT, 8)
        rt_keys = area(NT, 8)
        rt_sum = area(NT)
        rt_rsum = area(NT)
        weight_cat = area(NT, P).bitcast(F32R)
        assert spot[0] <= 10480, spot
        weight_t = [sb(f"weight_t{i}", [P, 512], F32R) for i in range(2)]
        spot[0] = 10000
        slots = area(PAIRS, TOP1).bitcast(I32)
        share = area(TOP1, PAIRS)
        block_target = area(BLOCKS).bitcast(I32)
        spot[0] = 9750
        ticks = area(PAIRS + BLOCKS + PART_PAIRS // 2)
        assert spot[0] <= 10480, spot
        spot[0] = 0
        d_x = [area(NT, H) for _ in range(2)]
        d_xt = [area(NT, H) for _ in range(2)]
        prob, others, key, place, scan0, scan1 = [area(PAIRS, E1) for _ in range(6)]
        chosen = [area(PAIRS, E1) for _ in range(TOP1)]
        top = [area(PAIRS) for _ in range(TOP1)]
        best = area(PAIRS)
        total = area(PAIRS)
        held, held_end0, held_end1 = [area(PARTS, E1) for _ in range(3)]
        table = area(BLOCKS, E1)
        table_e = area(BLOCKS)
        by_two = area(BLOCKS // 2 + 4, 2)
        packed = [area(BLOCKS // 2 + 2) for _ in range(2)]
        picked = area(PAIRS * E1 // 2).bitcast(BF16)
        assert spot[0] <= 9750, spot
        spot[0] = 0
        row_out = [[area(TOP1, H + 1) for _ in range(2)] for _ in range(2)]
        row_in = [area(H + 1) for _ in range(2)]
        b_silu = [area(512) for _ in range(2)]
        b_hidden = [area(512) for _ in range(2)]
        b_hidden_t = [area(512) for _ in range(2)]
        b_y = [area(H) for _ in range(2)]
        y_in = [area(TOP1, 2 * NT, H) for _ in range(2)]
        assert spot[0] <= 9750, spot
        x_hi = [sb(f"x_hi{i}", [P, 512], F32R) for i in range(2)]
        x_lo = [sb(f"x_lo{i}", [P, 512], F32R) for i in range(2)]

        ps_s = stack.enter_context(nc.psum_tensor("ps_s", [P, 1024], F32))
        ps_t = stack.enter_context(nc.psum_tensor("ps_t", [P, 1024], F32))
        ps = [stack.enter_context(nc.psum_tensor(f"ps_{n}", [P, 512], F32)) for n in "abcd"]
        ps_a, ps_b, ps_c, ps_d = ps
        gate_ps = [ps_s[:, 0:512], ps_s[:, 512:1024]]
        up_ps = [ps_t[:, 0:512], ps_t[:, 512:1024]]
        weight_ps = [ps_a, ps_b]
        y_ps, misc_ps = ps_c, ps_d
        setup_ps = [ps_s[:, 0:512], ps_s[:, 512:1024], ps_t[:, 0:512], ps_t[:, 512:1024]]

        var_done = sem("variance_done")
        std_done = sem("deviation_done")
        norm_link = sem("norm_step")
        fill_done = sem("rows_filled")
        consts = sem("consts_built")
        const_dma = sem("constants_loaded")
        x_in = [sem(f"x_loaded{c}") for c in range(4)]
        bias_link = sem("bias_rotated")
        out_done = sem("out_stored")
        staged = [sem(f"weights_staged{i}") for i in range(STAGES)]
        tanh_done = sem("tanh_of_gates")
        names_attn = ["small_in", "w_turned", "wo_arranged", "bias_turned", "attn_ready",
                      "stats_done", "cleared",
                      "x_norm", "ctx0", "ctx1", "keep0", "keep1", "turned_in", "xc_t", "projected", "v_projected", "rot_terms",
                      "rot_sum", "q_halves", "k_rot", "k_blocks", "v_blocks", "masked", "qk", "row_max", "shifted", "exp",
                      "p_turned", "probs_t", "pv", "rsum", "heads_out", "heads_turned", "heads_t", "y", "x_mid",
                      "x_new"]
        names_moe = ["w_turned", "w_hi", "w_lo", "w_down", "router_turned", "router_hi", "pick", "select", "router_in",
                     "sentinels", "stats_done",
                     "x_norm", "x_turned", "x_hi", "x_lo", "logits", "squashed", "rt", "weights_turned", "weight_t",
                     "gate_up", "ce", "silu", "gated", "hidden", "down", "y_kept", "y_turned", "x_new"]
        only_rotary = ("bias_turned", "rot_terms", "rot_sum")
        sa = [{n: sem(f"a{L}_{n}") for n in names_attn if L == 0 or n not in only_rotary} for L in range(2)]
        names_sparse = ["w_turned", "w_hi", "w_lo", "w_down", "router_turned",
                        "router", "router_in", "stats_done",
                        "x_norm", "x_turned", "x_t", "logits", "exp", "rt", "rows",  "scattered0",
                        "scattered1", "block_in0", "block_in1", "b_turned", "x_hi", "x_lo", "gate_up", "silu",
                        "hidden", "h_turned", "h_t", "y", "y_kept", "y_out0", "y_out1", "y_in0", "y_in1", "mixed",
                        "x_new"]
        sm = [{n: sem(f"m{L}_{n}") for n in (names_moe, names_sparse)[L]} for L in range(2)]
        rows_dram = nc.dram_tensor("expert_rows", [BLOCKS * P, H + 1], F32).ap()
        y_dram = nc.dram_tensor("expert_results", [TOP1 * TOKENS + BLOCKS * P, H], F32).ap()

        block = stack.enter_context(nc.Block())

        SENT_EARLY = 16 * TOP1 * PART_PAIRS // 2

        def attn_loads(eng, L, s):
            W = {n: A[f"L{L}_xattn_{n}"] for n in ("Wq", "Wk", "Wv", "Wo")}
            if L == 1:
                eng.wait_ge(sm[0]["x_new"], TILES)
            for j, n in enumerate(("Wq", "Wk", "Wv", "Wo")):
                eng.dma_start(w_nat[:, j, :], W[n]).then_inc(s["small_in"], 16)
            bo = A[f"L{L}_xattn_bo"]
            eng.dma_start(bias_o[:], bo.partition_broadcast(P)).then_inc(s["small_in"], 16)
            if L == 0:
                eng.dma_start(bias_v[:], A["L0_xattn_bv"].partition_broadcast(P)).then_inc(s["small_in"], 16)
                for j, n in enumerate(("bq", "bk")):
                    eng.dma_start(bias_row[:, j, :], A[f"L0_xattn_{n}"].partition_broadcast(1))\
                       .then_inc(s["small_in"], 16)
                eng.dma_start(gates[:, 0:2], A["g_xattn"].partition_broadcast(P)).then_inc(s["small_in"], 16)
                eng.dma_start(gates[:, 2:4], A["g_ffn"].partition_broadcast(P)).then_inc(s["small_in"], 16)

        SMALL = (16 * 10, 16 * 5)

        def attn_stream(eng, L, s):
            def step(p):
                if not p.has():
                    return
                need(eng, s["turned_in"], p.n(-1))
                eng.dma_start(ctx_in[p.parity()], ctx_dram[bass.ds(p.times(P), P), :])\
                   .then_inc(s[f"ctx{p.parity()}"], 16)
                need(eng, s["masked"], p.times(2, -1))
                keep = s[f"keep{p.parity()}"]
                if L == 0:
                    for b in range(2):
                        eng.dma_start(keep_in[p.parity()][64 * b:64 * b + 64, :],
                                      keep0_dram[bass.ds(p.times(2, plus=b), 1), :].squeeze(0)
                                      .partition_broadcast(64)).then_inc(keep, 16)
                else:
                    eng.dma_start(keep_in[p.parity()][:], keep1_dram[bass.ds(p.times(P), P), :])\
                       .then_inc(keep, 16)
            run_steps(eng, step, 0, 4, 59, PAIRS - 1, PAIRS)

        def stage_jobs(L):
            jobs = []
            if L == 0:
                for kind, w, shared in (("gate", "eg_w", "sg_w"), ("up", "eu_w", "su_w"), ("down", "ed_w", "sd_w")):
                    full, sh = A[f"L0_ffn_{w}"], A[f"L0_ffn_{shared}"]
                    for j in range(8):
                        if kind == "down":
                            src = full[8 * j:8 * j + 8].rearrange("e h i -> h e i")
                        else:
                            src = full[8 * j:8 * j + 8].rearrange("(c e) i h -> (e i) c h", e=2)
                        jobs.append((src, 4, kind, 4 * j))
                    jobs.append((sh, 1, kind, 32))
            else:
                gup, dp = A["L1_ffn_gate_up_proj"], A["L1_ffn_down_proj"]
                for kind in ("gate", "up", "down"):
                    for e in range(8):
                        if kind == "down":
                            src = dp[e]
                        else:
                            at = 512 * (kind == "up")
                            src = gup[e, at:at + 512, :].rearrange("(c p) h -> p c h", p=P)
                        jobs.append((src, 4, kind, 4 * e))
            return jobs

        def stage_of(L, j):
            j += L * len(stage_jobs(0))
            return j % STAGES, 16 * (j // STAGES + 1)

        def moe_loads(eng, L, m):
            if L == 1:
                eng.wait_ge(sm[0]["x_new"], TILES)
            E = EXPERTS[L]
            eng.dma_start(gw_nat[0:E, :], A[f"L{L}_ffn_gate_w"]).then_inc(m["router_in"], 16)
            if L == 0:
                eng.dma_start(router_bias[:], A["L0_ffn_gate_bias"].partition_broadcast(P))\
                   .then_inc(m["router_in"], 16)
            for j, (src, n, kind, c) in enumerate(stage_jobs(L)):
                need(eng, m["w_turned"], j + 1 - STAGES)
                buf, _ = stage_of(L, j)
                dst = stage[buf][:, 0:n, :]
                if kind == "down" and L == 0 and n == 4:
                    dst = dst.rearrange("p c (e i) -> p (c e) i", e=2)
                elif n == 1 or (kind == "down" and L == 1):
                    dst = dst.rearrange("p c h -> p (c h)")
                eng.dma_start(dst, src).then_inc(staged[buf], 16)

        def sparse_sync(eng, m):
            for par in range(2):
                eng.wait_ge(m[f"scattered{par}"], SENT_EARLY)

            def load_block(j):
                if not j.has():
                    return
                need(eng, m["x_lo"], j.n(-1))
                eng.dma_start(row_in[j.parity()], rows_dram[bass.ds(j.times(P), P), :])\
                   .then_inc(m[f"block_in{j.parity()}"], 16)
            run_steps(eng, load_block, 0, 2, PART_BLOCKS - 1, PART_BLOCKS - 1, BLOCKS)
            for par in range(2):
                eng.wait_ge(m[f"scattered{par}"], SENT_EARLY + 16 * PART_PAIRS)
            run_steps(eng, load_block, PART_BLOCKS, PART_BLOCKS, BLOCKS - 3, BLOCKS - 1, BLOCKS)
            for par in range(2):
                eng.wait_ge(m[f"y_out{par}"], 16 * BLOCKS // 2)

            def finish(c):
                par = c.parity()
                if c.has():
                    need(eng, m["x_new"], c.n(-1))
                    for k in range(TOP1):
                        eng.dma_start(y_in[par][:, k], y_dram[bass.ds(c.times(8 * P, plus=k * TOKENS), 8 * P), :]
                                      .rearrange("(q p) d -> p q d", p=P)).then_inc(m[f"y_in{par}"], 16)
                if c.has(-2):
                    need(eng, m["x_new"], c.n(-1))
                    eng.dma_start(o_dram[:, bass.ds(c.times(2 * NT, -2), 2 * NT), :],
                                  x_res[:, bass.ds(c.times(2 * NT, -2), 2 * NT), :]).then_inc(out_done, 16)
            run_steps(eng, finish, 0, 2, TILES // 2 - 3, TILES // 2 + 1, TILES // 2)
            eng.wait_ge(out_done, 16 * TILES // 2)

        @block.sync
        def _(sp):
            sp.dma_start(cos_sin[:], rotary).then_inc(const_dma, 16)
            attn_loads(sp, 0, sa[0])
            for c in range(4):
                sp.dma_start(x_res[:, 16 * c:16 * c + 16, :], x_dram[:, 16 * c:16 * c + 16, :]).then_inc(x_in[c], 16)
            moe_loads(sp, 0, sm[0])
            attn_stream(sp, 0, sa[0])
            sp.dma_start(rows_dram.rearrange("(n p) d -> p n d", p=P),
                         filler[:].unsqueeze(1).to_broadcast([P, BLOCKS, H + 1])).then_inc(fill_done, 16)
            attn_loads(sp, 1, sa[1])
            moe_loads(sp, 1, sm[1])
            attn_stream(sp, 1, sa[1])
            sparse_sync(sp, sm[1])

        def attn_pool(eng, L, s):
            g = nc.gpsimd
            if L == 1:
                eng.wait_ge(sm[0]["x_new"], TILES)
            for i in range(2):
                g.memset(q_halves[i], 0.0).then_inc(s["cleared"], 1)
                g.memset(v_blocks[i], 0.0).then_inc(s["cleared"], 1)
                g.memset(masked[i][:], 0.0).then_inc(s["cleared"], 1)
            eng.wait_ge(s["cleared"], 6)
            for i in range(2):
                for b in range(2):
                    g.memset(v_blocks[i][64 * b:64 * b + 64, :, b, 2 * HD:2 * HD + 1], 1.0).then_inc(s["cleared"], 1)
            eng.wait_ge(s["cleared"], 10)
            eng.wait_ge(s["attn_ready"], 1)

            def step(p):
                if p.has(-2):
                    need(eng, s["x_mid"], p.n(-1))
                    need(eng, s["k_blocks"], p.times(2, 2) if p.has(1) else 2 * PAIRS)
                    row = x_res[:, bass.ds(p.n(-2), 1), :].squeeze(1)
                    g.tensor_tensor(row, row, bias_o[:], ALU.add).then_inc(s["x_new"], 1)
                if p.has(2):
                    par = p.parity()
                    if L == 0:
                        need(eng, s["rot_sum"], p.n(3))
                        need(eng, s["qk"], p.n(1))
                        need(eng, s["k_blocks"], p.times(2, 2))
                        g.tensor_tensor(k_rot[par], rot_sum[:, 1, :], bias_rot[:, 1].rearrange("p b s -> p (b s)"),
                                        ALU.add).then_inc(s["k_rot"], 1)
                        need(eng, s["k_rot"], p.n(3))
                        for half in range(2):
                            rows = slice(S * half, S * half + S)
                            g.tensor_tensor(q_halves[par][rows, :, half, :],
                                            rot_sum[rows, 0, :].rearrange("p (b s) -> p b s", b=2),
                                            bias_rot[rows, 0], ALU.add).then_inc(s["q_halves"], 1)
                        need(eng, s["q_halves"], p.times(2, 3))
                    need(eng, s["k_rot"], p.n(3))
                    need(eng, s["qk"], p.n(1))
                    need(eng, s["x_new"], p.n(-1))
                    for b in range(2):
                        g.tensor_tensor(k_blocks[par][:, b],
                                        k_rot[par][:, S * b:S * b + S].unsqueeze(1).to_broadcast([P, HP, S]),
                                        half_mask[:].unsqueeze(2).to_broadcast([P, HP, S]), ALU.mult)\
                         .then_inc(s["k_blocks"], 1)
            run_steps(eng, step, -2, 4, 59, PAIRS + 1, PAIRS)

        def dense_pool(eng, m):
            g = nc.gpsimd
            eng.wait_ge(sa[0]["x_new"], PAIRS)
            eng.wait_ge(sa[0]["heads_t"], PAIRS)
            g.memset(rt_masked, ABSENT).then_inc(m["sentinels"], 1)
            g.memset(rt_group, ABSENT).then_inc(m["sentinels"], 1)
            g.memset(rt_keys, ABSENT).then_inc(m["sentinels"], 1)
            g.memset(rt_gkeys, ABSENT).then_inc(m["sentinels"], 1)

        def sparse_pool(eng, m):
            eng.wait_ge(fill_done, 16)

            def scatter_rows(p):
                par = p.parity()
                need(eng, m["rows"], p.times(2, 1))
                nc.gpsimd.tensor_tensor(ticks[0:1, bass.ds(p.n(PAIRS + BLOCKS), 1)], one[:], one[:], ALU.add)
                for n in range(2):
                    for k in range(TOP1):
                        eng.indirect_dma_start(rows_dram,
                                               bass.IndirectOffsetOnAxis(ap=slot_now[par][n][:, k:k + 1], axis=0),
                                               row_out[par][n][:, k, :], None).then_inc(m[f"scattered{par}"], 16)
            run_steps(eng, scatter_rows, 0, 2, PART_PAIRS // 2 - 3, PART_PAIRS // 2 - 1, PART_PAIRS // 2)

            def scatter_late(j):
                par = j.parity()
                need(eng, m["rows"], j.n(PART_PAIRS + 1))
                nc.gpsimd.tensor_tensor(ticks[0:1, bass.ds(j.n(), 1)], one[:], one[:], ALU.add)
                eng.indirect_dma_start(rows_dram, bass.IndirectOffsetOnAxis(ap=slot_now[par][0][:, 0:1], axis=0),
                                       row_out[par][0][:, 0, :], None).then_inc(m[f"scattered{par}"], 16)

            def scatter_results(j):
                if not j.has(-4):
                    return
                par = j.parity()
                need(eng, m["y_kept"], j.n(-3))
                nc.gpsimd.tensor_tensor(ticks[0:1, bass.ds(j.n(PAIRS - 4), 1)], one[:], one[:], ALU.add)
                eng.indirect_dma_start(y_dram, bass.IndirectOffsetOnAxis(ap=target_now[par][:, 0:1], axis=0),
                                       b_y[par], None).then_inc(m[f"y_out{par}"], 16)

            def both(j):
                scatter_late(j)
                scatter_results(j)
            late = 2 * PART_PAIRS
            run_steps(eng, both, 0, 6, late - 1, late - 1, BLOCKS)
            run_steps(eng, scatter_results, late, late, BLOCKS - 1, BLOCKS + 3, BLOCKS)

        CONSTS = 24
        RT_PICKED, RT_DONE = 17, 60

        @block.gpsimd
        def _(pool):
            g = nc.gpsimd
            g.memset(ident[:], 0.0).then_inc(consts, 1)
            g.memset(head_mask[:], 1.0).then_inc(consts, 1)
            g.memset(spread[:], 0.0).then_inc(consts, 1)
            g.memset(future[:], 1.0).then_inc(consts, 1)
            g.memset(one[:], 1.0).then_inc(consts, 1)
            g.memset(wo[:], 0.0).then_inc(consts, 1)
            g.memset(earlier[:], 1.0).then_inc(consts, 1)
            g.memset(all_ones[:], 1.0).then_inc(consts, 1)
            g.memset(filler[:], 0.0).then_inc(consts, 1)
            count_up = arena[:, 0:BLOCKS].bitcast(I32)
            g.iota(count_up, [[1, BLOCKS]], channel_multiplier=0).then_inc(consts, 1)
            g.iota(spare_row[:], [[P, BLOCKS]], base=TOP1 * TOKENS, channel_multiplier=1).then_inc(consts, 1)
            for k in range(TOP1):
                g.iota(targets[:, :, k], [[P, PAIRS]], base=k * TOKENS, channel_multiplier=1).then_inc(consts, 1)
            pool.wait_ge(consts, 13)
            g.tensor_copy(number[:], count_up).then_inc(consts, 1)
            g.iota(filler[:, H:H + 1].bitcast(I32), [[1, 1]], base=NO_ROW, channel_multiplier=0)\
             .then_inc(consts, 1)
            g.affine_select(out=earlier[:], in_=earlier[:], compare_op=ALU.is_ge, fill=0.0, base=-1,
                            pattern=[[1, P]], channel_multiplier=-1).then_inc(consts, 1)
            g.affine_select(out=ident[:], in_=ident[:], compare_op=ALU.not_equal, fill=1.0, base=0,
                            pattern=[[-1, P]], channel_multiplier=1).then_inc(consts, 1)
            g.affine_select(out=head_mask[:], in_=head_mask[:], compare_op=ALU.is_ge, fill=0.0, base=0,
                            pattern=[[-HD, HEADS]], channel_multiplier=1).then_inc(consts, 1)
            g.affine_select(out=spread[:], in_=spread[:], compare_op=ALU.not_equal, fill=MASKED, base=0,
                            pattern=[[0, 2], [-1, S]], channel_multiplier=1).then_inc(consts, 1)
            g.affine_select(out=future[:], in_=future[:], compare_op=ALU.is_ge, fill=0.0, base=-1,
                            pattern=[[S, 2], [1, S]], channel_multiplier=-1).then_inc(consts, 1)
            pool.wait_ge(consts, 20)
            g.tensor_scalar(descend[:], number[:, 0:E1], -1.0, float(E1), ALU.mult, ALU.add).then_inc(consts, 1)
            g.affine_select(out=head_mask[:], in_=head_mask[:], compare_op=ALU.is_ge, fill=0.0, base=HD - 1,
                            pattern=[[HD, HEADS]], channel_multiplier=-1).then_inc(consts, 1)
            g.affine_select(out=spread[:], in_=spread[:], compare_op=ALU.not_equal, fill=MASKED, base=-S,
                            pattern=[[0, 2], [-1, S]], channel_multiplier=1).then_inc(consts, 1)
            pool.wait_ge(consts, CONSTS - 1)
            g.tensor_tensor(half_mask[:], head_mask[:, 0:HP], head_mask[:, HP:HEADS], ALU.add).then_inc(consts, 1)
            pool.wait_ge(consts, CONSTS)
            attn_pool(pool, 0, sa[0])
            dense_pool(pool, sm[0])
            attn_pool(pool, 1, sa[1])
            sparse_pool(pool, sm[1])

        RT = 30

        def attn_pe_setup(eng, L, s):
            t = nc.tensor
            if L == 0:
                eng.wait_ge(consts, CONSTS)
            else:
                eng.wait_ge(sm[0]["x_new"], TILES)
            eng.wait_ge(s["small_in"], SMALL[L])
            for j in range(3):
                mm = t.transpose(ps_a[:, P * j:P * j + P], w_nat[:, j, :], ident[:])
            mm.then_inc(s["w_turned"], 1)
            eng.wait_ge(s["wo_arranged"], 2)
            for j in range(2):
                mm = t.transpose(ps_b[:, P * j:P * j + P], wo_nat[:, j].rearrange("p c g d -> p (c g d)"), ident[:])
            mm.then_inc(s["w_turned"], 1)
            if L == 0:
                eng.wait_ge(s["bias_turned"], 4)
                for j in range(4):
                    mm = t.matmul(ps_c[:, j:j + 1], bias_perm[0:1, j // 2, j % 2, :], one[0:1, 0:1],
                                  start=True, stop=True)
                mm.then_inc(s["w_turned"], 1)

        def attn_pe(eng, L, s):
            t = nc.tensor
            eng.wait_ge(s["attn_ready"], 1)
            eng.wait_ge(s["cleared"], 10)

            def step(p):
                par = p.parity()
                if p.has():
                    need(eng, s["q_halves"], p.times(2, 1))
                    need(eng, s["k_blocks"], p.times(2, 1))
                    need(eng, s["masked"], p.times(2, 1))
                    need(eng, s["shifted"], p.n())
                    for b in range(2):
                        t.matmul(ps_s[:, 512 * b:512 * b + 512], spread[:].rearrange("p a s -> p (a s)"),
                                 masked[par][:, b, :].unsqueeze(1).to_broadcast([P, HP, S]),
                                 start=True, stop=True, skip_group_check=True)
                        mm = t.matmul(ps_s[:, 512 * b:512 * b + 512], q_halves[par][:, b].rearrange("p h s -> p (h s)"),
                                      k_blocks[par][:, b].rearrange("p g k -> p (g k)"), start=False, stop=True,
                                      skip_group_check=True)
                    mm.then_inc(s["qk"], 1)
                if p.has(-2):
                    need(eng, s["heads_out"], p.times(2, -1))
                    need(eng, s["x_mid"], p.n(-2))
                    t.transpose(ps_d[:, 0:P], heads_out[par].rearrange("p b g d -> p (b g d)"), ident[:])\
                     .then_inc(s["heads_turned"], 1)
                if p.has(-1):
                    need(eng, s["exp"], p.n())
                    need(eng, s["probs_t"], p.n(-1))
                    q = p.parity(-1)
                    for hp in range(HP):
                        mm = t.transpose(ps_t[:, P * hp:P * hp + P],
                                         scores[q][:, hp].rearrange("p b k -> p (b k)"), ident[:])
                    mm.then_inc(s["p_turned"], 1)
                if p.has(-2):
                    need(eng, s["heads_t"], p.n(-1))
                    for b in range(2):
                        rows = slice(S * b, S * b + S)
                        for h in range(2):
                            mm = t.matmul(ps_d[rows, P:2 * P], heads_t[:, S * h:S * h + S], wo[:, b, h, :],
                                          start=(h == 0), stop=(h == 1))
                    mm.then_inc(s["y"], 1)
                if p.has(1):
                    need(eng, s["xc_t"], p.n(2))
                    need(eng, s["v_blocks"], p.times(2, 1))
                    t.matmul(ps_c[:, 0:P], xc_t[p.parity(1)][:, 1, :], wv[:], start=True, stop=True)\
                     .then_inc(s["v_projected"], 1)
                if p.has(3):
                    q = p.parity(3)
                    need(eng, s["x_norm"], p.n(4))
                    need(eng, s[f"ctx{q}"], p.of_parity(16, 3))
                    need(eng, s["heads_out"], p.times(2, -1))
                    need(eng, s["xc_t"], p.n(3))
                    t.transpose(ps_a[:, 0:P], x_norm[q], ident[:])
                    t.transpose(ps_a[:, P:2 * P], ctx_in[q], ident[:]).then_inc(s["turned_in"], 1)
                if p.has(2):
                    need(eng, s["xc_t"], p.n(3))
                    need(eng, s["rot_terms" if L == 0 else "k_rot"], p.n(2))
                    for j in range(4 if L == 0 else 2):
                        mm = t.matmul(ps_b[:, P * j:P * j + P], wqk[:, j, :], xc_t[par][:, j % 2, :],
                                      start=True, stop=True)
                    mm.then_inc(s["projected"], 1)
                if p.has(-1):
                    q = p.parity(-1)
                    need(eng, s["probs_t"], p.n())
                    need(eng, s["v_blocks"], p.times(2))
                    if p.has(3):
                        need(eng, s["xc_t"], p.n(4))
                    else:
                        need(eng, s["heads_out"], p.times(2, -1))
                    for hp in range(HP):
                        mm = t.matmul(ps_a[:, 34 * hp:34 * hp + 34], probs_t[:, hp, :],
                                      v_blocks[q][:, hp].rearrange("p b c -> p (b c)"), start=True, stop=True)
                    mm.then_inc(s["pv"], 1)
            run_steps(eng, step, -3, 4, 59, PAIRS + 1, PAIRS)

        def moe_pe_setup(eng, L, m):
            t = nc.tensor
            E = EXPERTS[L]
            eng.wait_ge(m["router_in"], 32 if L == 0 else 16)
            t.transpose(misc_ps[:, 0:E], gw_nat[0:E, :], ident[0:E, 0:E]).then_inc(m["router_turned"], 1)
            for j, (_, n, kind, c) in enumerate(stage_jobs(L)):
                buf, loaded = stage_of(L, j)
                eng.wait_ge(staged[buf], loaded)
                kept = [i for i in range(j) if i % 4 == j % 4]
                if kept:
                    jobs = stage_jobs(L)[:kept[-1] + 1]
                    need(eng, m["w_lo"], sum(k != "down" for _, _, k, _ in jobs))
                    need(eng, m["w_down"], sum(k == "down" for _, _, k, _ in jobs))
                for q in range(n):
                    mm = t.transpose(setup_ps[j % 4][:, P * q:P * q + P], stage[buf][:, q, :], ident[:])
                mm.then_inc(m["w_turned"], 1)

        def run_tiles(eng, slot):
            C = CHUNKS
            for c in range(-LOOK, 0):
                slot(Step(0, 0, TILES), c)
            for s in range(2):
                for c in range(C):
                    slot(Step(0, s, TILES), c)
            with eng.Fori(1, (TILES - 2) // 2) as i:
                for s in range(2):
                    for c in range(C):
                        slot(Step(i, s, TILES), c)
            for s in range(TILES - 2, TILES):
                for c in range(C):
                    slot(Step(0, s, TILES), c)

        def ahead(t, c, k):
            C = CHUNKS
            c += k
            if c < 0:
                return None
            if c < C:
                return t, c
            if not t.has(1):
                return None
            return Step(t.i, t.off + 1, TILES), c - C

        def dense_pe(eng, m):
            t_ = nc.tensor
            C, E = CHUNKS, EXPERTS[0]
            rows = 2 * E

            def hook(name, t):
                if name == "turn_y" and (t.has(-1)):
                    need(eng, m["y_kept"], t.n())
                    need(eng, m["weight_t"], t.n(1))
                    for q in range(NT):
                        mm = t_.transpose(misc_ps[:, P * q:P * q + P], y_t[:, P * q:P * q + P], ident[:])
                    mm.then_inc(m["y_turned"], 1)
                if not t.has(1):
                    return
                par = t.parity(1)
                if name == "turn_x":
                    need(eng, m["x_norm"], t.n(2))
                    need(eng, m["x_new"], t.n())
                    need(eng, m["weight_t"], t.n(1))
                    for q in range(NT):
                        mm = t_.transpose(misc_ps[:, P * q:P * q + P], xm_norm[:, q, :], ident[:])
                    mm.then_inc(m["x_turned"], 1)
                if name == "logits":
                    need(eng, m["x_lo"], t.n(2))
                    for q in range(NT):
                        toks = slice(P * q, P * q + P)
                        for n, (a, b) in enumerate(((x_hi, router_hi), (x_lo, router_hi), (x_hi, router_lo))):
                            mm = t_.matmul(misc_ps[:, E * q:E * q + E], a[par][:, toks], b[:, 0:E],
                                           start=(n == 0), stop=(n == 2))
                    mm.then_inc(m["logits"], 1)
                if name == "turn_weights":
                    need(eng, m["rt"], t.times(RT, 2))
                    for q in range(NT):
                        mm = t_.transpose(misc_ps[0:rows, P * q:P * q + P], weight_cat[:, q, 0:rows].bitcast(F32),
                                          ident[:])
                    mm.then_inc(m["weights_turned"], 1)

            def gate_up(t, c):
                par = t.parity()
                g = t.times(C, plus=c)
                k = (t.off * C + c) % 2
                if c == 0:
                    need(eng, m["x_lo"], t.n(1))
                need(eng, m["silu"], t.times(C, plus=c - 1))
                need(eng, m["gated"], t.times(C, plus=c - 1))
                for dst, hi, lo in ((gate_ps[k], gate_hi, gate_lo), (up_ps[k], up_hi, up_lo)):
                    t_.matmul(dst, hi[:, c, :], x_hi[par][:], start=True, stop=False)
                    t_.matmul(dst, hi[:, c, :], x_lo[par][:], start=False, stop=False)
                    mm = t_.matmul(dst, lo[:, c, :], x_hi[par][:], start=False, stop=True)
                mm.then_inc(m["gate_up"], 1)
                if c < WEIGHTED:
                    if c == 0:
                        need(eng, m["weight_t"], t.n(1))
                    if c >= 2:
                        need(eng, m["hidden"], t.times(C, plus=c - 1))
                    elif t.has(-1):
                        need(eng, m["hidden"], t.times(C, -1, WEIGHTED + c - 1))
                    t_.matmul(weight_ps[c % 2][:], select[:, P * c:P * c + P], weight_t[par][0:rows, :],
                              start=True, stop=True).then_inc(m["ce"], 1)

            def down_product(t, c):
                need(eng, m["hidden"], t.times(C, plus=c + 1))
                if c == 0:
                    need(eng, m["y_kept"], t.n())
                k = (t.off * C + c) % HBUFS
                t_.matmul(y_ps[:], down[:, c, :], hidden[k], start=(c == 0), stop=(c == C - 1))\
                  .then_inc(m["down"], 1)

            def slot(t, c):
                nxt = ahead(t, c, LOOK)
                if nxt:
                    gate_up(*nxt)
                if c >= 0:
                    down_product(t, c)
                for at, name in ((2, "turn_y"), (6, "turn_x"), (9, "logits"), (C - 8, "turn_weights")):
                    if c == at:
                        hook(name, t)

            eng.wait_ge(sa[0]["x_new"], PAIRS)
            eng.wait_ge(m["select"], 2)
            start = Step(0, -1, TILES)
            for name in ("turn_x", "logits", "turn_weights"):
                hook(name, start)
            jobs = stage_jobs(0)
            eng.wait_ge(m["w_lo"], sum(k != "down" for _, _, k, _ in jobs))
            eng.wait_ge(m["w_down"], sum(k == "down" for _, _, k, _ in jobs))
            run_tiles(eng, slot)
            need(eng, m["y_kept"], TILES)
            for q in range(NT):
                mm = t_.transpose(misc_ps[:, P * q:P * q + P], y_t[:, P * q:P * q + P], ident[:])
            mm.then_inc(m["y_turned"], 1)

        def sparse_pe(eng, m):
            t_ = nc.tensor

            def turn_and_route(t):
                par = t.parity()
                if t.has():
                    need(eng, m["x_norm"], t.n(1))
                    need(eng, m["x_t"], t.n(-1))
                    for q in range(NT):
                        mm = t_.transpose(gate_ps[par][:, P * q:P * q + P], d_x[par][:, q, :], ident[:])
                    mm.then_inc(m["x_turned"], 1)
                if t.has(-1):
                    need(eng, m["x_t"], t.n())
                    q0 = t.parity(-1)
                    for q in range(NT):
                        mm = t_.matmul(misc_ps[:, bass.ds(t.times(NT * E1, -1, E1 * q), E1)], d_xt[q0][:, q, :],
                                       router[:], start=True, stop=True)
                    mm.then_inc(m["logits"], 1)
            run_steps(eng, turn_and_route, 0, 2, TILES - 3, TILES, TILES)

            eng.wait_ge(m["rt"], RT_PICKED)
            t_.matmul(ps_a[:], earlier[:], picked, start=True, stop=True)
            t_.matmul(ps_b[:], all_ones[:], picked, start=True, stop=True).then_inc(m["logits"], 1)

            eng.wait_ge(m["rt"], RT_DONE)
            eng.wait_ge(m["w_lo"], 16)
            eng.wait_ge(m["w_down"], 8)

            def turn_rows(j):
                if not j.has():
                    return
                par = j.parity()
                need(eng, m[f"block_in{par}"], j.of_parity(16))
                need(eng, m["x_lo"], j.n())
                t_.transpose(ps_c[:, 0:P], row_in[par][:, 0:H], ident[:]).then_inc(m["b_turned"], 1)

            def experts_of(j):
                packed = eng.value_load(block_experts[0:1, bass.ds(j.i + j.off // 2, 1)], min_val=0, max_val=8 ** 4 - 1)
                gate_1, gate_2, down_1, down_2 = ((packed // 8 ** n) % 8 * 4 for n in range(4))
                return (gate_1, down_1), (gate_2, down_2)

            pair_chunks = []

            def step(j):
                par = j.parity()
                if j.off % 2 == 0:
                    pair_chunks[:] = experts_of(j)
                first, first_down = pair_chunks[j.off % 2]
                if j.has(-2):
                    need(eng, m["hidden"], j.n(-1))
                    need(eng, m["h_t"], j.n(-2))
                    for c in range(4):
                        mm = t_.transpose(ps_a[:, P * c:P * c + P], b_hidden[par][:, P * c:P * c + P], ident[:])
                    mm.then_inc(m["h_turned"], 1)
                if j.has(-3):
                    need(eng, m["h_t"], j.n(-2))
                    need(eng, m["y_kept"], j.n(-3))
                    for c in range(4):
                        mm = t_.matmul(ps_b[:, 0:P], b_hidden_t[j.parity(-3)][:, P * c:P * c + P],
                                       down[:, bass.ds(first_down + c, 1), :].squeeze(1),
                                       start=(c == 0), stop=(c == 3))
                    mm.then_inc(m["y"], 1)
                turn_rows(Step(j.i, j.off + 1, BLOCKS))
                if j.has():
                    need(eng, m["x_lo"], j.n(1))
                    need(eng, m["silu"], j.n(-1))
                    need(eng, m["hidden"], j.n(-1))
                    for dst, hi, lo in ((gate_ps[par], gate_hi, gate_lo), (up_ps[par], up_hi, up_lo)):
                        w_hi = hi[:, bass.ds(first, 4), :].rearrange("p c h -> p (c h)")
                        w_lo = lo[:, bass.ds(first, 4), :].rearrange("p c h -> p (c h)")
                        t_.matmul(dst, x_hi[par][:, 0:P], w_hi, start=True, stop=False)
                        t_.matmul(dst, x_lo[par][:, 0:P], w_hi, start=False, stop=False)
                        mm = t_.matmul(dst, x_hi[par][:, 0:P], w_lo, start=False, stop=True)
                    mm.then_inc(m["gate_up"], 1)
            turn_rows(Step(0, 0, BLOCKS))
            run_steps(eng, step, 0, 6, BLOCKS - 3, BLOCKS + 2, BLOCKS)

        @block.tensor
        def _(pe):
            for L in range(2):
                attn_pe_setup(pe, L, sa[L])
                moe_pe_setup(pe, L, sm[L])
                attn_pe(pe, L, sa[L])
                (dense_pe, sparse_pe)[L](pe, sm[L])

        def std(eng, k):
            eng.wait_ge(var_done, k + 1)
            nc.scalar.activation(ln_tmp[:, 0, :], ln_tmp[:, 2, :], ACT.Sqrt).then_inc(std_done, 1)

        def attn_act(eng, L, s):
            a = nc.scalar
            scale = SCALES[L]

            def step(p):
                par = p.parity()
                if p.has(-2):
                    need(eng, s["heads_turned"], p.n(-1))
                    need(eng, s["y"], p.n(-2))
                    a.copy(heads_t, ps_d[:, 0:P]).then_inc(s["heads_t"], 1)
                if p.has(-1):
                    need(eng, s["p_turned"], p.n())
                    need(eng, s["pv"], p.n(-1))
                    a.copy(probs_t.rearrange("p a b -> p (a b)"), ps_t[:]).then_inc(s["probs_t"], 1)
                if p.has(3):
                    need(eng, s["turned_in"], p.n(4))
                    need(eng, s["v_projected"], p.n(2))
                    a.copy(xc_t[p.parity(3)].rearrange("p a b -> p (a b)"), ps_a[:, 0:2 * P]).then_inc(s["xc_t"], 1)
                if L == 1 and p.has(2):
                    need(eng, s["projected"], p.n(3))
                    need(eng, s["qk"], p.n(1))
                    for half in range(2):
                        rows = slice(S * half, S * half + S)
                        a.copy(q_halves[par][rows, :, half, :], ps_b[rows, 0:P].rearrange("p (b s) -> p b s", b=2))\
                         .then_inc(s["q_halves"], 1)
                    need(eng, s["k_blocks"], p.times(2, 1))
                    a.copy(k_rot[par], ps_b[:, P:2 * P]).then_inc(s["k_rot"], 1)
                if p.has():
                    need(eng, s["shifted"], p.n(1))
                    flat = scores[par].rearrange("p g b k -> p (g b k)")
                    a.activation(flat, flat, ACT.Exp, scale=scale).then_inc(s["exp"], 1)
            run_steps(eng, step, -3, 4, 59, PAIRS + 1, PAIRS)

        def moe_act_setup(eng, L, m):
            a = nc.scalar
            E = EXPERTS[L]
            eng.wait_ge(m["router_turned"], 1)
            if L == 0:
                a.copy(router_hi[:, 0:E], misc_ps[:, 0:E]).then_inc(m["router_hi"], 1)
            else:
                a.copy(router[:], misc_ps[:, 0:E]).then_inc(m["router"], 1)
            for j, (_, n, kind, c) in enumerate(stage_jobs(L)):
                eng.wait_ge(m["w_turned"], j + 1)
                dst = {"gate": gate_hi, "up": up_hi, "down": down}[kind]
                ins = a.copy(dst[:, c:c + n, :].rearrange("p c h -> p (c h)"), setup_ps[j % 4][:, 0:P * n])
                ins.then_inc(m["w_down" if kind == "down" else "w_hi"], 1)

        def dense_act(eng, m):
            a = nc.scalar
            C, E = CHUNKS, EXPERTS[0]

            def hook(name, t):
                if name == "keep_y" and t.has(-1):
                    need(eng, m["down"], t.times(C))
                    need(eng, m["y_turned"], t.n(-1))
                    a.copy(y_t, y_ps[:]).then_inc(m["y_kept"], 1)
                if not t.has(1):
                    return
                par = t.parity(1)
                if name == "x_hi":
                    need(eng, m["x_turned"], t.n(2))
                    need(eng, m["gate_up"], t.times(C))
                    a.copy(x_hi[par][:], misc_ps[:]).then_inc(m["x_hi"], 1)
                if name == "squash":
                    need(eng, m["logits"], t.n(2))
                    a.activation(rt_tmp.rearrange("p a b -> p (a b)"), misc_ps[:, 0:NT * E], ACT.Tanh, scale=0.5)\
                     .then_inc(m["squashed"], 1)
                if name == "weight_t":
                    need(eng, m["weights_turned"], t.n(2))
                    need(eng, m["ce"], t.times(WEIGHTED))
                    a.copy(weight_t[par][0:2 * E, :], misc_ps[0:2 * E, :]).then_inc(m["weight_t"], 1)

            def slot(t, c):
                if c == 0:
                    hook("keep_y", t)
                nxt = ahead(t, c, LOOK)
                if nxt:
                    u, k = nxt
                    need(eng, m["gate_up"], u.times(C, plus=k + 1))
                    need(eng, m["gated"], u.times(C, plus=k - 1))
                    par = (u.off * C + k) % 2
                    a.activation(silu_g[par], gate_ps[par], ACT.Silu).then_inc(m["silu"], 1)
                for at, name in ((6, "x_hi"), (11, "squash"), (C - 7, "weight_t")):
                    if c == at:
                        hook(name, t)

            std(eng, 1)
            start = Step(0, -1, TILES)
            for name in ("x_hi", "squash", "weight_t"):
                hook(name, start)
            run_tiles(eng, slot)
            need(eng, m["down"], TILES * C)
            need(eng, m["y_turned"], TILES - 1)
            a.copy(y_t, y_ps[:]).then_inc(m["y_kept"], 1)

        def sparse_act(eng, m):
            a = nc.scalar
            std(eng, 3)

            def keep_x(t):
                par = t.parity()
                need(eng, m["x_turned"], t.n(1))
                need(eng, m["logits"], t.n(-1))
                a.copy(d_xt[par].rearrange("p q h -> p (q h)"), gate_ps[par]).then_inc(m["x_t"], 1)
            run_steps(eng, keep_x, 0, 2, TILES - 3, TILES - 1, TILES)
            eng.wait_ge(m["rt"], 2)
            a.activation(prob, prob, ACT.Exp).then_inc(m["exp"], 1)

            def keep_rows(j):
                if j.has():
                    need(eng, m["b_turned"], j.n(1))
                    need(eng, m["gate_up"], j.n(-1))
                    a.copy(x_hi[j.parity()][:, 0:P], ps_c[:, 0:P]).then_inc(m["x_hi"], 1)

            def step(j):
                keep_rows(Step(j.i, j.off + 1, BLOCKS))
                if j.has():
                    need(eng, m["gate_up"], j.n(1))
                    need(eng, m["hidden"], j.n(-1))
                    a.activation(b_silu[j.parity()], gate_ps[j.parity()], ACT.Silu).then_inc(m["silu"], 1)
                if j.has(-1):
                    need(eng, m["h_turned"], j.n())
                    need(eng, m["y"], j.n(-3))
                    a.copy(b_hidden_t[j.parity(-1)], ps_a[:]).then_inc(m["h_t"], 1)
            keep_rows(Step(0, 0, BLOCKS))
            run_steps(eng, step, 0, 4, BLOCKS - 3, BLOCKS, BLOCKS)

        @block.scalar
        def _(act):
            for L in range(2):
                if L == 0:
                    act.wait_ge(sa[0]["small_in"], SMALL[0])
                    nc.scalar.activation(tanh_g[:], gates[:], ACT.Tanh).then_inc(tanh_done, 1)
                std(act, 2 * L)
                moe_act_setup(act, L, sm[L])
                attn_act(act, L, sa[L])
                (dense_act, sparse_act)[L](act, sm[L])

        def layer_norm_scales(eng, s, k):
            v = nc.vector
            eng.wait_ge(s["stats_done"], PAIRS)
            me, qe, mo, qo = stats[:, :, 1], stats[:, :, 2], stats[:, :, 4], stats[:, :, 5]
            v.tensor_tensor(ln_tmp[:, 0, :], me, mo, ALU.subtract).then_inc(norm_link, 1)
            v.tensor_tensor(ln_tmp[:, 1, :], qe, qo, ALU.add).then_inc(norm_link, 1)
            v.tensor_tensor(mean[:], me, mo, ALU.add).then_inc(norm_link, 1)
            eng.wait_ge(norm_link, 7 * k + 3)
            v.scalar_tensor_tensor(ln_tmp[:, 2, :], ln_tmp[:, 0, :], 0.25, ln_tmp[:, 0, :], ALU.mult, ALU.mult)\
             .then_inc(norm_link, 1)
            v.tensor_scalar(mean[:], mean[:], 0.5, None, ALU.mult).then_inc(norm_link, 1)
            v.tensor_scalar(ln_tmp[:, 1, :], ln_tmp[:, 1, :], 1.0 / H, EPS, ALU.mult, ALU.add)\
             .then_inc(norm_link, 1)
            eng.wait_ge(norm_link, 7 * k + 6)
            v.tensor_tensor(ln_tmp[:, 2, :], ln_tmp[:, 2, :], ln_tmp[:, 1, :], ALU.add).then_inc(var_done, 1)
            eng.wait_ge(std_done, k + 1)
            v.reciprocal(rstd[:], ln_tmp[:, 0, :]).then_inc(norm_link, 1)
            eng.wait_ge(norm_link, 7 * k + 7)

        def attn_dve_setup(eng, L, s):
            v = nc.vector
            eng.wait_ge(s["small_in"], SMALL[L])
            if L == 0:
                eng.wait_ge(tanh_done, 1)
            else:
                eng.wait_ge(sm[0]["x_new"], TILES)
            by_head = w_nat[:, 3, :].rearrange("p (h g d) -> p h g d", g=HP, h=2)
            for copy in range(2):
                v.tensor_copy(wo_nat[:, :, copy], by_head).then_inc(s["wo_arranged"], 1)
            eng.wait_ge(s["w_turned"], 1)
            if L == 0:
                for j in range(2):
                    src = ps_a[:, P * j:P * j + P].rearrange("p (h j r) -> p h r j", h=HEADS, r=2)
                    for half in range(2):
                        for ab in range(2):
                            dst = wqk[:, 2 * ab + j, :].rearrange("p (h r j) -> p h r j", h=HEADS, r=2)
                            v.tensor_copy(dst[:, :, half, :], src[:, :, (half + ab) % 2, :])
                rows = bias_row.rearrange("p q (h j r) -> p q h r j", h=HEADS, r=2)
                for ab in range(2):
                    for half in range(2):
                        dst = bias_perm[:, ab].rearrange("p q (h r j) -> p q h r j", h=HEADS, r=2)
                        for q in range(2):
                            ins = v.tensor_copy(dst[:, q, :, half, :], rows[:, q, :, (half + ab) % 2, :])
                        ins.then_inc(s["bias_turned"], 1)
            else:
                v.tensor_copy(wqk[:, 0:2, :].rearrange("p a b -> p (a b)"), ps_a[:, 0:2 * P])
            v.tensor_copy(wv[:], ps_a[:, 2 * P:3 * P])
            eng.wait_ge(s["w_turned"], 2)
            eng.wait_ge(consts, CONSTS)
            for b in range(2):
                rows = slice(S * b, S * b + S)
                v.tensor_scalar(wo[rows, b].rearrange("p a b -> p (a b)"), ps_b[rows, 0:2 * P],
                                tanh_g[rows, L:L + 1], None, ALU.mult)
            last = v.tensor_scalar(bias_o[:], bias_o[:], tanh_g[:, L:L + 1], None, ALU.mult)
            if L == 0:
                eng.wait_ge(s["w_turned"], 3)
                eng.wait_ge(const_dma, 16)
                v.tensor_copy(bias_col[:], ps_c[:, 0:4]).then_inc(bias_link, 1)
                eng.wait_ge(bias_link, 1)
                for q in range(2):
                    v.tensor_scalar(bias_rot[:, q].rearrange("p b s -> p (b s)"),
                                    cos_sin[:, 0].rearrange("p b s -> p (b s)"), bias_col[:, q:q + 1], None, ALU.mult)\
                     .then_inc(bias_link, 1)
                eng.wait_ge(bias_link, 3)
                for q in range(2):
                    flat = bias_rot[:, q].rearrange("p b s -> p (b s)")
                    last = v.scalar_tensor_tensor(flat, cos_sin[:, 1].rearrange("p b s -> p (b s)"),
                                                  bias_col[:, 2 + q:3 + q], flat, ALU.mult, ALU.add)
            last.then_inc(s["attn_ready"], 1)
            eng.wait_ge(s["attn_ready"], 1)

        def moe_dve_setup(eng, L, m):
            v = nc.vector
            if L == 0:
                E = EXPERTS[0]
                eng.wait_ge(consts, CONSTS)
                v.tensor_tensor(pick[:], ident[:, 0:E], ident[:, E:2 * E], ALU.add).then_inc(m["pick"], 1)
                eng.wait_ge(m["pick"], 1)
                eng.wait_ge(m["router_hi"], 1)
                v.tensor_copy(select[:].rearrange("p (e m) -> p e m", e=E),
                              pick[:].unsqueeze(2).to_broadcast([P, E, P // 2])).then_inc(m["select"], 1)
                v.tensor_tensor(router_lo[:], misc_ps[:, 0:E], router_hi[:].bitcast(F32), ALU.subtract)\
                 .then_inc(m["select"], 1)
            split_weights(eng, L, m)

        def split_weights(eng, L, m):
            v = nc.vector
            n_lo = 0
            for j, (_, n, kind, c) in enumerate(stage_jobs(L)):
                if kind == "down":
                    continue
                n_lo += 1
                eng.wait_ge(m["w_hi"], n_lo)
                hi, lo = (gate_hi, gate_lo) if kind == "gate" else (up_hi, up_lo)
                v.tensor_tensor(lo[:, c:c + n, :].rearrange("p c h -> p (c h)"), setup_ps[j % 4][:, 0:P * n],
                                hi[:, c:c + n, :].bitcast(F32).rearrange("p c h -> p (c h)"), ALU.subtract)\
                 .then_inc(m["w_lo"], 1)

        def attn_dve(eng, L, s):
            v = nc.vector
            m = sm[L]
            eng.wait_ge(s["cleared"], 10)

            def step(p):
                par = p.parity()
                if p.has():
                    need(eng, s["qk"], p.n(1))
                    v.tensor_reduce(row_max[par], ps_s[:].rearrange("p (r k) -> p r k", k=S), AX.X, ALU.max)\
                     .then_inc(s["row_max"], 1)
                if p.has(4):
                    need(eng, s["turned_in"], p.n(3))
                    v.tensor_scalar(x_norm[par], x_res[:, bass.ds(p.n(4), 1), :].squeeze(1),
                                    mean[:, bass.ds(p.n(4), 1)], rstd[:, bass.ds(p.n(4), 1)],
                                    ALU.subtract, ALU.mult).then_inc(s["x_norm"], 1)
                if p.has():
                    need(eng, s["row_max"], p.n(1))
                    need(eng, s["p_turned"], p.n(-1))
                    v.tensor_tensor(scores[par].rearrange("p g b k -> p b g k"),
                                    ps_s[:].rearrange("p (b g k) -> p b g k", b=2, g=HP),
                                    row_max[par].rearrange("p (b g) -> p b g", b=2).unsqueeze(3)
                                    .to_broadcast([P, 2, HP, S]), ALU.subtract)\
                     .then_inc(s["shifted"], 1)
                if p.has(-2):
                    need(eng, s["y"], p.n(-1))
                    row = x_res[:, bass.ds(p.n(-2), 1), :].squeeze(1)
                    v.tensor_tensor(row, ps_d[:, P:2 * P], row, ALU.add).then_inc(s["x_mid"], 1)
                if p.has(-3):
                    need(eng, s["x_new"], p.n(-2))
                    v.bn_stats(stats[:, bass.ds(p.n(-3), 1), :].squeeze(1),
                               x_res[:, bass.ds(p.n(-3), 1), :].squeeze(1)).then_inc(m["stats_done"], 1)
                if p.has(1):
                    q = p.parity(1)
                    need(eng, s[f"keep{q}"], p.of_parity(32 if L == 0 else 16, 1))
                    need(eng, s["qk"], p.n())
                    for b in range(2):
                        rows = slice(S * b, S * b + S)
                        if L == 0:
                            ins = v.scalar_tensor_tensor(masked[q][rows, b, :], keep_in[q][rows, :], 0.0,
                                                         future[rows, b, :], ALU.is_equal, ALU.max)
                        else:
                            ins = v.tensor_scalar(masked[q][rows, b, :], keep_in[q][rows, :], 0.0, None, ALU.is_equal)
                        ins.then_inc(s["masked"], 1)
                if L == 0 and p.has(2):
                    need(eng, s["projected"], p.n(3))
                    need(eng, s["rot_sum"], p.n(2))
                    v.tensor_tensor(rot_terms, ps_b[:].rearrange("p (a q t) -> p a q t", a=2, q=2),
                                    cos_sin[:].rearrange("p a b s -> p a (b s)").unsqueeze(2)
                                    .to_broadcast([P, 2, 2, P]), ALU.mult).then_inc(s["rot_terms"], 1)
                if p.has(1):
                    q = p.parity(1)
                    need(eng, s["v_projected"], p.n(2))
                    need(eng, s["pv"], p.n())
                    for b in range(2):
                        rows = slice(S * b, S * b + S)
                        dst = v_blocks[q][rows, :, b, 0:2 * HD].rearrange("p g (h d) -> p g h d", h=2)
                        src = ps_c[rows, 0:P].rearrange("p (h g d) -> p g h d", g=HP, h=2)
                        if L == 0:
                            ins = v.tensor_tensor(dst, src, bias_v[rows, :]
                                                  .rearrange("p (h g d) -> p g h d", g=HP, h=2),
                                                  ALU.add)
                        else:
                            ins = v.tensor_copy(dst, src)
                        ins.then_inc(s["v_blocks"], 1)
                if L == 0 and p.has(2):
                    need(eng, s["rot_terms"], p.n(3))
                    need(eng, s["q_halves"], p.times(2, 2))
                    v.tensor_tensor(rot_sum, rot_terms[:, 0], rot_terms[:, 1], ALU.add)\
                     .then_inc(s["rot_sum"], 1)
                if p.has(-1):
                    q = p.parity(-1)
                    need(eng, s["pv"], p.n())
                    need(eng, s["heads_out"], p.times(2, -1))
                    sums = ps_a[:, 0:34 * HP].rearrange("p (r c) -> p r c", c=2 * HD + 1)
                    v.reciprocal(row_rsum, sums[:, :, 2 * HD]).then_inc(s["rsum"], 1)
                    need(eng, s["rsum"], p.n())
                    need(eng, s["heads_turned"], p.n(-2))
                    for h in range(2):
                        rows = slice(S * h, S * h + S)
                        src = ps_a[rows, 0:34 * HP].rearrange("p (g b c) -> p g b c", g=HP, b=2)
                        v.tensor_tensor(heads_out[q][rows].rearrange("p b g d -> p g b d"),
                                        src[:, :, :, HD * h:HD * h + HD],
                                        row_rsum[rows].rearrange("p (g b) -> p g b", g=HP).unsqueeze(3)
                                        .to_broadcast([S, HP, 2, HD]), ALU.mult).then_inc(s["heads_out"], 1)
            run_steps(eng, step, -4, 4, 59, PAIRS + 2, PAIRS)

        def dense_dve(eng, m):
            v = nc.vector
            C, E, K = CHUNKS, EXPERTS[0], TOP0
            layer_norm_scales(eng, m, 1)
            eng.wait_ge(m["sentinels"], 4)

            def each(f):
                return [lambda q=q: f(q) for q in range(NT)]

            def keep_keys(dst, n):
                return lambda: v.tensor_copy(dst[:, :, 0:n], rt_top[:, :, 0:n])

            choose = [
                each(lambda q: v.max(rt_top[:, q, :], rt_masked[:, q, 0:E])),
                [keep_keys(rt_keys, K)],
                each(lambda q: v.match_replace(rt_marked[:, q, 0:E + 8 - K], rt_keys[:, q, :],
                                               rt_masked[:, q, 0:E + 8 - K], TAKEN)),
                [lambda: v.scalar_tensor_tensor(rt_weight[:, :, 0:E], rt_marked[:, :, 0:E], TAKEN,
                                                rt_masked[:, :, 0:E], ALU.is_equal, ALU.mult)],
                [lambda: v.tensor_reduce(rt_sum, rt_weight[:, :, 0:E], AX.X, ALU.add)],
                [lambda: v.tensor_scalar(rt_sum, rt_sum, 1e-8, None, ALU.add)],
                [lambda: v.reciprocal(rt_rsum, rt_sum)],
                [lambda: v.tensor_tensor(rt_weight[:, :, 0:E], rt_weight[:, :, 0:E],
                                         rt_rsum.unsqueeze(2).to_broadcast([P, NT, E]), ALU.mult)],
                [lambda: v.tensor_copy(weight_cat[:, :, 0:E], rt_weight[:, :, 0:E])],
                [lambda: v.tensor_tensor(weight_cat[:, :, E:2 * E], rt_weight[:, :, 0:E],
                                         weight_cat[:, :, 0:E].bitcast(F32), ALU.subtract)],
            ]
            stages = [
                [lambda: v.tensor_scalar(rt_score, rt_tmp, 0.5, 0.5, ALU.mult, ALU.add)],
                [lambda: v.tensor_tensor(rt_score, rt_score, router_bias[:].unsqueeze(1).to_broadcast([P, NT, E]),
                                         ALU.add)],
                [lambda: v.tensor_reduce(rt_group[:, :, 0:8],
                                         rt_score.rearrange("p q (g e) -> p q g e", g=8), AX.X, ALU.max)],
                each(lambda q: v.max(rt_top[:, q, :], rt_group[:, q, 0:8])),
                [keep_keys(rt_gkeys, 4)],
                each(lambda q: v.match_replace(rt_gmark[:, q, :], rt_gkeys[:, q, :],
                                               rt_group[:, q, 0:12], TAKEN)),
                [lambda: v.tensor_scalar(rt_gsel, rt_gmark[:, :, 0:8], TAKEN, None, ALU.is_equal)],
                [lambda: v.tensor_tensor(rt_masked[:, :, 0:E].rearrange("p q (g e) -> p q g e", g=8),
                                         rt_score.rearrange("p q (g e) -> p q g e", g=8),
                                         rt_gsel.unsqueeze(3).to_broadcast([P, NT, 8, 8]), ALU.mult)],
            ] + choose
            assert sum(len(x) for x in stages) == RT, sum(len(x) for x in stages)
            done = [0]
            for x in stages:
                done.append(done[-1] + len(x))

            def route(t, k):
                need(eng, m["rt"], t.times(RT, 1, done[k]))
                if k == 0:
                    need(eng, m["squashed"], t.n(2))
                if k == len(stages) - 2:
                    need(eng, m["weights_turned"], t.n(1))
                if len(stages[k]) == NT and not isinstance(t.i, int):
                    v.tensor_copy(tick[:], one[:])
                for f in stages[k]:
                    f().then_inc(m["rt"], 1)

            def x_out(t):
                need(eng, m["y_turned"], t.n())
                rows = x_res[:, bass.ds(t.times(NT, -1), NT), :]
                v.scalar_tensor_tensor(rows, misc_ps[:].rearrange("p (q h) -> p q h", q=NT), tanh_g[:, 2:3],
                                       rows, ALU.mult, ALU.add).then_inc(m["x_new"], 1)

            def x_stats(t):
                need(eng, m["x_new"], t.n())
                for q in range(NT):
                    v.bn_stats(stats[:, bass.ds(t.times(NT, -1, q), 1), :].squeeze(1),
                               x_res[:, bass.ds(t.times(NT, -1, q), 1), :].squeeze(1))\
                     .then_inc(sa[1]["stats_done"], 1)

            def hook(c, t):
                if t.has(-1):
                    if c == 2:
                        x_out(t)
                    if c == 3:
                        x_stats(t)
                if not t.has(1):
                    return
                if c == 4:
                    need(eng, m["x_turned"], t.n(1))
                    for q in range(NT):
                        n = t.times(NT, 1, q)
                        ins = v.tensor_scalar(xm_norm[:, q, :], x_res[:, bass.ds(n, 1), :].squeeze(1),
                                              mean[:, bass.ds(n, 1)], rstd[:, bass.ds(n, 1)],
                                              ALU.subtract, ALU.mult)
                    ins.then_inc(m["x_norm"], 1)
                if c == 7:
                    need(eng, m["x_hi"], t.n(2))
                    par = t.parity(1)
                    v.tensor_tensor(x_lo[par][:], misc_ps[:], x_hi[par][:].bitcast(F32), ALU.subtract)\
                     .then_inc(m["x_lo"], 1)
                if 12 <= c < C - 8:
                    todo = list(range(len(stages)))
                    slots = C - 8 - 12
                    per = -(-len(todo) // slots)
                    for k in todo[(c - 12) * per:(c - 11) * per]:
                        route(t, k)

            def gate_times_up(t, c):
                need(eng, m["silu"], t.times(C, plus=c + 1))
                need(eng, m["gate_up"], t.times(C, plus=c + 1))
                par = (t.off * C + c) % 2
                if c >= WEIGHTED:
                    dst = hidden[(t.off * C + c) % HBUFS]
                    need(eng, m["down"], t.times(C, plus=c + 1 - HBUFS))
                else:
                    dst = gated[par]
                    need(eng, m["hidden"], t.times(C, plus=c - 1))
                v.tensor_tensor(dst, up_ps[par], silu_g[par], ALU.mult).then_inc(m["gated"], 1)

            def times_weight(t, c):
                par = (t.off * C + c) % 2
                if c >= WEIGHTED:
                    eng.wait_ge(m["gated"], t.times(C, plus=c + 1))
                    v.tensor_copy(rt_rsum[:, 0:1], rt_rsum[:, 0:1]).then_inc(m["hidden"], 1)
                    return
                need(eng, m["gated"], t.times(C, plus=c + 1))
                need(eng, m["ce"], t.times(WEIGHTED, plus=c + 1))
                need(eng, m["down"], t.times(C, plus=c + 1 - HBUFS))
                v.tensor_tensor(hidden[(t.off * C + c) % HBUFS], weight_ps[c % 2][:], gated[par], ALU.mult)\
                 .then_inc(m["hidden"], 1)

            def slot(t, c):
                nxt = ahead(t, c, LOOK)
                if nxt:
                    gate_times_up(*nxt)
                nxt = ahead(t, c, LOOK - 1)
                if nxt:
                    times_weight(*nxt)
                if c >= 0:
                    hook(c, t)

            start = Step(0, -1, TILES)
            for c in range(C):
                hook(c, start)
            run_tiles(eng, slot)
            end = Step(0, TILES, TILES)
            x_out(end)
            x_stats(end)

        def sparse_dve(eng, m):
            v = nc.vector
            layer_norm_scales(eng, m, 3)
            wide = [P, PAIRS, E1]

            def normalise(t):
                par = t.parity()
                need(eng, m["x_turned"], t.n(-1))
                for q in range(NT):
                    n = t.times(NT, plus=q)
                    ins = v.tensor_scalar(d_x[par][:, q, :], x_res[:, bass.ds(n, 1), :].squeeze(1),
                                          mean[:, bass.ds(n, 1)], rstd[:, bass.ds(n, 1)], ALU.subtract, ALU.mult)
                ins.then_inc(m["x_norm"], 1)
            run_steps(eng, normalise, 0, 2, TILES - 3, TILES - 1, TILES)

            done = [0]

            def count(ins):
                done[0] += 1
                return ins.then_inc(m["rt"], 1)

            def all_done():
                eng.wait_ge(m["rt"], done[0])

            def over_experts(per_token):
                return per_token.unsqueeze(2).to_broadcast(wide)

            def over_tokens(per_expert):
                return per_expert.unsqueeze(1).to_broadcast(wide)

            logits = misc_ps[:].rearrange("p (n e) -> p n e", e=E1)
            eng.wait_ge(m["logits"], TILES)
            count(v.tensor_reduce(best, logits, AX.X, ALU.max))
            all_done()
            count(v.tensor_tensor(prob, logits, over_experts(best), ALU.subtract))
            eng.wait_ge(m["exp"], 1)
            count(v.tensor_reduce(total, prob, AX.X, ALU.add))
            all_done()
            count(v.reciprocal(total, total))
            all_done()
            count(v.tensor_tensor(prob, prob, over_experts(total), ALU.mult))
            all_done()
            for k in range(TOP1):
                left = (prob, others)[k]
                count(v.tensor_reduce(top[k], left, AX.X, ALU.max))
                all_done()
                count(v.tensor_tensor(key, left, over_experts(top[k]), ALU.is_equal))
                all_done()
                count(v.tensor_tensor(key, key, over_tokens(descend[:]), ALU.mult))
                all_done()
                count(v.tensor_reduce(best, key, AX.X, ALU.max))
                all_done()
                count(v.tensor_tensor(chosen[k], over_tokens(descend[:]), over_experts(best), ALU.is_equal))
                all_done()
                if k == 0:
                    count(v.scalar_tensor_tensor(others, chosen[0], -2.0, prob, ALU.mult, ALU.add))
                    all_done()
            count(v.tensor_tensor(picked.rearrange("p (n e) -> p n e", e=E1), chosen[0], chosen[1], ALU.add))
            assert done[0] == RT_PICKED, done[0]
            count(v.tensor_tensor(total, top[0], top[1], ALU.add))
            all_done()
            count(v.reciprocal(total, total))
            all_done()
            for k in range(TOP1):
                count(v.scalar_tensor_tensor(share[:, k, :], top[k], tanh_g[:, 3:4], total, ALU.mult, ALU.mult))
            all_done()
            eng.wait_ge(m["logits"], TILES + 1)
            count(v.tensor_copy(scan0, ps_b[:].rearrange("p (n e) -> p n e", e=E1)))
            all_done()
            def by_part(x):
                return x.rearrange("p (t n) e -> p t n e", t=PARTS)

            src, dst = scan0, scan1
            for k in range(5):
                n = 1 << k
                count(v.tensor_copy(by_part(dst)[:, :, 0:n, :], by_part(src)[:, :, 0:n, :]))
                count(v.tensor_tensor(by_part(dst)[:, :, n:, :], by_part(src)[:, :, n:, :],
                                      by_part(src)[:, :, :PART_PAIRS - n, :], ALU.add))
                all_done()
                src, dst = dst, src
            count(v.tensor_scalar(held_end1, by_part(src)[:, :, PART_PAIRS - 1, :], 1.0 / P, None, ALU.mult))
            all_done()
            MOST = TOKENS // PARTS // P
            by_block = table[:, 0:PARTS * MOST, :].rearrange("p n e -> p (n e)")\
                .rearrange("p (t n) -> p t n", n=MOST)
            count(v.tensor_tensor(by_block, held_end1.rearrange("p t e -> p (t e)").unsqueeze(2)
                                  .to_broadcast([P, PARTS * E1, MOST]),
                                  number[:, 0:MOST].unsqueeze(1).to_broadcast([P, PARTS * E1, MOST]), ALU.is_gt))
            all_done()
            count(v.tensor_reduce(held.rearrange("p t e -> p (t e)"), by_block, AX.X, ALU.add))
            all_done()
            a, b = held, held_end0
            for n in (1, 2, 4):
                count(v.tensor_copy(b[:, :, 0:n], a[:, :, 0:n]))
                count(v.tensor_tensor(b[:, :, n:], a[:, :, n:], a[:, :, :E1 - n], ALU.add))
                all_done()
                a, b = b, (held_end1 if a is held else a)
            ends, first = a, b
            count(v.tensor_scalar(ends[:, 1, :], ends[:, 1, :], float(PART_BLOCKS), None, ALU.add))
            all_done()
            count(v.memset(by_two[0:1], 0.0))
            count(v.tensor_tensor(table[0:1].rearrange("p (t n) e -> p t n e", t=PARTS),
                                  ends[0:1].unsqueeze(2).to_broadcast([1, PARTS, PART_BLOCKS, E1]),
                                  number[0:1, :].rearrange("p (t n) -> p t n", t=PARTS).unsqueeze(3)
                                  .to_broadcast([1, PARTS, PART_BLOCKS, E1]), ALU.is_le))
            count(v.tensor_tensor(first, ends, held, ALU.subtract))
            all_done()
            count(v.tensor_reduce(table_e[0:1], table[0:1], AX.X, ALU.add))
            count(v.tensor_scalar(first, first, float(P), None, ALU.mult))
            count(v.tensor_tensor(place, src, ps_b[:].rearrange("p (n e) -> p n e", e=E1), ALU.subtract))
            all_done()
            flat = by_two[0:1].rearrange("p n t -> p (n t)")
            count(v.tensor_scalar(flat[:, 4:4 + BLOCKS], table_e[0:1], float(E1 - 1), None, ALU.min))
            count(v.tensor_tensor(place, place, ps_a[:].rearrange("p (n e) -> p n e", e=E1), ALU.add))
            all_done()
            N = BLOCKS // 2 + 2
            count(v.scalar_tensor_tensor(packed[0][0:1], by_two[0:1, 2:2 + N, 1], 8.0, by_two[0:1, 2:2 + N, 0],
                                         ALU.mult, ALU.add))
            count(v.tensor_tensor(by_part(place), by_part(place),
                                  first.unsqueeze(2).to_broadcast([P, PARTS, PART_PAIRS, E1]), ALU.add))
            all_done()
            count(v.scalar_tensor_tensor(packed[1][0:1], by_two[0:1, 0:N, 1], 64.0, packed[0][0:1],
                                         ALU.mult, ALU.add))
            for k in range(TOP1):
                count(v.tensor_tensor((key, others)[k], chosen[k], place, ALU.mult))
            all_done()
            count(v.scalar_tensor_tensor(block_experts[:], by_two[0:1, 1:1 + N, 0], 512.0, packed[1][0:1],
                                         ALU.mult, ALU.add))
            for k in range(TOP1):
                count(v.tensor_reduce(top[k], (key, others)[k], AX.X, ALU.add))
            all_done()
            for k in range(TOP1):
                count(v.tensor_copy(slots[:, :, k], top[k]))
            all_done()
            assert done[0] == RT_DONE, done[0]

            def fill_rows(rows, slot, pair):
                v.tensor_scalar(rows[:, :, 0:H], x_res[:, bass.ds(pair, 1), :].to_broadcast([P, TOP1, H]),
                                mean[:, bass.ds(pair, 1)], rstd[:, bass.ds(pair, 1)], ALU.subtract, ALU.mult)
                v.tensor_copy(rows[:, :, H].bitcast(I32), targets[:, bass.ds(pair, 1), :].squeeze(1))
                return v.tensor_copy(slot[:], slots[:, bass.ds(pair, 1), :].squeeze(1))

            def make_rows(p):
                par = p.parity()
                need(eng, m[f"scattered{par}"], p.of_parity(32 * TOP1, -2))
                for n in range(2):
                    fill_rows(row_out[par][n], slot_now[par][n], p.times(2, plus=n)).then_inc(m["rows"], 1)
            run_steps(eng, make_rows, 0, 2, PART_PAIRS // 2 - 3, PART_PAIRS // 2 - 1, PART_PAIRS // 2)

            def late_rows(j):
                par = j.parity()
                pair = j.i + (PART_PAIRS + j.off // 2)
                need(eng, m[f"scattered{par}"], j.of_parity(16, -2) + SENT_EARLY)
                v.tensor_scalar(row_out[par][0][:, 0, 0:H], x_res[:, bass.ds(pair, 1), :].squeeze(1),
                                mean[:, bass.ds(pair, 1)], rstd[:, bass.ds(pair, 1)], ALU.subtract, ALU.mult)
                v.tensor_copy(row_out[par][0][:, 0, H:H + 1].bitcast(I32), targets[:, bass.ds(pair, 1), par])
                v.tensor_copy(slot_now[par][0][:, 0:1], slots[:, bass.ds(pair, 1), par]).then_inc(m["rows"], 1)

            def split_rows(j):
                if j.has():
                    par = j.parity()
                    need(eng, m["x_hi"], j.n(1))
                    v.tensor_tensor(block_target[:, bass.ds(j.n(), 1)], row_in[par][:, H:H + 1].bitcast(I32),
                                    spare_row[:, bass.ds(j.n(), 1)], ALU.min)
                    v.tensor_tensor(x_lo[par][:, 0:P], ps_c[:, 0:P], x_hi[par][:, 0:P].bitcast(F32), ALU.subtract)\
                     .then_inc(m["x_lo"], 1)

            def step(j):
                par = j.parity()
                split_rows(Step(j.i, j.off + 1, BLOCKS))
                if j.has(-3):
                    q = j.parity(-3)
                    need(eng, m["y"], j.n(-2))
                    need(eng, m[f"y_out{q}"], j.of_parity(16, -5))
                    v.tensor_copy(target_now[q][:], block_target[:, bass.ds(j.n(-3), 1)])
                    v.tensor_copy(b_y[q], ps_b[:, 0:P]).then_inc(m["y_kept"], 1)
                if j.has():
                    need(eng, m["silu"], j.n(1))
                    need(eng, m["h_turned"], j.n(-1))
                    v.tensor_tensor(b_hidden[par], up_ps[par], b_silu[par], ALU.mult).then_inc(m["hidden"], 1)
            def both(j):
                late_rows(j)
                step(j)
            split_rows(Step(0, 0, BLOCKS))
            late = 2 * PART_PAIRS
            run_steps(eng, both, 0, 6, late - 1, late - 1, BLOCKS)
            run_steps(eng, step, late, late, BLOCKS - 3, BLOCKS + 2, BLOCKS)

            def mix(c):
                par = c.parity()
                need(eng, m[f"y_in{par}"], c.of_parity(16 * TOP1))
                for k in range(TOP1):
                    if k == 1:
                        need(eng, m["mixed"], c.n(1))
                    for q in range(2 * NT):
                        n = c.times(2 * NT, plus=q)
                        row = x_res[:, bass.ds(n, 1), :].squeeze(1)
                        ins = v.scalar_tensor_tensor(row, y_in[par][:, k, q, :],
                                                     share[:, k, :][:, bass.ds(n, 1)], row, ALU.mult, ALU.add)
                    ins.then_inc(m["mixed" if k == 0 else "x_new"], 1)
            run_steps(eng, mix, 0, 2, TILES // 2 - 3, TILES // 2 - 1, TILES // 2)

        def input_stats(dve):
            for c in range(4):
                dve.wait_ge(x_in[c], 16)
                for n in range(16 * c, 16 * c + 16):
                    nc.vector.bn_stats(stats[:, n, :], x_res[:, n, :]).then_inc(sa[0]["stats_done"], 1)

        @block.vector
        def _(dve):
            for L in range(2):
                attn_dve_setup(dve, L, sa[L])
                if L == 0:
                    input_stats(dve)
                layer_norm_scales(dve, sa[L], 2 * L)
                moe_dve_setup(dve, L, sm[L])
                attn_dve(dve, L, sa[L])
                (dense_dve, sparse_dve)[L](dve, sm[L])


def rotary_constants():
    inv = (1.0 / np.float32(10000.0) ** (np.arange(0, HD, 2, dtype=np.float32) / np.float32(HD))).astype(np.float32)
    freq = (np.arange(S, dtype=np.float32)[:, None] * inv[None, :]).astype(np.float32)
    cos, sin = np.cos(freq).T, np.sin(freq).T
    c = np.tile(np.concatenate([cos, cos]), (HEADS, 1))
    s = np.tile(np.concatenate([-sin, sin]), (HEADS, 1))
    table = np.stack([c, s], axis=1)
    return np.ascontiguousarray(np.repeat(table[:, :, None, :], 2, axis=2).astype(np.float32))


def kernel(**inputs):
    import numpy as _np
    import concourse.bacc as _bacc
    from concourse import mybir as _mybir
    from concourse.bass_utils import run_bass_kernel_spmd as _run

    nc = _bacc.Bacc("TRN2", target_bir_lowering=False, num_devices=1)
    arrays, args = {}, {}
    for name in inputs:
        a = _np.ascontiguousarray(inputs[name])
        arrays[f"in_{name}_dram"] = a
        args[name] = nc.dram_tensor(f"in_{name}_dram", a.shape, _mybir.dt.from_np(a.dtype), kind="ExternalInput").ap()
    table = rotary_constants()
    arrays["rotary_dram"] = table
    rot = nc.dram_tensor("rotary_dram", table.shape, _mybir.dt.float32, kind="ExternalInput").ap()
    out = nc.dram_tensor("out_0_dram", (B, S, H), _mybir.dt.float32, kind="ExternalOutput").ap()
    build(nc, args, rot, out)
    r = _run(nc, [arrays], core_ids=[0])
    return r.results[0]["out_0_dram"]
```
